# Optimizing a Trainium2 kernel written in Bass

```python
import numpy as np
import jax
import jax.numpy as jnp

def _softmax(x, axis=-1):
    return jax.nn.softmax(x, axis=axis)

def _gelu(x):
    return jax.nn.gelu(x, approximate=True)

def _silu(x):
    return jax.nn.silu(x)

def _sigmoid(x):
    return jax.nn.sigmoid(x)

def _layernorm(x, axis=-1, eps=1e-05):
    m = jnp.mean(x, axis=axis, keepdims=True)
    v = jnp.var(x, axis=axis, keepdims=True)
    return (x - m) / jnp.sqrt(v + eps)

def _scatter_add(tgt, idx, src, axis=0):
    return tgt.at[idx].add(src)

def _segment_sum(src, seg, n):
    return jax.ops.segment_sum(src, seg, n)
kernel_name = 'mk_gnn_ffn_d1_gnn_r32_87b2a9'

def setup_inputs(seed: int=0):
    np.random.seed(seed)
    _w = jnp.asarray

    def _rec_inputs():
        import jax
        import jax.numpy as jnp
        _gk = jax.random.key(seed)
        x = -0.0003713 + 1 * jax.random.normal(jax.random.fold_in(_gk, 1), (3125, 256), jnp.float32)
        _s = jax.random.randint(jax.random.fold_in(_gk, 2), (25000,), 0, 3125, jnp.int32)
        _d = jax.random.randint(jax.random.fold_in(_gk, 3), (25000,), 0, 3125, jnp.int32)
        _loop = jnp.arange(3125, dtype=jnp.int32)
        src = jnp.concatenate([_s, _d, _loop])
        dst = jnp.concatenate([_d, _s, _loop])
        _o = jnp.argsort(dst, stable=True)
        src = src[_o]
        dst = dst[_o]
        return (x, src, dst)
    x, src, dst = _rec_inputs()

    def _L0_gnn_setup():
        import jax, jax.numpy as jnp
        import numpy as np
        N_NODES = 50000
        N_EDGES = 25000
        IN_DIM = 256
        HEADS = 4
        HEAD_DIM = 64
        NEG_SLOPE = 0.2
        key = jax.random.key(seed)
        k1, k2, k3, k4, k5 = jax.random.split(key, 5)
        x = jax.random.normal(k1, (N_NODES, IN_DIM), dtype=jnp.float32)
        edge_index = jax.random.randint(k2, (2, N_EDGES), 0, N_NODES, dtype=jnp.int64)
        W = jax.random.normal(k3, (IN_DIM, HEADS * HEAD_DIM), dtype=jnp.float32) * (1.0 / np.sqrt(IN_DIM))
        att_src = jax.random.normal(k4, (HEADS, HEAD_DIM), dtype=jnp.float32) * (1.0 / np.sqrt(HEAD_DIM))
        att_dst = jax.random.normal(k5, (HEADS, HEAD_DIM), dtype=jnp.float32) * (1.0 / np.sqrt(HEAD_DIM))
        bias = jnp.zeros((HEADS * HEAD_DIM,), dtype=jnp.float32)
        return {'x': x, 'edge_index': edge_index, 'W': W, 'att_src': att_src, 'att_dst': att_dst, 'bias': bias}
    _L0_gnn_all = _L0_gnn_setup()
    _L0_gnn_in = {k: v for k, v in _L0_gnn_all.items() if k in ('W', 'att_src', 'att_dst', 'bias')}
    del _L0_gnn_all

    def _L0_ffn_setup():
        import jax, jax.numpy as jnp
        import numpy as np
        B, T, D, H, L = (16, 128, 256, 256, 2)

        def _lstm(x, W_ih, W_hh, b_ih, b_hh):
            x_proj = jnp.einsum('btd,gd->btg', x, W_ih) + b_ih + b_hh
            h0 = jnp.zeros((x.shape[0], W_hh.shape[1]), x.dtype)
            c0 = jnp.zeros_like(h0)

            def step(carry, xp):
                h, c = carry
                gates = xp + h @ W_hh.T
                i, f, g, o = jnp.split(gates, 4, axis=-1)
                c = jax.nn.sigmoid(f) * c + jax.nn.sigmoid(i) * jnp.tanh(g)
                h = jax.nn.sigmoid(o) * jnp.tanh(c)
                return ((h, c), h)
            _, hs = jax.lax.scan(step, (h0, c0), jnp.swapaxes(x_proj, 0, 1))
            return jnp.swapaxes(hs, 0, 1)
        key = jax.random.key(seed)
        ks = jax.random.split(key, 9)
        s = 1.0 / np.sqrt(H)
        u = lambda k, shape: jax.random.uniform(k, shape, jnp.float32, -s, s)
        return {'x': jax.random.normal(ks[0], (B, T, D), jnp.float32), 'W_ih': u(ks[1], (4 * H, D)), 'W_hh': u(ks[2], (4 * H, H)), 'b_ih': u(ks[3], (4 * H,)), 'b_hh': u(ks[4], (4 * H,)), 'W_lin': u(ks[5], (L, H)), 'b_lin': u(ks[6], (L,)), 'fw_att': jnp.full((1, H), 0.001, jnp.float32), 'bw_att': jnp.full((1, H), 0.001, jnp.float32)}
    _L0_ffn_all = _L0_ffn_setup()
    _L0_ffn_in = {k: v for k, v in _L0_ffn_all.items() if k in ('W_ih', 'W_hh', 'b_ih', 'b_hh', 'W_lin', 'b_lin', 'fw_att', 'bw_att')}
    del _L0_ffn_all
    return {'x': x, 'src': src, 'dst': dst, 'L0_gnn_W': _L0_gnn_in['W'], 'L0_gnn_att_src': _L0_gnn_in['att_src'], 'L0_gnn_att_dst': _L0_gnn_in['att_dst'], 'L0_gnn_bias': _L0_gnn_in['bias'], 'L0_ffn_W_ih': _L0_ffn_in['W_ih'], 'L0_ffn_W_hh': _L0_ffn_in['W_hh'], 'L0_ffn_b_ih': _L0_ffn_in['b_ih'], 'L0_ffn_b_hh': _L0_ffn_in['b_hh'], 'L0_ffn_W_lin': _L0_ffn_in['W_lin'], 'L0_ffn_b_lin': _L0_ffn_in['b_lin'], 'L0_ffn_fw_att': _L0_ffn_in['fw_att'], 'L0_ffn_bw_att': _L0_ffn_in['bw_att']}

def reference(x, src, dst, L0_gnn_W, L0_gnn_att_src, L0_gnn_att_dst, L0_gnn_bias, L0_ffn_W_ih, L0_ffn_W_hh, L0_ffn_b_ih, L0_ffn_b_hh, L0_ffn_W_lin, L0_ffn_b_lin, L0_ffn_fw_att, L0_ffn_bw_att):
    import jax
    import jax.numpy as jnp

    def _L0_gnn_ref(x, edge_index, W, att_src, att_dst, bias):
        import jax, jax.numpy as jnp
        import numpy as np
        N_NODES = 50000
        N_EDGES = 25000
        IN_DIM = 256
        HEADS = 4
        HEAD_DIM = 64
        NEG_SLOPE = 0.2
        N = x.shape[0]
        loops = jnp.arange(N, dtype=edge_index.dtype)
        src = jnp.concatenate([edge_index[0], loops])
        dst = jnp.concatenate([edge_index[1], loops])
        h = (x @ W).reshape(N, HEADS, HEAD_DIM)
        a_src = jnp.einsum('nhd,hd->nh', h, att_src)
        a_dst = jnp.einsum('nhd,hd->nh', h, att_dst)
        e = a_src[src] + a_dst[dst]
        e = jax.nn.leaky_relu(e, NEG_SLOPE)
        m = jax.ops.segment_max(e, dst, num_segments=N)
        e = jnp.exp(e - m[dst])
        denom = jax.ops.segment_sum(e, dst, num_segments=N)
        alpha = e / denom[dst]
        msg = alpha[:, :, None] * h[src]
        out = jax.ops.segment_sum(msg, dst, num_segments=N)
        return out.reshape(N, HEADS * HEAD_DIM) + bias

    def _L0_ffn_ref(x, W_ih, W_hh, b_ih, b_hh, W_lin, b_lin, fw_att, bw_att):
        import jax, jax.numpy as jnp
        import numpy as np
        B, T, D, H, L = (16, 128, 256, 256, 2)

        def _lstm(x, W_ih, W_hh, b_ih, b_hh):
            x_proj = jnp.einsum('btd,gd->btg', x, W_ih) + b_ih + b_hh
            h0 = jnp.zeros((x.shape[0], W_hh.shape[1]), x.dtype)
            c0 = jnp.zeros_like(h0)

            def step(carry, xp):
                h, c = carry
                gates = xp + h @ W_hh.T
                i, f, g, o = jnp.split(gates, 4, axis=-1)
                c = jax.nn.sigmoid(f) * c + jax.nn.sigmoid(i) * jnp.tanh(g)
                h = jax.nn.sigmoid(o) * jnp.tanh(c)
                return ((h, c), h)
            _, hs = jax.lax.scan(step, (h0, c0), jnp.swapaxes(x_proj, 0, 1))
            return jnp.swapaxes(hs, 0, 1)
        lstm_out = _lstm(x, W_ih, W_hh, b_ih, b_hh)
        logits = jnp.einsum('bth,lh->btl', lstm_out, W_lin) + b_lin
        g = jax.lax.stop_gradient(jnp.argmax(logits, axis=-1).astype(lstm_out.dtype))[..., None]
        w = g * lstm_out
        inc = jnp.cumsum(w, axis=1)
        prefix = inc - w
        suffix = inc[:, -1:, :] - inc
        return 2.0 * lstm_out + prefix * fw_att + suffix * bw_att
    edge_index = jnp.stack([src, dst])
    x = x + _L0_gnn_ref(_layernorm(x, axis=-1), edge_index, L0_gnn_W, L0_gnn_att_src, L0_gnn_att_dst, L0_gnn_bias)
    x = x + _L0_ffn_ref(_layernorm(x, axis=-1)[None], L0_ffn_W_ih, L0_ffn_W_hh, L0_ffn_b_ih, L0_ffn_b_hh, L0_ffn_W_lin, L0_ffn_b_lin, L0_ffn_fw_att, L0_ffn_bw_att)[0]
    return x

_drawn_inputs = setup_inputs


def setup_inputs(seed=0):
    import zlib

    import numpy as np

    out = dict(_drawn_inputs(seed))
    spreads = {'L0_gnn_bias': (0.0, 0.1),
     'L0_ffn_fw_att': (0.0010000000474974513, 0.2),
     'L0_ffn_bw_att': (0.0010000000474974513, 0.2)}
    factors = {}
    for name, (base, spread) in spreads.items():
        noise = np.random.default_rng([zlib.crc32(name.encode()), seed]).standard_normal(out[name].shape)
        drawn = base * np.exp(spread * noise) if base else spread * noise
        out[name] = jnp.asarray(drawn.astype(out[name].dtype))
    for name, factor in factors.items():
        out[name] = (out[name] * factor).astype(out[name].dtype)
    return out
```

```python
from contextlib import ExitStack

import numpy as np

import concourse.bass as bass
from concourse import mybir

F32 = mybir.dt.float32
F16 = mybir.dt.float16
BF16 = mybir.dt.bfloat16
I32 = mybir.dt.int32
ALU = mybir.AluOpType
ACT = mybir.ActivationFunctionType
AX = mybir.AxisListType

N = 3125
D = 256
HEADS, HD = 4, 64
EDGES = 53125
WIN = 125
NW = N // WIN
TILES = 18
UNIT = TILES * 128
HR = HD + 1
MSG = HEADS * HR
ROW = MSG + HEADS
BIG = 1.0e30
EXTRA = EDGES // UNIT
SLOTS = NW + EXTRA + 4
CH, KS = 125, 25
WARM = 36
HALF = [(0, 63), (63, CH)]
SLOT_GATE = [0, 1, 2, 3, 6, 7, 4, 5]
TOL = 2.0 ** -20
EPS = 1e-5
SLOPE = 0.2


def build(nc, x, src, dst, gnn_w, att_src, att_dst, gnn_bias, w_ih, w_hh, b_ih, b_hh,
          w_lin, b_lin, fw_att, bw_att, out):
    ctx = ExitStack()

    def sb(name, shape, dt=F32):
        return ctx.enter_context(nc.sbuf_tensor(name, shape, dt))

    def ps(name, shape=(128, 512)):
        return ctx.enter_context(nc.psum_tensor(name, list(shape), F32))

    def sem(name):
        return ctx.enter_context(nc.semaphore(name))

    with ctx:
        table = nc.dram_tensor("node_table", [N, ROW], F32).ap()
        dst_f = nc.dram_tensor("dst_f", [EDGES + UNIT], F32).ap()
        src_f = nc.dram_tensor("src_f", [EDGES + UNIT], F32).ap()

        x1 = sb("x1", [WIN, NW, D])
        hT = sb("hT", [128, 2 * (KS + 1) * CH])
        arena = sb("arena", [128, 8 * N])
        acc = sb("acc", [WIN, NW, ROW])
        wihT = sb("wihT", [128, 2, 4 * D])
        whhT = sb("whhT", [128, 2, 4 * D])
        ident = sb("ident", [128, 128])
        ones = sb("ones", [128, 128])
        small = sb("small", [24, 128])
        smallT = sb("smallT", [128, 24])
        biasT = sb("biasT", [128, 8])
        ad_l = sb("ad_l", [WIN, NW, HEADS])
        mx_l = sb("mx_l", [WIN, NW, HEADS])
        units_i = sb("units_i", [1, 2, SLOTS], I32)
        pairs_i = sb("pairs_i", [1, 1], I32)
        cell = sb("cell", [128, 2, CH])
        start_c = sb("start_c", [128, 2, CH])

        h_rows = hT[:, :].rearrange("p (a k c) -> p a k c", a=2, k=KS + 1)
        xproj = arena[:, :].rearrange("p (s k c) -> p s k c", s=8, k=KS)
        at = 0

        def carve(rows, size):
            nonlocal at
            at += size
            return arena[0:rows, at - size:at]
        gath = [carve(128, TILES * ROW).rearrange("p (i r) -> p i r", i=TILES) for _ in range(2)]
        onehot = [carve(128, TILES * WIN).rearrange("p (i n) -> p i n", i=TILES) for _ in range(2)]
        onehot_h = [carve(128, TILES * WIN // 2).bitcast(BF16).rearrange("p (i n) -> p i n", i=TILES) for _ in range(2)]
        onehotT = [carve(WIN, UNIT // 2).bitcast(BF16).rearrange("p (i e) -> p i e", i=TILES) for _ in range(2)]
        node_id = hT[:, 0:N]
        stage_w = [arena[:, i * 8 * D:(i + 1) * 8 * D]
                   .rearrange("p (m d) -> p m d", m=8) for i in range(2)]

        bank = [ps(f"bank{i}") for i in range(8)]

        with ExitStack() as c1:
            def sb1(name, shape, dt=F32):
                return c1.enter_context(nc.sbuf_tensor(name, shape, dt))

            def sem1(name):
                return c1.enter_context(nc.semaphore(name))
            gw = sb1("gw", [128, 2, D])
            att = sb1("att", [WIN, 2, D])
            edge_i = sb1("edge_i", [WIN, 2, EDGES // WIN], I32)
            at = 2 * 8 * D
            edge_f = carve(WIN, 2 * (EDGES // WIN)).rearrange("p (a e) -> p a e", a=2)
            pad = sb1("pad", [128, 2, TILES])
            below = carve(WIN, EDGES // WIN)
            counts = sb1("counts", [WIN, NW + 1])
            stats = sb1("stats", [WIN, NW, 6])
            meanvar = sb1("meanvar", [WIN, NW, 2])
            rstd = sb1("rstd", [WIN, NW])
            tmp = sb1("tmp", [WIN, 3, NW])
            yn = carve(WIN, 5 * D).rearrange("p (b d) -> p b d", b=5)
            ynT = carve(128, 10 * WIN).rearrange("p (b a n) -> p b a n", b=5, a=2)
            prod = carve(WIN, 2 * D).rearrange("p (a d) -> p a d", a=2)
            fst = sb1("fst", [1, NW + 1])
            blk = sb1("blk", [1, NW, EXTRA + 1])
            step_k = sb1("step_k", [1, EXTRA + 1])
            nblk = sb1("nblk", [1, NW])
            zer = sb1("zer", [1, NW])
            uend = sb1("uend", [1, NW + 1])
            ubeg = sb1("ubeg", [1, NW + 1])
            adj = sb1("adj", [1, NW + 1])
            uid = sb1("uid", [1, SLOTS])
            wid = sb1("wid", [1, NW + 1])
            cmp = carve(1, SLOTS * (NW + 1)).rearrange("p (u w) -> p u w", u=SLOTS)
            uwin = sb1("uwin", [1, SLOTS])
            uoff = sb1("uoff", [1, SLOTS])
            pcmp = sb1("pcmp", [1, EXTRA + 2])
            pairs = sb1("pairs", [1, 1])

            x_in, w_in, e_in, att_in, lw_in, sm_in = map(sem1, ("x_in", "w_in", "e_in", "att_in", "lw_in", "sm_in"))
            pool_step, const_done, e_float, scratch = map(sem1, ("pool_step", "const_done", "e_float", "scratch"))
            dve_step, var_ready, sd_ready = map(sem1, ("dve_step", "var_ready", "sd_ready"))
            yn_ready, ynt_psum, ynt_ready, h_psum = map(sem1, ("yn_ready", "ynt_psum", "ynt_ready", "h_psum"))
            h_copied, logit_done, cnt_ready, fst_psum = map(sem1, ("h_copied", "logit_done", "cnt_ready", "fst_psum"))
            wt_psum, wt_copied, smt_psum, tab_out = map(sem1, ("wt_psum", "wt_copied", "smt_psum", "tab_out"))
            units_done = sem1("units_done")
            block = c1.enter_context(nc.Block())

            yT_p = [bank[0][:, 0:2 * WIN].rearrange("p (a n) -> p a n", a=2),
                    bank[1][:, 0:2 * WIN].rearrange("p (a n) -> p a n", a=2)]
            h_p = [bank[2][0:WIN, 0:D], bank[3][0:WIN, 0:D]]
            fst_p = bank[4][0:1, 0:NW + 1]
            wT_p = [bank[5], bank[6]]
            small_p = bank[7][:, 0:24]

            @block.sync
            def _(sp):
                sp.dma_start(edge_i[:, 0, :], dst.rearrange("(p e) -> p e", p=WIN)).then_inc(e_in, 16)
                sp.dma_start(edge_i[:, 1, :], src.rearrange("(p e) -> p e", p=WIN)).then_inc(e_in, 16)
                sp.dma_start(x1[:, :, :], x.rearrange("(w p) f -> p w f", p=WIN)).then_inc(x_in, 16)
                sp.wait_ge(e_float, 2)
                sp.dma_start(dst_f[0:EDGES].rearrange("(p e) -> p e", p=WIN), edge_f[:, 0, :]).then_inc(scratch, 16)
                sp.dma_start(src_f[0:EDGES].rearrange("(p e) -> p e", p=WIN), edge_f[:, 1, :]).then_inc(scratch, 16)
                sp.wait_ge(const_done, 1)
                sp.dma_start(dst_f[EDGES:EDGES + UNIT].rearrange("(p e) -> p e", p=128), pad[:, 0, :]).then_inc(scratch, 16)
                sp.dma_start(src_f[EDGES:EDGES + UNIT].rearrange("(p e) -> p e", p=128), pad[:, 1, :]).then_inc(scratch, 16)
                rows = table.rearrange("(w p) r -> p w r", p=WIN)
                for b in range(5):
                    sp.wait_ge(h_copied, 5 * b + 5)
                    sp.wait_ge(logit_done, 5 * b + 5)
                    sp.dma_start(rows[:, 5 * b:5 * b + 5, :], acc[:, 5 * b:5 * b + 5, :]).then_inc(tab_out, 16)
                sp.wait_ge(scratch, 64)
                sp.wait_ge(tab_out, 80)

            @block.gpsimd
            def _(pool):
                pool.memset(ident[:, :], 0.0).then_inc(pool_step, 1)
                pool.wait_ge(pool_step, 1)
                pool.affine_select(out=ident[:, :], in_=ident[:, :], compare_op=ALU.not_equal, fill=1.0, base=0,
                                   pattern=[[-1, 128]], channel_multiplier=1).then_inc(pool_step, 1)
                pool.memset(ones[:, :], 1.0).then_inc(pool_step, 1)
                pool.memset(pad[:, 0, :], 4096.0).then_inc(pool_step, 1)
                pool.memset(pad[:, 1, :], 0.0).then_inc(pool_step, 1)
                pool.memset(acc[:, :, 0:MSG].rearrange("p w (h r) -> p w h r", h=HEADS)[:, :, :, HD:HR], 1.0).then_inc(pool_step, 1)
                pool.iota(step_k[:, :], pattern=[[UNIT, EXTRA + 1]], base=0, channel_multiplier=0,
                          allow_small_or_imprecise_dtypes=True).then_inc(pool_step, 1)
                pool.iota(uid[:, :], pattern=[[1, SLOTS]], base=0, channel_multiplier=0,
                          allow_small_or_imprecise_dtypes=True).then_inc(pool_step, 1)
                pool.iota(wid[:, :], pattern=[[1, NW + 1]], base=0, channel_multiplier=0,
                          allow_small_or_imprecise_dtypes=True).then_inc(pool_step, 1)
                pool.memset(counts[:, 0:1], 0.0).then_inc(pool_step, 1)
                pool.memset(counts[:, NW:NW + 1], float(EDGES // WIN)).then_inc(pool_step, 1)
                pool.memset(zer[:, :], 0.0).then_inc(pool_step, 1)
                pool.wait_ge(pool_step, 12)
                pool.memset(ubeg[:, 0:1], 0.0).then_inc(const_done, 1)

            @block.scalar
            def _(act):
                act.dma_start(gw[:, :, :], gnn_w.rearrange("(a p) n -> p a n", p=128)).then_inc(w_in, 16)
                act.dma_start(att[:, 0, :], att_src.rearrange("h d -> (h d)").partition_broadcast(WIN)).then_inc(att_in, 16)
                act.dma_start(att[:, 1, :], att_dst.rearrange("h d -> (h d)").partition_broadcast(WIN)).then_inc(att_in, 16)
                act.dma_start(small[0:8, :], b_ih.rearrange("(m p) -> m p", p=128)).then_inc(sm_in, 16)
                act.dma_start(small[8:16, :], b_hh.rearrange("(m p) -> m p", p=128)).then_inc(sm_in, 16)
                act.dma_start(small[16:20, :], w_lin.rearrange("l (a p) -> (l a) p", p=128)).then_inc(sm_in, 16)
                act.dma_start(small[20:22, :], fw_att.rearrange("o (a p) -> (o a) p", p=128)).then_inc(sm_in, 16)
                act.dma_start(small[22:24, :], bw_att.rearrange("o (a p) -> (o a) p", p=128)).then_inc(sm_in, 16)
                act.dma_start(stage_w[0], w_ih.rearrange("(m p) d -> p m d", p=128)).then_inc(lw_in, 16)
                act.dma_start(stage_w[1], w_hh.rearrange("(m p) d -> p m d", p=128)).then_inc(lw_in, 16)
                act.wait_ge(var_ready, 1)
                act.activation(rstd[:, :], tmp[:, 0, :], ACT.Sqrt).then_inc(sd_ready, 1)
                for w in range(NW):
                    act.wait_ge(ynt_psum, w + 1)
                    act.activation(ynT[:, w % 5, :, :], yT_p[w % 2], ACT.Copy).then_inc(ynt_ready, 1)
                    act.wait_ge(h_psum, w + 1)
                    act.activation(acc[:, w, 0:MSG].rearrange("p (h r) -> p h r", h=HEADS)[:, :, 0:HD],
                                   h_p[w % 2].rearrange("p (h r) -> p h r", h=HEADS), ACT.Copy).then_inc(h_copied, 1)
                for g in range(8):
                    act.wait_ge(wt_psum, g + 1)
                    w_t, a, half = (wihT, whhT)[g // 4], (g % 4) // 2, g % 2
                    act.activation(w_t[:, a, 512 * half:512 * half + 512], wT_p[g % 2][:, :], ACT.Copy).then_inc(wt_copied, 1)

            @block.vector
            def _(dve):
                n = 0

                def chain(ins):
                    nonlocal n
                    n += 1
                    ins.then_inc(dve_step, 1)
                    dve.wait_ge(dve_step, n)
                dve.wait_ge(e_in, 32)
                dve.tensor_copy(edge_f[:, 0, :], edge_i[:, 0, :]).then_inc(e_float, 1)
                dve.tensor_copy(edge_f[:, 1, :], edge_i[:, 1, :]).then_inc(e_float, 1)
                dve.wait_ge(x_in, 16)
                for w in range(NW):
                    dve.bn_stats(stats[:, w, :], x1[:, w, :]).then_inc(dve_step, 1)
                n += NW
                dve.wait_ge(dve_step, n)
                for w in range(NW):
                    dve.bn_aggr(meanvar[:, w, :], stats[:, w, :]).then_inc(dve_step, 1)
                n += NW
                dve.wait_ge(dve_step, n)
                dve.tensor_scalar(tmp[:, 0, :], meanvar[:, :, 1], EPS, None, ALU.add).then_inc(var_ready, 1)
                dve.wait_ge(e_float, 2)
                dve.wait_ge(const_done, 1)
                for w in range(1, NW):
                    chain(dve.tensor_scalar(below[:, :], edge_f[:, 0, :], float(WIN * w), 0.0, ALU.is_lt, ALU.add,
                                            accum_out=counts[:, w:w + 1]))
                dve.tensor_copy(counts[:, 0:1], counts[:, 0:1]).then_inc(cnt_ready, 1)
                dve.wait_ge(sd_ready, 1)
                chain(dve.reciprocal(tmp[:, 1, :], rstd[:, :]))
                chain(dve.tensor_tensor(tmp[:, 2, :], tmp[:, 1, :], tmp[:, 1, :], ALU.mult))
                chain(dve.tensor_tensor(tmp[:, 2, :], tmp[:, 2, :], tmp[:, 0, :], ALU.mult))
                chain(dve.tensor_scalar(tmp[:, 2, :], tmp[:, 2, :], -0.5, 1.5, ALU.mult, ALU.add))
                chain(dve.tensor_tensor(rstd[:, :], tmp[:, 2, :], tmp[:, 1, :], ALU.mult))
                dve.wait_ge(att_in, 32)

                def normalise(w):
                    if w >= 5:
                        dve.wait_ge(ynt_psum, w - 4)
                    dve.tensor_scalar(yn[:, w % 5, :], x1[:, w, :], meanvar[:, w, 0:1], rstd[:, w:w + 1],
                                      ALU.subtract, ALU.mult).then_inc(yn_ready, 1)
                for w in range(3):
                    normalise(w)
                for w in range(NW):
                    if w + 3 < NW:
                        normalise(w + 3)
                    dve.wait_ge(h_copied, w + 1)
                    if w:
                        dve.wait_ge(logit_done, w)
                    h_w = acc[:, w, 0:MSG].rearrange("p (h r) -> p h r", h=HEADS)[:, :, 0:HD]
                    for j in range(2):
                        dve.tensor_tensor(prod[:, j, :].rearrange("p (h r) -> p h r", h=HEADS), h_w,
                                          att[:, j, :].rearrange("p (h r) -> p h r", h=HEADS), ALU.mult).then_inc(dve_step, 1)
                    n += 2
                    dve.wait_ge(dve_step, n)
                    chain(dve.tensor_reduce(ad_l[:, w, :], prod[:, 1, :].rearrange("p (h r) -> p h r", h=HEADS),
                                            AX.X, ALU.add))
                    dve.tensor_reduce(acc[:, w, MSG:ROW], prod[:, 0, :].rearrange("p (h r) -> p h r", h=HEADS),
                                      AX.X, ALU.add).then_inc(logit_done, 1)
                dve.wait_ge(logit_done, NW)
                chain(dve.tensor_tensor(mx_l[:, :, :], acc[:, :, MSG:ROW], ad_l[:, :, :], ALU.add))
                chain(dve.scalar_tensor_tensor(out=mx_l[:, :, :].rearrange("p w h -> p (w h)"),
                                               in0=mx_l[:, :, :].rearrange("p w h -> p (w h)"), scalar=SLOPE,
                                               in1=mx_l[:, :, :].rearrange("p w h -> p (w h)"),
                                               op0=ALU.mult, op1=ALU.max))
                dve.wait_ge(smt_psum, 1)
                chain(dve.tensor_copy(smallT[:, :], small_p))
                for s, m in enumerate(SLOT_GATE):
                    dve.tensor_tensor(biasT[:, s:s + 1], smallT[:, m:m + 1], smallT[:, 8 + m:9 + m], ALU.add).then_inc(dve_step, 1)
                n += 8
                dve.wait_ge(fst_psum, 1)
                chain(dve.tensor_copy(fst[:, :], fst_p))
                chain(dve.tensor_tensor(nblk[:, :], fst[:, 1:NW + 1], fst[:, 0:NW], ALU.subtract))
                chain(dve.tensor_tensor(blk[:, :, :], nblk[:, :].unsqueeze(2).to_broadcast([1, NW, EXTRA + 1]),
                                        step_k[:, :].unsqueeze(1).to_broadcast([1, NW, EXTRA + 1]), ALU.is_gt))
                chain(dve.tensor_reduce(nblk[:, :], blk[:, :, :], AX.X, ALU.add))
                chain(dve.tensor_scalar(nblk[:, :], nblk[:, :], 1.0, None, ALU.max))
                chain(dve.tensor_tensor_scan(uend[:, 0:NW], nblk[:, :], zer[:, :], 0.0, ALU.add, ALU.add))
                chain(dve.tensor_copy(ubeg[:, 1:NW + 1], uend[:, 0:NW]))
                chain(dve.tensor_tensor(cmp[:, :, 0:NW], uend[:, 0:NW].unsqueeze(1).to_broadcast([1, SLOTS, NW]),
                                        uid[:, :].unsqueeze(2).to_broadcast([1, SLOTS, NW]), ALU.is_le))
                chain(dve.tensor_reduce(uwin[:, :], cmp[:, :, 0:NW], AX.X, ALU.add))
                chain(dve.scalar_tensor_tensor(out=adj[:, :], in0=ubeg[:, :], scalar=-float(UNIT), in1=fst[:, :],
                                               op0=ALU.mult, op1=ALU.add))
                chain(dve.tensor_tensor(cmp[:, :, :], uwin[:, :].unsqueeze(2).to_broadcast([1, SLOTS, NW + 1]),
                                        wid[:, :].unsqueeze(1).to_broadcast([1, SLOTS, NW + 1]), ALU.is_equal))
                chain(dve.tensor_tensor(cmp[:, :, :], cmp[:, :, :], adj[:, :].unsqueeze(1).to_broadcast([1, SLOTS, NW + 1]), ALU.mult))
                chain(dve.tensor_reduce(uoff[:, :], cmp[:, :, :], AX.X, ALU.add))
                chain(dve.scalar_tensor_tensor(out=uoff[:, :], in0=uid[:, :], scalar=float(UNIT), in1=uoff[:, :],
                                               op0=ALU.mult, op1=ALU.add))
                chain(dve.tensor_scalar(uoff[:, :], uoff[:, :], float(EDGES), None, ALU.min))
                chain(dve.tensor_copy(units_i[:, 1, :], uoff[:, :]))
                chain(dve.tensor_scalar(uwin[:, :], uwin[:, :], float(NW - 1), None, ALU.min))
                chain(dve.tensor_copy(units_i[:, 0, :], uwin[:, :]))
                chain(dve.tensor_scalar(uid[:, :], uid[:, :], 2.0, 1.0, ALU.mult, ALU.add))
                chain(dve.tensor_tensor(uwin[:, :], uend[:, NW - 1:NW].to_broadcast([1, SLOTS]), uid[:, :], ALU.is_gt))
                chain(dve.tensor_reduce(pairs[:, :], uwin[:, :], AX.X, ALU.add))
                dve.tensor_copy(pairs_i[:, :], pairs[:, :]).then_inc(units_done, 1)

            @block.tensor
            def _(pe):
                pe.wait_ge(const_done, 1)
                pe.wait_ge(w_in, 16)

                def project(w):
                    pe.wait_ge(ynt_ready, w + 1)
                    if w >= 2:
                        pe.wait_ge(h_copied, w - 1)
                    for a in range(2):
                        last = pe.matmul(h_p[w % 2], ynT[:, w % 5, a, :], gw[:, a, :], start=(a == 0), stop=(a == 1))
                    last.then_inc(h_psum, 1)
                for w in range(NW):
                    pe.wait_ge(yn_ready, w + 1)
                    if w >= 2:
                        pe.wait_ge(ynt_ready, w - 1)
                    for a in range(2):
                        last = pe.transpose(yT_p[w % 2][:, a, :], yn[:, w % 5, 128 * a:128 * a + 128], ident[0:WIN, 0:WIN])
                    last.then_inc(ynt_psum, 1)
                    if w >= 1:
                        project(w - 1)
                project(NW - 1)
                pe.wait_ge(cnt_ready, 1)
                pe.matmul(fst_p, ones[0:WIN, 0:1], counts[:, :], start=True, stop=True).then_inc(fst_psum, 1)
                pe.wait_ge(sm_in, 80)
                pe.transpose(small_p, small[:, :], ident[0:24, 0:24]).then_inc(smt_psum, 1)
                pe.wait_ge(lw_in, 32)
                for g in range(8):
                    a, half = (g % 4) // 2, g % 2
                    if g >= 2:
                        pe.wait_ge(wt_copied, g - 1)
                    for j in range(4):
                        m = 4 * half + j
                        last = pe.transpose(wT_p[g % 2][:, 128 * j:128 * j + 128],
                                            stage_w[g // 4][:, m, 128 * a:128 * a + 128], ident[:, :])
                    last.then_inc(wt_psum, 1)

        with ExitStack() as c2:
            def sb2(name, shape, dt=F32):
                return c2.enter_context(nc.sbuf_tensor(name, shape, dt))

            def sem2(name):
                return c2.enter_context(nc.semaphore(name))
            H18 = HEADS * TILES
            raw = [sb2(f"raw{q}", [2 * TILES, 128]) for q in range(2)]
            dst_x = [sb2(f"dst_x{q}", [H18, 128]) for q in range(2)]
            ends = [sb2(f"ends{q}", [H18, 129]) for q in range(2)]
            cut = [sb2(f"cut{q}", [H18, 128]) for q in range(2)]
            dst_p = [sb2(f"dst_p{q}", [128, TILES]) for q in range(2)]
            src_p = [sb2(f"src_p{q}", [128, TILES], I32) for q in range(2)]
            ident_h = sb2("ident_h", [128, 128], BF16)
            slog = sb2("slog", [128, HEADS, TILES])
            vmax = sb2("vmax", [H18, 128])
            vend = sb2("vend", [H18, 128])
            vrest = sb2("vrest", [128, HEADS, TILES])
            vT = sb2("vT", [128, TILES, 3 * HEADS + 1], BF16)
            absent = sb2("absent", [WIN, TILES])
            cand = sb2("cand", [WIN, HEADS, TILES])
            bmax = sb2("bmax", [WIN, HEADS])
            zt = sb2("zt", [WIN, HEADS])
            mnew = sb2("mnew", [WIN, HEADS])
            mrest = sb2("mrest", [WIN, HEADS])
            tab = sb2("tab", [WIN, 6 * HEADS], BF16)
            ad_parts = sb2("ad_parts", [WIN, NW, 3 * HEADS], BF16)
            ad_rest = sb2("ad_rest", [WIN, NW, HEADS])
            dm = sb2("dm", [WIN, HEADS])
            shrink = sb2("shrink", [WIN, HEADS])
            by_edge = sb2("by_edge", [128, 2, TILES, HEADS])
            ez = sb2("ez", [128, TILES, HEADS])
            el = sb2("el", [128, TILES, HEADS])
            prob = sb2("prob", [128, TILES, HEADS])

            edges_in = [sem2("edges_in0"), sem2("edges_in1")]
            gathered = [sem2("gathered0"), sem2("gathered1")]
            (prep_done, pidx_ready, idx_ready, oh_ready, oht_psum, oht_ready, slog_ready, slogT_ready, vend_ready,
             vT_psum, vT_ready, nmax_psum, tab_ready, dm_ready, shrink_ready, edge_psum, el_ready, prob_ready,
             msg_ready, agg_done, acc_done, set_once, ids_ready, dst_ready, ends_ready, gat_step, waited,
             ident_ready, ohf_ready, adp_ready, cand_ready, mnew_ready, mx_kept, acc_shrunk, edge_step) = map(sem2, (
                 "prep_done", "pidx_ready", "idx_ready", "oh_ready", "oht_psum", "oht_ready", "slog_ready",
                 "slogT_ready", "vend_ready", "vT_psum", "vT_ready", "nmax_psum", "tab_ready", "dm_ready",
                 "shrink_ready", "edge_psum", "el_ready", "prob_ready", "msg_ready", "agg_done", "acc_done",
                 "set_once", "ids_ready", "dst_ready", "ends_ready", "gat_step", "waited", "ident_ready",
                 "ohf_ready", "adp_ready", "cand_ready", "mnew_ready", "mx_kept", "acc_shrunk", "edge_step"))
            block = c2.enter_context(nc.Block())

            pidx_p = bank[0][:, 0:2 * TILES]
            slogT_p = bank[1][0:H18, 0:128]
            vT_p = bank[2][:, 0:H18].rearrange("p (h i) -> p h i", h=HEADS)
            nmax_p = bank[3][0:WIN, 0:TILES * (3 * HEADS + 1)].rearrange("p (i h) -> p i h", i=TILES)
            edge_p = bank[4][:, 0:TILES * 6 * HEADS].rearrange("p (i h) -> p i h", i=TILES)
            agg_p = bank[5][0:WIN, 0:MSG]
            def g_bank(u, q, g):
                return (q + g) % 2
            GT = 6
            GROUPS = TILES // GT
            oht_p = [bank[6 + b][0:WIN, :].bitcast(BF16)[:, 0:GT * 128] for b in range(2)]

            def after(eng, signal, count):
                if not (isinstance(count, int) and count <= 0):
                    eng.wait_ge(signal, count)

            def schedule(eng, index, spread, compute):
                index(0, 0, 0)
                index(1, 1, 0)
                spread(0, 0, 0)
                spread(1, 1, 0)
                compute(0, 0, 0)
                n_pairs = eng.value_load(pairs_i[0:1, 0:1], min_val=NW // 2, max_val=(NW + EXTRA) // 2)
                with eng.Fori(0, n_pairs) as k:
                    spread(2 * k + 2, 0, k + 1)
                    compute(2 * k + 1, 1, k)
                    spread(2 * k + 3, 1, k + 1)
                    compute(2 * k + 2, 0, k + 1)

            def nothing(u, q, turn):
                pass

            @block.sync
            def _(sp):
                def load(u, q, turn):
                    after(sp, prep_done, u - 1)
                    off = sp.value_load(units_i[0:1, 1, bass.ds(u, 1)], min_val=0, max_val=EDGES)
                    sp.dma_start(raw[q][0:TILES, :], dst_f[bass.ds(off, UNIT)].rearrange("(i p) -> i p", p=128)).then_inc(edges_in[q], 16)
                    sp.dma_start(raw[q][TILES:2 * TILES, :], src_f[bass.ds(off, UNIT)].rearrange("(i p) -> i p", p=128)).then_inc(edges_in[q], 16)
                    for h in range(HEADS):
                        sp.dma_start(dst_x[q][TILES * h:TILES * h + TILES, :],
                                     dst_f[bass.ds(off, UNIT)].rearrange("(i p) -> i p", p=128)).then_inc(edges_in[q], 16)
                load(0, 0, 0)
                load(1, 1, 0)
                schedule(sp, nothing, nothing, lambda u, q, turn: load(u + 2, q, turn + 1))

            @block.gpsimd
            def _(pool):
                pool.iota(node_id, pattern=[[1, N]], base=0, channel_multiplier=0,
                          allow_small_or_imprecise_dtypes=True).then_inc(ids_ready, 1)

                def gather(u, q, turn):
                    pool.wait_ge(idx_ready, u + 1)
                    for j in range(GROUPS):
                        pool.wait_ge(agg_done, GROUPS * u + j + 1)
                        pool.sem_inc(waited, 1)
                        for i in range(GT * j, GT * j + GT):
                            pool.indirect_dma_start(out=gath[q][:, i, :], out_offset=None, in_=table,
                                                    in_offset=bass.IndirectOffsetOnAxis(src_p[q][:, i:i + 1], 0)
                                                    ).then_inc(gathered[q], 16)
                schedule(pool, nothing, nothing, gather)

            @block.scalar
            def _(act):
                act.activation(ident_h[:, :], ident[:, :], ACT.Copy).then_inc(ident_ready, 1)

                def spread(u, q, turn):
                    after(act, edge_psum, u - 1)
                    for g in range(GROUPS):
                        act.wait_ge(oht_psum, GROUPS * u + g + 1)
                        act.activation(onehotT[q][:, GT * g:GT * g + GT, :], oht_p[g_bank(u, q, g)].rearrange("p (i e) -> p i e", i=GT),
                                       ACT.Copy).then_inc(oht_ready, 1)
                    act.wait_ge(agg_done, GROUPS * u + GROUPS)
                    act.activation(onehot[q], onehot_h[q][:, :, :], ACT.Copy).then_inc(ohf_ready, 1)

                def compute(u, q, turn):
                    act.wait_ge(dm_ready, u + 1)
                    after(act, acc_done, u)
                    act.activation(shrink[:, :], dm[:, :], ACT.Exp).then_inc(shrink_ready, 1)
                    act.wait_ge(el_ready, u + 1)
                    act.activation(prob[:, :, :], el[:, :, :], ACT.Exp).then_inc(prob_ready, 1)
                schedule(act, nothing, spread, compute)

            @block.tensor
            def _(pe):
                pe.sem_inc(agg_done, 2 * GROUPS)
                pe.wait_ge(ident_ready, 1)

                def index(u, q, turn):
                    pe.wait_ge(edges_in[q], 96 * turn + 96)
                    after(pe, idx_ready, u)
                    pe.sem_inc(waited, 1)
                    pe.transpose(pidx_p, raw[q][:, :], ident[0:2 * TILES, 0:2 * TILES]).then_inc(pidx_ready, 1)

                def spread(u, q, turn):
                    pe.wait_ge(oh_ready, u + 1)
                    for g in range(GROUPS):
                        after(pe, oht_ready, GROUPS * u + g - 1)
                        pe.sem_inc(waited, 1)
                        for j in range(GT):
                            last = pe.transpose(oht_p[g_bank(u, q, g)][:, 128 * j:128 * j + 128],
                                                onehot_h[q][:, GT * g + j, :], ident_h[:, :])
                        last.then_inc(oht_psum, 1)

                def compute(u, q, turn):
                    pe.wait_ge(slog_ready, u + 1)
                    pe.transpose(slogT_p, slog[:, :, :].rearrange("p h i -> p (h i)"), ident[:, :]).then_inc(slogT_ready, 1)
                    index(u + 2, q, turn + 1)
                    pe.wait_ge(vend_ready, u + 1)
                    pe.sem_inc(waited, 1)
                    pe.transpose(vT_p.rearrange("p h i -> p (h i)"), vend[:, :], ident[0:H18, 0:H18]).then_inc(vT_psum, 1)
                    pe.wait_ge(vT_ready, u + 1)
                    pe.sem_inc(waited, 1)
                    for i in range(TILES):
                        last = pe.matmul(nmax_p[:, i, :], onehot_h[q][:, i, :], vT[:, i, :], start=True, stop=True)
                    last.then_inc(nmax_psum, 1)
                    pe.wait_ge(tab_ready, u + 1)
                    pe.wait_ge(oht_ready, GROUPS * u + GROUPS)
                    pe.sem_inc(waited, 1)
                    for i in range(TILES):
                        last = pe.matmul(edge_p[:, i, :], onehotT[q][:, i, :], tab[:, :], start=True, stop=True)
                    last.then_inc(edge_psum, 1)
                    after(pe, acc_done, u)
                    pe.wait_ge(ohf_ready, u + 1)
                    for g in range(GROUPS):
                        pe.wait_ge(msg_ready, GROUPS * u + g + 1)
                        for i in range(GT * g, GT * g + GT):
                            last = pe.matmul(agg_p, onehot[q][:, i, :], gath[q][:, i, 0:MSG], start=(i == 0), stop=(i == TILES - 1))
                        last.then_inc(agg_done, 1)
                schedule(pe, index, spread, compute)

            @block.vector
            def _(dve):
                for q in range(2):
                    dve.memset(ends[q][:, :], 1.0).then_inc(set_once, 1)
                dve.memset(vT[:, :, :], 1.0).then_inc(set_once, 1)
                dve.wait_ge(set_once, 3)
                dve.wait_ge(ids_ready, 1)
                CHAIN = 11
                dve.tensor_copy(ad_parts[:, :, 0:HEADS], ad_l[:, :, :]).then_inc(set_once, 1)
                dve.wait_ge(set_once, 4)
                dve.tensor_tensor(ad_rest[:, :, :], ad_l[:, :, :], ad_parts[:, :, 0:HEADS], ALU.subtract).then_inc(set_once, 1)
                dve.wait_ge(set_once, 5)
                dve.tensor_copy(ad_parts[:, :, HEADS:2 * HEADS], ad_rest[:, :, :]).then_inc(set_once, 1)
                dve.wait_ge(set_once, 6)
                dve.tensor_tensor(ad_parts[:, :, 2 * HEADS:3 * HEADS], ad_rest[:, :, :], ad_parts[:, :, HEADS:2 * HEADS],
                                  ALU.subtract).then_inc(set_once, 1)
                dve.wait_ge(set_once, 7)

                def index(u, q, turn):
                    dve.wait_ge(pidx_ready, u + 1)
                    dve.tensor_copy(dst_p[q][:, :], pidx_p[:, 0:TILES]).then_inc(dst_ready, 1)
                    dve.tensor_copy(src_p[q][:, :], pidx_p[:, TILES:2 * TILES]).then_inc(idx_ready, 1)

                def spread(u, q, turn):
                    win = dve.value_load(units_i[0:1, 0, bass.ds(u, 1)], min_val=0, max_val=NW - 1)
                    dve.wait_ge(dst_ready, u + 1)
                    dve.wait_ge(agg_done, GROUPS * u + GROUPS)
                    dve.tensor_tensor(onehot_h[q][:, :, :], dst_p[q][:, :].unsqueeze(2).to_broadcast([128, TILES, WIN]),
                                      node_id[:, bass.ds(win * WIN, WIN)].unsqueeze(1).to_broadcast([128, TILES, WIN]),
                                      ALU.is_equal).then_inc(oh_ready, 1)
                    dve.wait_ge(edges_in[q], 96 * turn + 96)
                    dve.tensor_tensor(ends[q][:, 1:128], dst_x[q][:, 1:128], dst_x[q][:, 0:127], ALU.not_equal).then_inc(ends_ready, 1)
                    dve.wait_ge(ends_ready, u + 1)
                    dve.tensor_scalar(cut[q][:, :], ends[q][:, 0:128], -BIG, None, ALU.mult).then_inc(prep_done, 1)

                def compute(u, q, turn):
                    win = dve.value_load(units_i[0:1, 0, bass.ds(u, 1)], min_val=0, max_val=NW - 1)
                    n = 0

                    def chain(ins):
                        nonlocal n
                        n += 1
                        ins.then_inc(gat_step, 1)
                        dve.wait_ge(gat_step, CHAIN * u + n)

                    def parts(out3, value, rest):
                        chain(dve.tensor_copy(out3[0], value))
                        chain(dve.tensor_tensor(rest, value, out3[0], ALU.subtract))
                        chain(dve.tensor_copy(out3[1], rest))
                        return dve.tensor_tensor(out3[2], rest, out3[1], ALU.subtract)
                    ad_w = ad_l[:, bass.ds(win, 1), :].rearrange("p w h -> p (w h)")
                    mx_w = mx_l[:, bass.ds(win, 1), :].rearrange("p w h -> p (w h)")
                    acc_w = acc[:, bass.ds(win, 1), 0:MSG].rearrange("p w r -> p (w r)")
                    acc_wh = acc_w.rearrange("p (h r) -> p h r", h=HEADS)
                    adp_w = ad_parts[:, bass.ds(win, 1), :].rearrange("p w h -> p (w h)")
                    dve.wait_ge(gathered[q], 16 * TILES * (turn + 1))
                    dve.tensor_copy(slog[:, :, :], gath[q][:, :, MSG:ROW].rearrange("p i h -> p h i")).then_inc(slog_ready, 1)
                    dve.tensor_scalar(tab[:, 0:3 * HEADS], adp_w, 1.0, None, ALU.mult).then_inc(adp_ready, 1)
                    dve.wait_ge(slogT_ready, u + 1)
                    dve.wait_ge(prep_done, u + 1)
                    chain(dve.tensor_tensor_scan(vmax[:, :], cut[q][:, :], slogT_p, -BIG, ALU.add, ALU.max))
                    dve.tensor_tensor(vend[:, :], vmax[:, :], ends[q][:, 1:129], ALU.mult).then_inc(vend_ready, 1)
                    index(u + 2, q, turn + 1)
                    dve.wait_ge(vT_psum, u + 1)
                    parts([vT[:, :, HEADS * j:HEADS * j + HEADS].rearrange("p i h -> p h i") for j in range(3)],
                          vT_p, vrest[:, :, :]).then_inc(vT_ready, 1)
                    dve.wait_ge(nmax_psum, u + 1)
                    dve.tensor_reduce(cand[:, :, :], nmax_p[:, :, 0:3 * HEADS].rearrange("p i (j h) -> p h i j", j=3),
                                      AX.X, ALU.add).then_inc(cand_ready, 1)
                    dve.tensor_scalar(absent[:, :], nmax_p[:, :, 3 * HEADS], 0.0, -BIG, ALU.is_equal, ALU.mult).then_inc(cand_ready, 1)
                    dve.wait_ge(cand_ready, 2 * u + 2)
                    chain(dve.tensor_tensor(cand[:, :, :], cand[:, :, :], absent[:, :].unsqueeze(1).to_broadcast([WIN, HEADS, TILES]), ALU.add))
                    chain(dve.tensor_reduce(bmax[:, :], cand[:, :, :], AX.X, ALU.max))
                    chain(dve.tensor_tensor(zt[:, :], bmax[:, :], ad_w, ALU.add))
                    chain(dve.scalar_tensor_tensor(out=zt[:, :], in0=zt[:, :], scalar=SLOPE, in1=zt[:, :],
                                                   op0=ALU.mult, op1=ALU.max))
                    dve.tensor_tensor(mnew[:, :], zt[:, :], mx_w, ALU.max).then_inc(mnew_ready, 1)
                    dve.wait_ge(mnew_ready, u + 1)
                    parts([tab[:, HEADS * j:HEADS * j + HEADS] for j in range(3, 6)], mnew[:, :], mrest[:, :]).then_inc(tab_ready, 1)
                    dve.tensor_tensor(dm[:, :], mx_w, mnew[:, :], ALU.subtract).then_inc(dm_ready, 1)
                    dve.wait_ge(dm_ready, u + 1)
                    dve.tensor_scalar(mx_w, mnew[:, :], 1.0, None, ALU.mult).then_inc(mx_kept, 1)
                    dve.wait_ge(shrink_ready, u + 1)
                    dve.tensor_tensor(acc_wh, acc_wh, shrink[:, :].unsqueeze(2).to_broadcast([WIN, HEADS, HR]), ALU.mult).then_inc(acc_shrunk, 1)
                    dve.wait_ge(edge_psum, u + 1)
                    edge_steps(u, q)
                    dve.wait_ge(prob_ready, u + 1)
                    for j in range(GROUPS):
                        rows = gath[q][:, GT * j:GT * j + GT, 0:MSG].rearrange("p i (h r) -> p i h r", h=HEADS)
                        dve.tensor_tensor(rows, rows, prob[:, GT * j:GT * j + GT, :].unsqueeze(3).to_broadcast([128, GT, HEADS, HR]),
                                          ALU.mult).then_inc(msg_ready, 1)
                    dve.wait_ge(acc_shrunk, u + 1)
                    dve.wait_ge(agg_done, GROUPS * u + 3 * GROUPS)
                    dve.tensor_tensor(acc_w, acc_w, agg_p, ALU.add).then_inc(acc_done, 1)
                    assert n == CHAIN, n

                def edge_steps(u, q):
                    n = 0

                    def chain(ins):
                        nonlocal n
                        n += 1
                        ins.then_inc(edge_step, 1)
                        dve.wait_ge(edge_step, 4 * u + n)
                    chain(dve.tensor_reduce(by_edge[:, :, :, :], edge_p.rearrange("p i (g j h) -> p g i h j", g=2, j=3), AX.X, ALU.add))
                    chain(dve.tensor_tensor(ez[:, :, :], slog[:, :, :].rearrange("p h i -> p i h"), by_edge[:, 0, :, :], ALU.add))
                    flat = ez[:, :, :].rearrange("p i h -> p (i h)")
                    chain(dve.scalar_tensor_tensor(out=flat, in0=flat, scalar=SLOPE, in1=flat, op0=ALU.mult, op1=ALU.max))
                    chain(dve.tensor_tensor(ez[:, :, :], ez[:, :, :], by_edge[:, 1, :, :], ALU.subtract))
                    dve.tensor_scalar(el[:, :, :], ez[:, :, :], 0.0, None, ALU.min).then_inc(el_ready, 1)
                schedule(dve, index, spread, compute)

        with ExitStack() as c3:
            def sb3(name, shape, dt=F32):
                return c3.enter_context(nc.sbuf_tensor(name, shape, dt))

            def sem3(name):
                return c3.enter_context(nc.semaphore(name))
            WB = 5
            gbias = sb3("gbias", [WIN, D])
            rden = sb3("rden", [WIN, NW, HEADS])
            stats3 = sb3("stats3", [WIN, WB, 6])
            mv3 = sb3("mv3", [WIN, WB, 2])
            var3 = sb3("var3", [WIN, WB])
            sd3 = sb3("sd3", [WIN, WB])
            inv3 = sb3("inv3", [WIN, WB])
            t3 = sb3("t3", [WIN, WB])
            y3 = sb3("y3", [WIN, WB, D])
            gat = y3
            y3T = sb3("y3T", [128, WB, 2, WIN])
            (bias_in, rden_ready, x1_step, var3_ready, sd3_ready, y3_ready, y3T_psum, y3T_ready,
             proj_psum, proj_done, inv_ready, waited3) = map(sem3, ("bias_in", "rden_ready", "x1_step", "var3_ready",
             "sd3_ready", "y3_ready", "y3T_psum", "y3T_ready",
             "proj_psum", "proj_done", "inv_ready", "waited3"))
            block = c3.enter_context(nc.Block())
            y3T_p = [bank[i][:, 0:2 * WIN].rearrange("p (a n) -> p a n", a=2) for i in range(2)]
            proj_p = [[bank[2 + 2 * i + j][:, 0:4 * WIN].rearrange("p (s n) -> p s n", s=4) for j in range(2)]
                      for i in range(2)]

            @block.sync
            def _(sp):
                sp.dma_start(gbias[:, :], gnn_bias.partition_broadcast(WIN)).then_inc(bias_in, 16)

            @block.scalar
            def _(act):
                with act.Fori(0, NW // WB) as b:
                    act.wait_ge(var3_ready, b + 1)
                    act.activation(sd3[:, :], var3[:, :], ACT.Sqrt).then_inc(sd3_ready, 1)
                    for i in range(WB):
                        act.wait_ge(y3T_psum, WB * b + i + 1)
                        act.activation(y3T[:, i, :, :], y3T_p[i % 2], ACT.Copy).then_inc(y3T_ready, 1)

            @block.vector
            def _(dve):
                dve.wait_ge(bias_in, 16)
                dve.reciprocal(rden[:, :, :], acc[:, :, 0:MSG].rearrange("p w (h r) -> p w h r", h=HEADS)[:, :, :, HD]
                               ).then_inc(rden_ready, 1)
                dve.wait_ge(rden_ready, 1)
                STEPS = 3 * WB + 2 * WB + 4

                def body(b):
                    n = 0

                    def each(make):
                        nonlocal n
                        for i in range(WB):
                            make(i).then_inc(x1_step, 1)
                        n += WB
                        dve.wait_ge(x1_step, STEPS * b + n)

                    def chain(ins):
                        nonlocal n
                        n += 1
                        ins.then_inc(x1_step, 1)
                        dve.wait_ge(x1_step, STEPS * b + n)

                    def win(t, i, size):
                        return t[:, bass.ds(WB * b + i, 1), 0:size].rearrange("p w r -> p (w r)")
                    each(lambda i: dve.tensor_tensor(
                        gat[:, i, :].rearrange("p (h r) -> p h r", h=HEADS),
                        win(acc, i, MSG).rearrange("p (h r) -> p h r", h=HEADS)[:, :, 0:HD],
                        win(rden, i, HEADS).unsqueeze(2).to_broadcast([WIN, HEADS, HD]), ALU.mult))
                    each(lambda i: dve.tensor_tensor(gat[:, i, :], gat[:, i, :], gbias[:, :], ALU.add))
                    each(lambda i: dve.tensor_tensor(win(x1, i, D), win(x1, i, D), gat[:, i, :], ALU.add))
                    dve.sem_inc(waited3, 1)
                    each(lambda i: dve.bn_stats(stats3[:, i, :], win(x1, i, D)))
                    dve.sem_inc(waited3, 1)
                    each(lambda i: dve.bn_aggr(mv3[:, i, :], stats3[:, i, :]))
                    dve.tensor_scalar(var3[:, :], mv3[:, :, 1], EPS, None, ALU.add).then_inc(var3_ready, 1)
                    dve.wait_ge(sd3_ready, b + 1)
                    chain(dve.reciprocal(inv3[:, :], sd3[:, :]))
                    chain(dve.tensor_tensor(t3[:, :], inv3[:, :], inv3[:, :], ALU.mult))
                    chain(dve.tensor_tensor(t3[:, :], t3[:, :], var3[:, :], ALU.mult))
                    chain(dve.tensor_scalar(t3[:, :], t3[:, :], -0.5, 1.5, ALU.mult, ALU.add))
                    assert n == STEPS, n
                    dve.tensor_tensor(inv3[:, :], inv3[:, :], t3[:, :], ALU.mult).then_inc(inv_ready, 1)
                    dve.wait_ge(inv_ready, b + 1)
                    for i in range(WB):
                        dve.tensor_scalar(y3[:, i, :], win(x1, i, D), mv3[:, i, 0:1], inv3[:, i:i + 1],
                                          ALU.subtract, ALU.mult).then_inc(y3_ready, 1)

                def evacuate(b):
                    for i in range(WB):
                        dve.wait_ge(proj_psum, WB * b + i + 1)
                        for j in range(2):
                            dst_v = xproj[:, 4 * j:4 * j + 4, :, bass.ds(5 * (WB * b + i), 5)].rearrange("p s k c -> p s c k")
                            for s in range(4):
                                dve.tensor_scalar(dst_v[:, s, :, :], proj_p[i % 2][j][:, s, :].rearrange("p (c k) -> p c k", c=5),
                                                  biasT[:, 4 * j + s:4 * j + s + 1], None, ALU.add).then_inc(proj_done, 1)
                    dve.wait_ge(proj_done, 8 * WB * b + 8 * WB)
                    dve.sem_inc(waited3, 1)
                with dve.Fori(0, NW // WB) as b:
                    body(b)
                    evacuate(b)

            @block.tensor
            def _(pe):
                def project(b, i):
                    pe.wait_ge(y3T_ready, WB * b + i + 1)
                    if i >= 2:
                        pe.wait_ge(proj_done, 8 * (WB * b + i - 1))
                    for j in range(2):
                        for s in range(4):
                            m = SLOT_GATE[4 * j + s]
                            for a in range(2):
                                last = pe.matmul(proj_p[i % 2][j][:, s, :], wihT[:, a, 128 * m:128 * m + 128],
                                                 y3T[:, i, a, :], start=(a == 0), stop=(a == 1))
                    last.then_inc(proj_psum, 1)
                with pe.Fori(0, NW // WB) as b:
                    for i in range(WB):
                        pe.wait_ge(y3_ready, WB * b + i + 1)
                        if i >= 2:
                            pe.wait_ge(y3T_ready, WB * b + i - 1)
                        for a in range(2):
                            last = pe.transpose(y3T_p[i % 2][:, a, :], y3[:, i, 128 * a:128 * a + 128], ident[0:WIN, 0:WIN])
                        last.then_inc(y3T_psum, 1)
                        if i >= 1:
                            project(b, i - 1)
                    project(b, WB - 1)

        with ExitStack() as c4:
            def sb4(name, shape, dt=F32):
                return c4.enter_context(nc.sbuf_tensor(name, shape, dt))

            def sem4(name):
                return c4.enter_context(nc.semaphore(name))
            gates = [sb4(f"gates{q}", [128, 8, 63]) for q in range(2)]
            fc = [sb4(f"fc{q}", [128, 2, 63]) for q in range(2)]
            ig = [sb4(f"ig{q}", [128, 2, 63]) for q in range(2)]
            th = [sb4(f"th{q}", [128, 2, 63]) for q in range(2)]
            diff = sb4("diff", [128, 2, 2, CH - 1])
            agree = sb4("agree", [128, 1])
            again_f = sb4("again_f", [1, 1])
            again = sb4("again", [1, 1], I32)
            h_ready, gates_psum, gates_sum, sig_done, tanh_done, cell_ready, th_ready, cell_parts = (
                [sem4(f"{name}{q}") for q in range(2)] for name in
                ("h_ready", "gates_psum", "gates_sum", "sig_done", "tanh_done", "cell_ready", "th_ready", "cell_parts"))
            zeroed, check_step, agree_ready, agree_psum, again_ready, restarted, waited4 = map(
                sem4, ("zeroed", "check_step", "agree_ready", "agree_psum", "again_ready", "restarted", "waited4"))
            block = c4.enter_context(nc.Block())
            gates_p = [bank[q][:, 0:504].rearrange("p (s n) -> p s n", s=8) for q in range(2)]
            agree_p = bank[2][0:1, 0:1]

            def phases(eng, step, reset, check):
                early = WARM - KS
                with eng.Fori(0, early) as s:
                    step(s, 0, 0, s + (KS - early), 2, 2)
                with eng.Fori(0, KS) as s:
                    step(s + early, 0, 0, s, 1, 1)
                if reset:
                    reset(0, WARM)
                with eng.Fori(0, KS) as s:
                    step(s + WARM, s, s + 1, s, 0, 0)
                if check:
                    check()
                eng.wait_ge(again_ready, 1)
                flag = eng.value_load(again[0:1, 0:1], min_val=0, max_val=1)
                with eng.If(flag > 0):
                    with eng.Fori(0, CH - 1) as r:
                        base = r * KS + (WARM + KS)
                        if reset:
                            reset(r + 1, base)
                        with eng.Fori(0, KS) as s:
                            step(base + s, s, s + 1, s, 0, 0)

            def span(q, lo):
                a, b = HALF[q]
                return max(a, lo), b

            def hrow(row, a, b):
                return h_rows[:, :, bass.ds(row, 1), a:b].rearrange("p a k c -> p a (k c)")

            @block.sync
            def _(sp):
                sp.wait_ge(again_ready, 1)

            @block.tensor
            def _(pe):
                pe.wait_ge(zeroed, 3)

                def step(n, row_in, row_out, k, lo, shift):
                    for q in range(2):
                        a, b = span(q, lo)
                        pe.wait_ge(h_ready[q], n + 1)
                        for s, m in enumerate(SLOT_GATE):
                            for kk in range(2):
                                last = pe.matmul(gates_p[q][:, s, 0:b - a], whhT[:, kk, 128 * m:128 * m + 128],
                                                 h_rows[:, kk, bass.ds(row_in, 1), a:b].rearrange("p k c -> p (k c)"),
                                                 start=(kk == 0), stop=(kk == 1))
                        last.then_inc(gates_psum[q], 1)

                def check():
                    pe.wait_ge(agree_ready, 1)
                    pe.matmul(agree_p, ones[:, 0:1], agree[:, :], start=True, stop=True).then_inc(agree_psum, 1)
                phases(pe, step, None, check)

            @block.scalar
            def _(act):
                def step(n, row_in, row_out, k, lo, shift):
                    for q in range(2):
                        a, b = span(q, lo)
                        g = gates[q][:, :, 0:b - a]
                        act.wait_ge(gates_sum[q], n + 1)
                        act.activation(g[:, 0:6, :], g[:, 0:6, :], ACT.Sigmoid).then_inc(sig_done[q], 1)
                        act.activation(g[:, 6:8, :], g[:, 6:8, :], ACT.Tanh).then_inc(tanh_done[q], 1)
                    for q in range(2):
                        a, b = span(q, lo)
                        act.wait_ge(cell_ready[q], n + 1)
                        act.activation(th[q][:, :, 0:b - a], cell[:, :, a:b], ACT.Tanh).then_inc(th_ready[q], 1)
                phases(act, step, None, None)

            @block.vector
            def _(dve):
                dve.memset(hT[:, :], 0.0).then_inc(zeroed, 1)
                dve.memset(cell[:, :, :], 0.0).then_inc(zeroed, 1)
                dve.memset(start_c[:, :, :], 0.0).then_inc(zeroed, 1)
                dve.wait_ge(zeroed, 3)
                for q in range(2):
                    dve.engine_nop().then_inc(h_ready[q], 1)
                dve.wait_ge(h_ready[1], 1)
                dve.wait_ge(h_ready[0], 1)

                def step(n, row_in, row_out, k, lo, shift):
                    for q in range(2):
                        a, b = span(q, lo)
                        g = gates[q][:, :, 0:b - a]
                        dve.wait_ge(gates_psum[q], n + 1)
                        dve.wait_ge(h_ready[q], n + 1)
                        dve.tensor_tensor(g, gates_p[q][:, :, 0:b - a],
                                          xproj[:, :, bass.ds(k, 1), a - shift:b - shift].rearrange("p s k c -> p s (k c)"),
                                          ALU.add).then_inc(gates_sum[q], 1)
                    for q in range(2):
                        a, b = span(q, lo)
                        g = gates[q][:, :, 0:b - a]
                        dve.wait_ge(sig_done[q], n + 1)
                        dve.tensor_tensor(fc[q][:, :, 0:b - a], g[:, 2:4, :], cell[:, :, a:b], ALU.mult).then_inc(cell_parts[q], 1)
                        dve.wait_ge(tanh_done[q], n + 1)
                        dve.tensor_tensor(ig[q][:, :, 0:b - a], g[:, 0:2, :], g[:, 6:8, :], ALU.mult).then_inc(cell_parts[q], 1)
                        dve.wait_ge(cell_parts[q], 2 * n + 2)
                        dve.tensor_tensor(cell[:, :, a:b], fc[q][:, :, 0:b - a], ig[q][:, :, 0:b - a], ALU.add).then_inc(cell_ready[q], 1)
                    for q in range(2):
                        a, b = span(q, lo)
                        g = gates[q][:, :, 0:b - a]
                        dve.wait_ge(th_ready[q], n + 1)
                        dve.tensor_tensor(hrow(row_out, a, b), g[:, 4:6, :], th[q][:, :, 0:b - a], ALU.mult).then_inc(h_ready[q], 1)

                def reset(r, n):
                    for q in range(2):
                        dve.wait_ge(h_ready[q], n + 1)
                        dve.wait_ge(cell_ready[q], n)
                    if isinstance(r, int):
                        dve.tensor_copy(start_c[:, :, :], cell[:, :, :]).then_inc(restarted, 1)
                        dve.wait_ge(restarted, 1)
                    else:
                        dve.tensor_copy(start_c[:, :, 1:CH], cell[:, :, 0:CH - 1]).then_inc(restarted, 1)
                        dve.wait_ge(restarted, 3 * r - 1)
                        dve.tensor_copy(cell[:, :, :], start_c[:, :, :]).then_inc(restarted, 1)
                        dve.tensor_copy(h_rows[:, :, 0, 1:CH], h_rows[:, :, KS, 0:CH - 1]).then_inc(restarted, 1)
                        dve.wait_ge(restarted, 3 * r + 1)
                        dve.sem_inc(waited4, 1)

                def check():
                    n = WARM + KS
                    for q in range(2):
                        dve.wait_ge(h_ready[q], n + 1)
                        dve.wait_ge(cell_ready[q], n)
                    dve.tensor_tensor(diff[:, 0, :, :], h_rows[:, :, 0, 1:CH], h_rows[:, :, KS, 0:CH - 1], ALU.subtract).then_inc(check_step, 1)
                    dve.tensor_tensor(diff[:, 1, :, :], start_c[:, :, 1:CH], cell[:, :, 0:CH - 1], ALU.subtract).then_inc(check_step, 1)
                    dve.wait_ge(check_step, 2)
                    flat = diff[:, :, :, :].rearrange("p x a c -> p (x a c)")
                    dve.scalar_tensor_tensor(out=flat, in0=flat, scalar=-1.0, in1=flat, op0=ALU.mult, op1=ALU.max).then_inc(check_step, 1)
                    dve.wait_ge(check_step, 3)
                    dve.tensor_scalar(flat, flat, TOL, None, ALU.is_le).then_inc(check_step, 1)
                    dve.wait_ge(check_step, 4)
                    dve.tensor_reduce(agree[:, :], flat, AX.X, ALU.min).then_inc(agree_ready, 1)
                    dve.wait_ge(agree_psum, 1)
                    dve.tensor_scalar(again_f[:, :], agree_p, 127.5, None, ALU.is_lt).then_inc(check_step, 1)
                    dve.wait_ge(check_step, 5)
                    dve.tensor_copy(again[:, :], again_f[:, :]).then_inc(again_ready, 1)
                phases(dve, step, reset, check)

        with ExitStack() as c5:
            def sb5(name, shape, dt=F32):
                return c5.enter_context(nc.sbuf_tensor(name, shape, dt))

            def sem5(name):
                return c5.enter_context(nc.semaphore(name))
            masked = arena[:, 0:2 * N].rearrange("p (a t) -> p a t", a=2)
            incl = arena[:, 2 * N:4 * N].rearrange("p (a t) -> p a t", a=2)
            res = arena[:, 4 * N:6 * N].rearrange("p (a t) -> p a t", a=2)
            wdiff = sb5("wdiff", [128, 2, 128])
            wd = sb5("wd", [128, 2])
            blin = sb5("blin", [128, 2])
            tie = sb5("tie", [128, 1])
            nfw = sb5("nfw", [128, 2])
            fmb = sb5("fmb", [128, 2])
            tbw = sb5("tbw", [128, 2])
            zeros = arena[:, 6 * N:7 * N]
            (blin_in, out_step, wdiff_ready, logit_psum, mask_done, incl_done, scaled, tbw_ready, res_done,
             resT_psum, x_done, stored, zero_ready) = map(sem5, ("blin_in", "out_step", "wdiff_ready", "logit_psum", "mask_done",
             "incl_done", "scaled", "tbw_ready", "res_done", "resT_psum", "x_done", "stored", "zero_ready"))
            block = c5.enter_context(nc.Block())
            RB = 4
            blocks = [(k, min(k + RB, KS)) for k in range(0, KS, RB)]
            logit_p = [bank[i][:, :] for i in range(4)]
            resT_p = [bank[4 + i][0:WIN, 0:D] for i in range(4)]

            def in_time(v, k0, k1):
                return v.rearrange("p (c k) -> p k c", k=KS)[:, k0:k1, :]

            @block.sync
            def _(sp):
                sp.dma_start(blin[:, :], b_lin.partition_broadcast(128)).then_inc(blin_in, 16)
                rows = out.rearrange("(w p) f -> p w f", p=WIN)
                for b in range(5):
                    sp.wait_ge(x_done, 5 * b + 5)
                    sp.dma_start(rows[:, 5 * b:5 * b + 5, :], x1[:, 5 * b:5 * b + 5, :]).then_inc(stored, 16)
                sp.wait_ge(stored, 80)

            @block.gpsimd
            def _(pool):
                pool.memset(zeros, 0.0).then_inc(zero_ready, 1)

            @block.tensor
            def _(pe):
                pe.wait_ge(wdiff_ready, 2)
                for i, (k0, k1) in enumerate(blocks):
                    if i >= 4:
                        pe.wait_ge(mask_done, 2 * (i - 3))
                    for a in range(2):
                        last = pe.matmul(logit_p[i % 4][:, 0:(k1 - k0) * CH], wdiff[:, a, :],
                                         h_rows[:, a, 1 + k0:1 + k1, :].rearrange("p k c -> p (k c)"),
                                         start=(a == 0), stop=(a == 1))
                    last.then_inc(logit_psum, 1)
                pe.wait_ge(res_done, 2)
                for w in range(NW):
                    if w >= 4:
                        pe.wait_ge(x_done, w - 3)
                    for a in range(2):
                        last = pe.transpose(resT_p[w % 4][:, 128 * a:128 * a + 128], res[:, a, WIN * w:WIN * w + WIN], ident[:, :])
                    last.then_inc(resT_psum, 1)

            @block.scalar
            def _(act):
                act.wait_ge(tbw_ready, 1)
                for a in range(2):
                    act.activation(incl[:, a, :], incl[:, a, :], ACT.Identity, bias=tbw[:, a:a + 1],
                                   scale=fmb[:, a:a + 1]).then_inc(scaled, 1)

            @block.vector
            def _(dve):
                n = 0

                def chain(ins):
                    nonlocal n
                    n += 1
                    ins.then_inc(out_step, 1)
                    dve.wait_ge(out_step, n)
                chain(dve.tensor_tensor(wd[:, :], smallT[:, 18:20], smallT[:, 16:18], ALU.subtract))
                for a in range(2):
                    dve.tensor_scalar(wdiff[:, a, :], ones[:, :], wd[:, a:a + 1], None, ALU.mult).then_inc(wdiff_ready, 1)
                dve.wait_ge(blin_in, 16)
                chain(dve.tensor_tensor(tie[:, :], blin[:, 0:1], blin[:, 1:2], ALU.subtract))
                chain(dve.tensor_scalar(nfw[:, :], smallT[:, 20:22], -1.0, None, ALU.mult))
                chain(dve.tensor_tensor(fmb[:, :], smallT[:, 20:22], smallT[:, 22:24], ALU.subtract))
                for i, (k0, k1) in enumerate(blocks):
                    dve.wait_ge(logit_psum, i + 1)
                    for a in range(2):
                        dve.scalar_tensor_tensor(out=in_time(masked[:, a, :], k0, k1),
                                                 in0=logit_p[i % 4][:, 0:(k1 - k0) * CH].rearrange("p (k c) -> p k c", c=CH),
                                                 scalar=tie[:, :], in1=h_rows[:, a, 1 + k0:1 + k1, :],
                                                 op0=ALU.is_gt, op1=ALU.mult).then_inc(mask_done, 1)
                dve.wait_ge(mask_done, 2 * len(blocks))
                dve.wait_ge(zero_ready, 1)
                for a in range(2):
                    dve.tensor_tensor_scan(incl[:, a, :], masked[:, a, :], zeros, 0.0, ALU.add, ALU.add).then_inc(incl_done, 1)
                dve.wait_ge(incl_done, 2)
                dve.tensor_tensor(tbw[:, :], incl[:, :, N - 1], smallT[:, 22:24], ALU.mult).then_inc(tbw_ready, 1)
                for a in range(2):
                    dve.wait_ge(scaled, a + 1)
                    chain(dve.scalar_tensor_tensor(out=masked[:, a, :], in0=masked[:, a, :], scalar=nfw[:, a:a + 1],
                                                   in1=incl[:, a, :], op0=ALU.mult, op1=ALU.add))
                    dve.scalar_tensor_tensor(out=res[:, a, :].rearrange("p (c k) -> p c k", k=KS),
                                             in0=h_rows[:, a, 1:KS + 1, :].rearrange("p k c -> p c k"), scalar=2.0,
                                             in1=masked[:, a, :].rearrange("p (c k) -> p c k", k=KS),
                                             op0=ALU.mult, op1=ALU.add).then_inc(res_done, 1)
                for w in range(NW):
                    dve.wait_ge(resT_psum, w + 1)
                    dve.tensor_tensor(x1[:, w, :], x1[:, w, :], resT_p[w % 4], ALU.add).then_inc(x_done, 1)


_INS = ["x", "src", "dst", "L0_gnn_W", "L0_gnn_att_src", "L0_gnn_att_dst", "L0_gnn_bias", "L0_ffn_W_ih",
        "L0_ffn_W_hh", "L0_ffn_b_ih", "L0_ffn_b_hh", "L0_ffn_W_lin", "L0_ffn_b_lin", "L0_ffn_fw_att",
        "L0_ffn_bw_att"]


def kernel(**inputs):
    import concourse.bacc as bacc
    from concourse.bass_utils import run_bass_kernel_spmd

    nc = bacc.Bacc("TRN2", target_bir_lowering=False, num_devices=1)
    arrays, args = {}, []
    for name in _INS:
        a = np.ascontiguousarray(inputs[name])
        arrays[f"in_{name}"] = a
        args.append(nc.dram_tensor(f"in_{name}", a.shape, mybir.dt.from_np(a.dtype), kind="ExternalInput").ap())
    out = nc.dram_tensor("out", [N, D], F32, kind="ExternalOutput").ap()
    build(nc, *args, out)
    r = run_bass_kernel_spmd(nc, [arrays], core_ids=[0])
    return r.results[0]["out"]
```

```python
from contextlib import ExitStack

import numpy as np

import concourse.bass as bass
from concourse import mybir

F32 = mybir.dt.float32
F16 = mybir.dt.float16
BF16 = mybir.dt.bfloat16
I32 = mybir.dt.int32
ALU = mybir.AluOpType
ACT = mybir.ActivationFunctionType
AX = mybir.AxisListType

N = 3125
D = 256
HEADS, HD = 4, 64
EDGES = 53125
WIN = 125
NW = N // WIN
TILES = 18
UNIT = TILES * 128
HR = HD + 1
MSG = HEADS * HR
ROW = MSG + HEADS
BIG = 1.0e30
EXTRA = EDGES // UNIT
SPAN = 6
SLOTS = NW + EXTRA + 8
CH, KS = 125, 25
WARM = 36
HALF = [(0, 63), (63, CH)]
SLOT_GATE = [0, 1, 2, 3, 6, 7, 4, 5]
TOL = 2.0 ** -20
EPS = 1e-5
SLOPE = 0.2


def build(nc, x, src, dst, gnn_w, att_src, att_dst, gnn_bias, w_ih, w_hh, b_ih, b_hh,
          w_lin, b_lin, fw_att, bw_att, out):
    ctx = ExitStack()

    def sb(name, shape, dt=F32):
        return ctx.enter_context(nc.sbuf_tensor(name, shape, dt))

    def ps(name, shape=(128, 512)):
        return ctx.enter_context(nc.psum_tensor(name, list(shape), F32))

    def sem(name):
        return ctx.enter_context(nc.semaphore(name))

    with ctx:
        table = nc.dram_tensor("node_table", [N, ROW], F32).ap()
        dst_f = nc.dram_tensor("dst_f", [EDGES + UNIT], F32).ap()
        src_f = nc.dram_tensor("src_f", [EDGES + UNIT], F32).ap()

        x1 = sb("x1", [WIN, NW, D])
        hT = sb("hT", [128, 2 * (KS + 1) * CH])
        arena = sb("arena", [128, 8 * N])
        acc_all = sb("acc_all", [128, NW * ROW])
        wihT = sb("wihT", [128, 2, 4 * D])
        whhT = sb("whhT", [128, 2, 4 * D])
        ident = sb("ident", [128, 128])
        ones = sb("ones", [128, 128])
        small = sb("small", [24, 128])
        smallT = sb("smallT", [128, 24])
        biasT = sb("biasT", [128, 8])
        ad_l = sb("ad_l", [WIN, NW, HEADS])
        mx_l = sb("mx_l", [WIN, NW, HEADS])
        units_i = sb("units_i", [1, 2, SLOTS], I32)
        pairs_i = sb("pairs_i", [1, 1], I32)
        cell = sb("cell", [128, 2, CH])
        start_c = sb("start_c", [128, 2, CH])

        acc = acc_all[0:WIN, :].rearrange("p (w r) -> p w r", w=NW)
        h_rows = hT[:, :].rearrange("p (a k c) -> p a k c", a=2, k=KS + 1)
        xproj = arena[:, :].rearrange("p (s k c) -> p s k c", s=8, k=KS)
        at = 0

        def carve(rows, size):
            nonlocal at
            at += size
            return arena[0:rows, at - size:at]
        gath = [carve(128, TILES * ROW).rearrange("p (i r) -> p i r", i=TILES) for _ in range(3)]
        onehot = [carve(128, TILES * 128).rearrange("p (i n) -> p i n", i=TILES) for _ in range(2)]
        onehot_h = [carve(128, TILES * 128 // 2).bitcast(BF16).rearrange("p (i n) -> p i n", i=TILES) for _ in range(2)]
        onehotT = [carve(128, UNIT // 2).bitcast(BF16).rearrange("p (i e) -> p i e", i=TILES) for _ in range(2)]
        node_id = hT[:, 0:N + 3]
        stage_w = [arena[:, i * 8 * D:(i + 1) * 8 * D]
                   .rearrange("p (m d) -> p m d", m=8) for i in range(2)]

        bank = [ps(f"bank{i}") for i in range(8)]

        with ExitStack() as c1:
            def sb1(name, shape, dt=F32):
                return c1.enter_context(nc.sbuf_tensor(name, shape, dt))

            def sem1(name):
                return c1.enter_context(nc.semaphore(name))
            gw = sb1("gw", [128, 2, D])
            att = sb1("att", [WIN, 2, D])
            edge_i = sb1("edge_i", [WIN, 2, EDGES // WIN], I32)
            at = 2 * 8 * D
            edge_f = carve(WIN, 2 * (EDGES // WIN)).rearrange("p (a e) -> p a e", a=2)
            pad = sb1("pad", [128, 2, TILES])
            below = carve(WIN, EDGES // WIN)
            counts = sb1("counts", [WIN, NW + 1])
            stats = sb1("stats", [WIN, NW, 6])
            meanvar = sb1("meanvar", [WIN, NW, 2])
            rstd = sb1("rstd", [WIN, NW])
            tmp = sb1("tmp", [WIN, 3, NW])
            yn = carve(WIN, 5 * D).rearrange("p (b d) -> p b d", b=5)
            ynT = carve(128, 10 * WIN).rearrange("p (b a n) -> p b a n", b=5, a=2)
            prod = carve(WIN, 2 * D).rearrange("p (a d) -> p a d", a=2)
            fst = sb1("fst", [1, NW + 1])
            blk = sb1("blk", [1, NW, EXTRA + 1])
            step_k = sb1("step_k", [1, EXTRA + 1])
            nblk = sb1("nblk", [1, NW])
            zer = sb1("zer", [1, NW])
            uend = sb1("uend", [1, NW + 1])
            ubeg = sb1("ubeg", [1, NW + 1])
            adj = sb1("adj", [1, NW + 1])
            uid = sb1("uid", [1, SLOTS])
            wid = sb1("wid", [1, NW + 1])
            cmp = carve(1, SLOTS * (NW + 1)).rearrange("p (u w) -> p u w", u=SLOTS)
            uwin = sb1("uwin", [1, SLOTS])
            uoff = sb1("uoff", [1, SLOTS])
            pcmp = sb1("pcmp", [1, EXTRA + 2])
            pairs = sb1("pairs", [1, 1])

            x_in, w_in, e_in, att_in, lw_in, sm_in = map(sem1, ("x_in", "w_in", "e_in", "att_in", "lw_in", "sm_in"))
            pool_step, const_done, e_float, scratch = map(sem1, ("pool_step", "const_done", "e_float", "scratch"))
            dve_step, var_ready, sd_ready = map(sem1, ("dve_step", "var_ready", "sd_ready"))
            yn_ready, ynt_psum, ynt_ready, h_psum = map(sem1, ("yn_ready", "ynt_psum", "ynt_ready", "h_psum"))
            h_copied, logit_done, cnt_ready, fst_psum = map(sem1, ("h_copied", "logit_done", "cnt_ready", "fst_psum"))
            wt_psum, wt_copied, smt_psum, tab_out = map(sem1, ("wt_psum", "wt_copied", "smt_psum", "tab_out"))
            units_done = sem1("units_done")
            block = c1.enter_context(nc.Block())

            yT_p = [bank[0][:, 0:2 * WIN].rearrange("p (a n) -> p a n", a=2),
                    bank[1][:, 0:2 * WIN].rearrange("p (a n) -> p a n", a=2)]
            h_p = [bank[2][0:WIN, 0:D], bank[3][0:WIN, 0:D]]
            fst_p = bank[4][0:1, 0:NW + 1]
            wT_p = [bank[5], bank[6]]
            small_p = bank[7][:, 0:24]

            @block.sync
            def _(sp):
                sp.dma_start(edge_i[:, 0, :], dst.rearrange("(p e) -> p e", p=WIN)).then_inc(e_in, 16)
                sp.dma_start(edge_i[:, 1, :], src.rearrange("(p e) -> p e", p=WIN)).then_inc(e_in, 16)
                sp.dma_start(x1[:, :, :], x.rearrange("(w p) f -> p w f", p=WIN)).then_inc(x_in, 16)
                sp.wait_ge(e_float, 2)
                sp.dma_start(dst_f[0:EDGES].rearrange("(p e) -> p e", p=WIN), edge_f[:, 0, :]).then_inc(scratch, 16)
                sp.dma_start(src_f[0:EDGES].rearrange("(p e) -> p e", p=WIN), edge_f[:, 1, :]).then_inc(scratch, 16)
                sp.wait_ge(const_done, 1)
                sp.dma_start(dst_f[EDGES:EDGES + UNIT].rearrange("(p e) -> p e", p=128), pad[:, 0, :]).then_inc(scratch, 16)
                sp.dma_start(src_f[EDGES:EDGES + UNIT].rearrange("(p e) -> p e", p=128), pad[:, 1, :]).then_inc(scratch, 16)
                rows = table.rearrange("(w p) r -> p w r", p=WIN)
                for b in range(5):
                    sp.wait_ge(h_copied, 5 * b + 5)
                    sp.wait_ge(logit_done, 5 * b + 5)
                    sp.dma_start(rows[:, 5 * b:5 * b + 5, :], acc[:, 5 * b:5 * b + 5, :]).then_inc(tab_out, 16)
                sp.wait_ge(scratch, 64)
                sp.wait_ge(tab_out, 80)

            @block.gpsimd
            def _(pool):
                pool.memset(ident[:, :], 0.0).then_inc(pool_step, 1)
                pool.wait_ge(pool_step, 1)
                pool.affine_select(out=ident[:, :], in_=ident[:, :], compare_op=ALU.not_equal, fill=1.0, base=0,
                                   pattern=[[-1, 128]], channel_multiplier=1).then_inc(pool_step, 1)
                pool.memset(ones[:, :], 1.0).then_inc(pool_step, 1)
                pool.memset(pad[:, 0, :], 4096.0).then_inc(pool_step, 1)
                pool.memset(pad[:, 1, :], 0.0).then_inc(pool_step, 1)
                pool.memset(acc[:, :, 0:MSG].rearrange("p w (h r) -> p w h r", h=HEADS)[:, :, :, HD:HR], 1.0).then_inc(pool_step, 1)
                pool.iota(step_k[:, :], pattern=[[UNIT, EXTRA + 1]], base=0, channel_multiplier=0,
                          allow_small_or_imprecise_dtypes=True).then_inc(pool_step, 1)
                pool.iota(uid[:, :], pattern=[[1, SLOTS]], base=0, channel_multiplier=0,
                          allow_small_or_imprecise_dtypes=True).then_inc(pool_step, 1)
                pool.iota(wid[:, :], pattern=[[1, NW + 1]], base=0, channel_multiplier=0,
                          allow_small_or_imprecise_dtypes=True).then_inc(pool_step, 1)
                pool.memset(counts[:, 0:1], 0.0).then_inc(pool_step, 1)
                pool.memset(counts[:, NW:NW + 1], float(EDGES // WIN)).then_inc(pool_step, 1)
                pool.memset(zer[:, :], 0.0).then_inc(pool_step, 1)
                pool.wait_ge(pool_step, 12)
                pool.memset(ubeg[:, 0:1], 0.0).then_inc(const_done, 1)

            @block.scalar
            def _(act):
                act.dma_start(gw[:, :, :], gnn_w.rearrange("(a p) n -> p a n", p=128)).then_inc(w_in, 16)
                act.dma_start(att[:, 0, :], att_src.rearrange("h d -> (h d)").partition_broadcast(WIN)).then_inc(att_in, 16)
                act.dma_start(att[:, 1, :], att_dst.rearrange("h d -> (h d)").partition_broadcast(WIN)).then_inc(att_in, 16)
                act.dma_start(small[0:8, :], b_ih.rearrange("(m p) -> m p", p=128)).then_inc(sm_in, 16)
                act.dma_start(small[8:16, :], b_hh.rearrange("(m p) -> m p", p=128)).then_inc(sm_in, 16)
                act.dma_start(small[16:20, :], w_lin.rearrange("l (a p) -> (l a) p", p=128)).then_inc(sm_in, 16)
                act.dma_start(small[20:22, :], fw_att.rearrange("o (a p) -> (o a) p", p=128)).then_inc(sm_in, 16)
                act.dma_start(small[22:24, :], bw_att.rearrange("o (a p) -> (o a) p", p=128)).then_inc(sm_in, 16)
                act.dma_start(stage_w[0], w_ih.rearrange("(m p) d -> p m d", p=128)).then_inc(lw_in, 16)
                act.dma_start(stage_w[1], w_hh.rearrange("(m p) d -> p m d", p=128)).then_inc(lw_in, 16)
                act.wait_ge(var_ready, 1)
                act.activation(rstd[:, :], tmp[:, 0, :], ACT.Sqrt).then_inc(sd_ready, 1)
                for w in range(NW):
                    act.wait_ge(ynt_psum, w + 1)
                    act.activation(ynT[:, w % 5, :, :], yT_p[w % 2], ACT.Copy).then_inc(ynt_ready, 1)
                    act.wait_ge(h_psum, w + 1)
                    act.activation(acc[:, w, 0:MSG].rearrange("p (h r) -> p h r", h=HEADS)[:, :, 0:HD],
                                   h_p[w % 2].rearrange("p (h r) -> p h r", h=HEADS), ACT.Copy).then_inc(h_copied, 1)
                for g in range(8):
                    act.wait_ge(wt_psum, g + 1)
                    w_t, a, half = (wihT, whhT)[g // 4], (g % 4) // 2, g % 2
                    act.activation(w_t[:, a, 512 * half:512 * half + 512], wT_p[g % 2][:, :], ACT.Copy).then_inc(wt_copied, 1)

            @block.vector
            def _(dve):
                n = 0

                def chain(ins):
                    nonlocal n
                    n += 1
                    ins.then_inc(dve_step, 1)
                    dve.wait_ge(dve_step, n)
                dve.wait_ge(e_in, 32)
                dve.tensor_copy(edge_f[:, 0, :], edge_i[:, 0, :]).then_inc(e_float, 1)
                dve.tensor_copy(edge_f[:, 1, :], edge_i[:, 1, :]).then_inc(e_float, 1)
                dve.wait_ge(x_in, 16)
                for w in range(NW):
                    dve.bn_stats(stats[:, w, :], x1[:, w, :]).then_inc(dve_step, 1)
                n += NW
                dve.wait_ge(dve_step, n)
                for w in range(NW):
                    dve.bn_aggr(meanvar[:, w, :], stats[:, w, :]).then_inc(dve_step, 1)
                n += NW
                dve.wait_ge(dve_step, n)
                dve.tensor_scalar(tmp[:, 0, :], meanvar[:, :, 1], EPS, None, ALU.add).then_inc(var_ready, 1)
                dve.wait_ge(e_float, 2)
                dve.wait_ge(const_done, 1)
                for w in range(1, NW):
                    chain(dve.tensor_scalar(below[:, :], edge_f[:, 0, :], float(WIN * w), 0.0, ALU.is_lt, ALU.add,
                                            accum_out=counts[:, w:w + 1]))
                dve.tensor_copy(counts[:, 0:1], counts[:, 0:1]).then_inc(cnt_ready, 1)
                dve.wait_ge(sd_ready, 1)
                chain(dve.reciprocal(tmp[:, 1, :], rstd[:, :]))
                chain(dve.tensor_tensor(tmp[:, 2, :], tmp[:, 1, :], tmp[:, 1, :], ALU.mult))
                chain(dve.tensor_tensor(tmp[:, 2, :], tmp[:, 2, :], tmp[:, 0, :], ALU.mult))
                chain(dve.tensor_scalar(tmp[:, 2, :], tmp[:, 2, :], -0.5, 1.5, ALU.mult, ALU.add))
                chain(dve.tensor_tensor(rstd[:, :], tmp[:, 2, :], tmp[:, 1, :], ALU.mult))
                dve.wait_ge(att_in, 32)

                def normalise(w):
                    if w >= 5:
                        dve.wait_ge(ynt_psum, w - 4)
                    dve.tensor_scalar(yn[:, w % 5, :], x1[:, w, :], meanvar[:, w, 0:1], rstd[:, w:w + 1],
                                      ALU.subtract, ALU.mult).then_inc(yn_ready, 1)
                for w in range(3):
                    normalise(w)
                for w in range(NW):
                    if w + 3 < NW:
                        normalise(w + 3)
                    dve.wait_ge(h_copied, w + 1)
                    if w:
                        dve.wait_ge(logit_done, w)
                    h_w = acc[:, w, 0:MSG].rearrange("p (h r) -> p h r", h=HEADS)[:, :, 0:HD]
                    for j in range(2):
                        dve.tensor_tensor(prod[:, j, :].rearrange("p (h r) -> p h r", h=HEADS), h_w,
                                          att[:, j, :].rearrange("p (h r) -> p h r", h=HEADS), ALU.mult).then_inc(dve_step, 1)
                    n += 2
                    dve.wait_ge(dve_step, n)
                    chain(dve.tensor_reduce(ad_l[:, w, :], prod[:, 1, :].rearrange("p (h r) -> p h r", h=HEADS),
                                            AX.X, ALU.add))
                    dve.tensor_reduce(acc[:, w, MSG:ROW], prod[:, 0, :].rearrange("p (h r) -> p h r", h=HEADS),
                                      AX.X, ALU.add).then_inc(logit_done, 1)
                dve.wait_ge(logit_done, NW)
                chain(dve.tensor_tensor(mx_l[:, :, :], acc[:, :, MSG:ROW], ad_l[:, :, :], ALU.add))
                chain(dve.scalar_tensor_tensor(out=mx_l[:, :, :].rearrange("p w h -> p (w h)"),
                                               in0=mx_l[:, :, :].rearrange("p w h -> p (w h)"), scalar=SLOPE,
                                               in1=mx_l[:, :, :].rearrange("p w h -> p (w h)"),
                                               op0=ALU.mult, op1=ALU.max))
                dve.wait_ge(smt_psum, 1)
                chain(dve.tensor_copy(smallT[:, :], small_p))
                for s, m in enumerate(SLOT_GATE):
                    dve.tensor_tensor(biasT[:, s:s + 1], smallT[:, m:m + 1], smallT[:, 8 + m:9 + m], ALU.add).then_inc(dve_step, 1)
                n += 8
                dve.wait_ge(fst_psum, 1)
                chain(dve.tensor_copy(fst[:, :], fst_p))
                chain(dve.tensor_tensor(nblk[:, :], fst[:, 1:NW + 1], fst[:, 0:NW], ALU.subtract))
                chain(dve.tensor_tensor(blk[:, :, :], nblk[:, :].unsqueeze(2).to_broadcast([1, NW, EXTRA + 1]),
                                        step_k[:, :].unsqueeze(1).to_broadcast([1, NW, EXTRA + 1]), ALU.is_gt))
                chain(dve.tensor_reduce(nblk[:, :], blk[:, :, :], AX.X, ALU.add))
                chain(dve.tensor_scalar(nblk[:, :], nblk[:, :], 1.0, None, ALU.max))
                chain(dve.tensor_tensor_scan(uend[:, 0:NW], nblk[:, :], zer[:, :], 0.0, ALU.add, ALU.add))
                chain(dve.tensor_copy(ubeg[:, 1:NW + 1], uend[:, 0:NW]))
                chain(dve.tensor_tensor(cmp[:, :, 0:NW], uend[:, 0:NW].unsqueeze(1).to_broadcast([1, SLOTS, NW]),
                                        uid[:, :].unsqueeze(2).to_broadcast([1, SLOTS, NW]), ALU.is_le))
                chain(dve.tensor_reduce(uwin[:, :], cmp[:, :, 0:NW], AX.X, ALU.add))
                chain(dve.scalar_tensor_tensor(out=adj[:, :], in0=ubeg[:, :], scalar=-float(UNIT), in1=fst[:, :],
                                               op0=ALU.mult, op1=ALU.add))
                chain(dve.tensor_tensor(cmp[:, :, :], uwin[:, :].unsqueeze(2).to_broadcast([1, SLOTS, NW + 1]),
                                        wid[:, :].unsqueeze(1).to_broadcast([1, SLOTS, NW + 1]), ALU.is_equal))
                chain(dve.tensor_tensor(cmp[:, :, :], cmp[:, :, :], adj[:, :].unsqueeze(1).to_broadcast([1, SLOTS, NW + 1]), ALU.mult))
                chain(dve.tensor_reduce(uoff[:, :], cmp[:, :, :], AX.X, ALU.add))
                chain(dve.scalar_tensor_tensor(out=uoff[:, :], in0=uid[:, :], scalar=float(UNIT), in1=uoff[:, :],
                                               op0=ALU.mult, op1=ALU.add))
                chain(dve.tensor_scalar(uoff[:, :], uoff[:, :], float(EDGES), None, ALU.min))
                chain(dve.tensor_copy(units_i[:, 1, :], uoff[:, :]))
                chain(dve.tensor_scalar(uwin[:, :], uwin[:, :], float(NW - 1), None, ALU.min))
                chain(dve.tensor_copy(units_i[:, 0, :], uwin[:, :]))
                chain(dve.tensor_scalar(uid[:, :], uid[:, :], float(SPAN), 1.0, ALU.mult, ALU.add))
                chain(dve.tensor_tensor(uwin[:, :], uend[:, NW - 1:NW].to_broadcast([1, SLOTS]), uid[:, :], ALU.is_gt))
                chain(dve.tensor_reduce(pairs[:, :], uwin[:, :], AX.X, ALU.add))
                dve.tensor_copy(pairs_i[:, :], pairs[:, :]).then_inc(units_done, 1)

            @block.tensor
            def _(pe):
                pe.wait_ge(const_done, 1)
                pe.wait_ge(w_in, 16)

                def project(w):
                    pe.wait_ge(ynt_ready, w + 1)
                    if w >= 2:
                        pe.wait_ge(h_copied, w - 1)
                    for a in range(2):
                        last = pe.matmul(h_p[w % 2], ynT[:, w % 5, a, :], gw[:, a, :], start=(a == 0), stop=(a == 1))
                    last.then_inc(h_psum, 1)
                for w in range(NW):
                    pe.wait_ge(yn_ready, w + 1)
                    if w >= 2:
                        pe.wait_ge(ynt_ready, w - 1)
                    for a in range(2):
                        last = pe.transpose(yT_p[w % 2][:, a, :], yn[:, w % 5, 128 * a:128 * a + 128], ident[0:WIN, 0:WIN])
                    last.then_inc(ynt_psum, 1)
                    if w >= 1:
                        project(w - 1)
                project(NW - 1)
                pe.wait_ge(cnt_ready, 1)
                pe.matmul(fst_p, ones[0:WIN, 0:1], counts[:, :], start=True, stop=True).then_inc(fst_psum, 1)
                pe.wait_ge(sm_in, 80)
                pe.transpose(small_p, small[:, :], ident[0:24, 0:24]).then_inc(smt_psum, 1)
                pe.wait_ge(lw_in, 32)
                for g in range(8):
                    a, half = (g % 4) // 2, g % 2
                    if g >= 2:
                        pe.wait_ge(wt_copied, g - 1)
                    for j in range(4):
                        m = 4 * half + j
                        last = pe.transpose(wT_p[g % 2][:, 128 * j:128 * j + 128],
                                            stage_w[g // 4][:, m, 128 * a:128 * a + 128], ident[:, :])
                    last.then_inc(wt_psum, 1)

        with ExitStack() as c2:
            def sb2(name, shape, dt=F32):
                return c2.enter_context(nc.sbuf_tensor(name, shape, dt))

            def sem2(name):
                return c2.enter_context(nc.semaphore(name))
            H18 = HEADS * TILES
            raw = [sb2(f"raw{q}", [2 * TILES, 128]) for q in range(2)]
            dst_x = [sb2(f"dst_x{q}", [H18, 128]) for q in range(2)]
            ends = [sb2(f"ends{q}", [H18, 129]) for q in range(2)]
            cut = [sb2(f"cut{q}", [H18, 128]) for q in range(2)]
            dst_p = [sb2(f"dst_p{q}", [128, TILES]) for q in range(2)]
            src_p = [sb2(f"src_p{t}", [128, TILES], I32) for t in range(3)]
            ident_h = sb2("ident_h", [128, 128], BF16)
            slog = sb2("slog", [128, HEADS, TILES])
            vmax = sb2("vmax", [H18, 128])
            vend = sb2("vend", [H18, 128])
            vrest = sb2("vrest", [128, HEADS, TILES])
            vT = sb2("vT", [128, TILES, 3 * HEADS + 1], BF16)
            absent = sb2("absent", [WIN, TILES])
            cand = sb2("cand", [WIN, HEADS, TILES])
            bmax = sb2("bmax", [WIN, HEADS])
            zt = sb2("zt", [WIN, HEADS])
            mnew = sb2("mnew", [WIN, HEADS])
            mrest = sb2("mrest", [WIN, HEADS])
            tab = sb2("tab", [128, 6 * HEADS], BF16)
            ad_parts = sb2("ad_parts", [WIN, NW, 3 * HEADS], BF16)
            ad_rest = sb2("ad_rest", [WIN, NW, HEADS])
            dm = sb2("dm", [WIN, HEADS])
            shrink = sb2("shrink", [WIN, HEADS])
            by_edge = sb2("by_edge", [128, 2, TILES, HEADS])
            ez = sb2("ez", [128, TILES, HEADS])
            el = sb2("el", [128, TILES, HEADS])
            prob = [sb2(f"prob{q}", [128, TILES, HEADS]) for q in range(2)]

            edges_in = [sem2("edges_in0"), sem2("edges_in1")]
            gathered = [sem2(f"gathered{t}") for t in range(3)]
            (prep_done, pidx_ready, idx_ready, oh_ready, oht_psum, oht_ready, slog_ready, slogT_ready, vend_ready,
             vT_psum, vT_ready, nmax_psum, tab_ready, dm_ready, shrink_ready, edge_psum, el_ready, prob_ready,
             msg_ready, agg_done, acc_done, set_once, ids_ready, dst_ready, ends_ready, gat_step, waited,
             ident_ready, ohf_ready, adp_ready, cand_ready, mnew_ready, mx_kept, acc_shrunk, edge_step,
             vmax_ready, split_step) = map(sem2, (
                 "prep_done", "pidx_ready", "idx_ready", "oh_ready", "oht_psum", "oht_ready", "slog_ready",
                 "slogT_ready", "vend_ready", "vT_psum", "vT_ready", "nmax_psum", "tab_ready", "dm_ready",
                 "shrink_ready", "edge_psum", "el_ready", "prob_ready", "msg_ready", "agg_done", "acc_done",
                 "set_once", "ids_ready", "dst_ready", "ends_ready", "gat_step", "waited", "ident_ready",
                 "ohf_ready", "adp_ready", "cand_ready", "mnew_ready", "mx_kept", "acc_shrunk", "edge_step",
                 "vmax_ready", "split_step"))
            block = c2.enter_context(nc.Block())

            pidx_p = bank[0][:, 0:2 * TILES]
            slogT_p = bank[1][0:H18, 0:128]
            vT_p = bank[2][:, 0:H18].rearrange("p (h i) -> p h i", h=HEADS)
            nmax_p = bank[3][:, 0:TILES * (3 * HEADS + 1)].rearrange("p (i h) -> p i h", i=TILES)
            edge_p = bank[4][:, 0:TILES * 6 * HEADS].rearrange("p (i h) -> p i h", i=TILES)
            agg_p = bank[5][:, 0:MSG]
            def g_bank(u, q, g):
                return (q + g) % 2
            GT = 6
            GROUPS = TILES // GT
            oht_p = [bank[6 + b][:, :].bitcast(BF16)[:, 0:GT * 128] for b in range(2)]

            def after(eng, signal, count):
                if not (isinstance(count, int) and count <= 0):
                    eng.wait_ge(signal, count)

            def schedule(eng, index, spread, front, step, back):
                index(0, 0)
                for u in range(2):
                    index(u + 1, u + 1)
                    spread(u, u)
                front(0, 0)
                groups = eng.value_load(pairs_i[0:1, 0:1], min_val=(NW - 1) // SPAN, max_val=(NW + EXTRA) // SPAN)
                with eng.Fori(0, groups) as k:
                    for m in range(SPAN):
                        step(SPAN * k + m, m, k)
                back(eng.snap(groups * SPAN), 0)

            def nothing(u, m):
                pass

            def turns(k, m, n):
                return k * (SPAN // n) + (m // n + 1)

            @block.sync
            def _(sp):
                def load(u, m):
                    q = m % 2
                    after(sp, prep_done, u - 1)
                    off = sp.value_load(units_i[0:1, 1, bass.ds(u, 1)], min_val=0, max_val=EDGES)
                    sp.dma_start(raw[q][0:TILES, :], dst_f[bass.ds(off, UNIT)].rearrange("(i p) -> i p", p=128)).then_inc(edges_in[q], 16)
                    sp.dma_start(raw[q][TILES:2 * TILES, :], src_f[bass.ds(off, UNIT)].rearrange("(i p) -> i p", p=128)).then_inc(edges_in[q], 16)
                    for h in range(HEADS):
                        sp.dma_start(dst_x[q][TILES * h:TILES * h + TILES, :],
                                     dst_f[bass.ds(off, UNIT)].rearrange("(i p) -> i p", p=128)).then_inc(edges_in[q], 16)
                schedule(sp, load, nothing, nothing, lambda i, m, k: load(i + 3, m + 3), nothing)

            @block.gpsimd
            def _(pool):
                pool.iota(node_id, pattern=[[1, N + 3]], base=0, channel_multiplier=0,
                          allow_small_or_imprecise_dtypes=True).then_inc(ids_ready, 1)

                def gather(u, m):
                    t = m % 3
                    pool.wait_ge(idx_ready, u + 1)
                    for j in range(GROUPS):
                        pool.wait_ge(agg_done, GROUPS * u + j + 1)
                        pool.sem_inc(waited, 1)
                        for i in range(GT * j, GT * j + GT):
                            pool.indirect_dma_start(out=gath[t][:, i, :], out_offset=None, in_=table,
                                                    in_offset=bass.IndirectOffsetOnAxis(src_p[t][:, i:i + 1], 0)
                                                    ).then_inc(gathered[t], 16)
                schedule(pool, nothing, nothing, gather, lambda i, m, k: gather(i + 1, m + 1), nothing)

            @block.scalar
            def _(act):
                act.activation(ident_h[:, :], ident[:, :], ACT.Copy).then_inc(ident_ready, 1)

                def spread(u, m):
                    q = m % 2
                    after(act, edge_psum, u - 1)
                    for g in range(GROUPS):
                        act.wait_ge(oht_psum, GROUPS * u + g + 1)
                        act.activation(onehotT[q][:, GT * g:GT * g + GT, :], oht_p[(m + g) % 2].rearrange("p (i e) -> p i e", i=GT),
                                       ACT.Copy).then_inc(oht_ready, 1)
                    act.wait_ge(agg_done, GROUPS * u + 2 * GROUPS)
                    act.activation(onehot[q], onehot_h[q], ACT.Copy).then_inc(ohf_ready, 1)

                def front(u, m):
                    act.wait_ge(dm_ready, u + 1)
                    after(act, acc_shrunk, u)
                    act.activation(shrink[:, :], dm[:, :], ACT.Exp).then_inc(shrink_ready, 1)
                    act.wait_ge(el_ready, u + 1)
                    act.activation(prob[m % 2][:, :, :], el[:, :, :], ACT.Exp).then_inc(prob_ready, 1)

                def step(i, m, k):
                    front(i + 1, m + 1)
                    spread(i + 2, m + 2)
                schedule(act, nothing, spread, front, step, nothing)

            @block.tensor
            def _(pe):
                pe.sem_inc(agg_done, 3 * GROUPS)
                pe.wait_ge(ident_ready, 1)

                def index(u, m, k=0):
                    q = m % 2
                    pe.wait_ge(edges_in[q], 96 * turns(k, m, 2))
                    after(pe, idx_ready, u)
                    pe.sem_inc(waited, 1)
                    pe.transpose(pidx_p, raw[q][:, :], ident[0:2 * TILES, 0:2 * TILES]).then_inc(pidx_ready, 1)

                def spread(u, m):
                    q = m % 2
                    pe.wait_ge(oh_ready, u + 1)
                    for g in range(GROUPS):
                        after(pe, oht_ready, GROUPS * u + g - 1)
                        pe.sem_inc(waited, 1)
                        for j in range(GT):
                            last = pe.transpose(oht_p[(m + g) % 2][:, 128 * j:128 * j + 128],
                                                onehot_h[q][:, GT * g + j, :], ident_h[:, :])
                        last.then_inc(oht_psum, 1)

                def turn_logits(u, m):
                    pe.wait_ge(slog_ready, u + 1)
                    pe.transpose(slogT_p, slog[:, :, :].rearrange("p h i -> p (h i)"), ident[:, :]).then_inc(slogT_ready, 1)

                def turn_ends(u, m):
                    pe.wait_ge(vend_ready, u + 1)
                    pe.sem_inc(waited, 1)
                    pe.transpose(vT_p.rearrange("p h i -> p (h i)"), vend[:, :], ident[0:H18, 0:H18]).then_inc(vT_psum, 1)

                def tile_maxima(u, m):
                    pe.wait_ge(vT_ready, u + 1)
                    pe.sem_inc(waited, 1)
                    for i in range(TILES):
                        last = pe.matmul(nmax_p[:, i, :], onehot_h[m % 2][:, i, :], vT[:, i, :], start=True, stop=True)
                    last.then_inc(nmax_psum, 1)

                def expand(u, m):
                    pe.wait_ge(tab_ready, u + 1)
                    pe.wait_ge(oht_ready, GROUPS * u + GROUPS)
                    pe.sem_inc(waited, 1)
                    for i in range(TILES):
                        last = pe.matmul(edge_p[:, i, :], onehotT[m % 2][:, i, :], tab[:, :], start=True, stop=True)
                    last.then_inc(edge_psum, 1)

                def add_up(u, m, g):
                    if g == 0:
                        after(pe, acc_done, u + 1)
                        pe.wait_ge(ohf_ready, u + 1)
                    pe.wait_ge(msg_ready, GROUPS * u + g + 1)
                    for i in range(GT * g, GT * g + GT):
                        last = pe.matmul(agg_p, onehot[m % 2][:, i, :], gath[m % 3][:, i, 0:MSG], start=(i == 0), stop=(i == TILES - 1))
                    last.then_inc(agg_done, 1)

                def front(u, m):
                    turn_logits(u, m)
                    turn_ends(u, m)
                    tile_maxima(u, m)
                    expand(u, m)

                def step(i, m, k):
                    turn_logits(i + 1, m + 1)
                    add_up(i, m, 0)
                    turn_ends(i + 1, m + 1)
                    add_up(i, m, 1)
                    tile_maxima(i + 1, m + 1)
                    add_up(i, m, 2)
                    expand(i + 1, m + 1)
                    spread(i + 2, m + 2)
                    index(i + 3, m + 3, k)

                def back(u, m):
                    for g in range(GROUPS):
                        add_up(u, m, g)
                schedule(pe, index, spread, front, step, back)

            @block.vector
            def _(dve):
                for q in range(2):
                    dve.memset(ends[q][:, :], 1.0).then_inc(set_once, 1)
                dve.memset(vT[:, :, :], 1.0).then_inc(set_once, 1)
                dve.memset(tab[:, :], 0.0).then_inc(set_once, 1)
                dve.wait_ge(set_once, 4)
                dve.wait_ge(ids_ready, 1)
                dve.sem_inc(acc_done, 1)
                dve.tensor_copy(ad_parts[:, :, 0:HEADS], ad_l[:, :, :]).then_inc(set_once, 1)
                dve.wait_ge(set_once, 5)
                dve.tensor_tensor(ad_rest[:, :, :], ad_l[:, :, :], ad_parts[:, :, 0:HEADS], ALU.subtract).then_inc(set_once, 1)
                dve.wait_ge(set_once, 6)
                dve.tensor_copy(ad_parts[:, :, HEADS:2 * HEADS], ad_rest[:, :, :]).then_inc(set_once, 1)
                dve.wait_ge(set_once, 7)
                dve.tensor_tensor(ad_parts[:, :, 2 * HEADS:3 * HEADS], ad_rest[:, :, :], ad_parts[:, :, HEADS:2 * HEADS],
                                  ALU.subtract).then_inc(set_once, 1)
                dve.wait_ge(set_once, 8)

                def window(u):
                    return dve.value_load(units_i[0:1, 0, bass.ds(u, 1)], min_val=0, max_val=NW - 1)

                def of(t, win, size):
                    return t[:, bass.ds(win, 1), 0:size].rearrange("p w r -> p (w r)")

                def stepper(signal, count, u):
                    n = 0

                    def chain(ins):
                        nonlocal n
                        n += 1
                        assert n <= count
                        ins.then_inc(signal, 1)
                        dve.wait_ge(signal, count * u + n)
                    return chain

                def parts(chain, out3, value, rest):
                    chain(dve.tensor_copy(out3[0], value))
                    chain(dve.tensor_tensor(rest, value, out3[0], ALU.subtract))
                    chain(dve.tensor_copy(out3[1], rest))
                    return dve.tensor_tensor(out3[2], rest, out3[1], ALU.subtract)

                def index(u, m):
                    dve.wait_ge(pidx_ready, u + 1)
                    dve.tensor_copy(dst_p[m % 2][:, :], pidx_p[:, 0:TILES]).then_inc(dst_ready, 1)
                    dve.tensor_copy(src_p[m % 3][:, :], pidx_p[:, TILES:2 * TILES]).then_inc(idx_ready, 1)

                def spread(u, m, win):
                    q = m % 2
                    dve.wait_ge(dst_ready, u + 1)
                    after(dve, ohf_ready, u - 1)
                    after(dve, nmax_psum, u - 1)
                    after(dve, oht_psum, GROUPS * u - GROUPS)
                    dve.tensor_tensor(onehot_h[q], dst_p[q][:, :].unsqueeze(2).to_broadcast([128, TILES, 128]),
                                      node_id[:, bass.ds(win * WIN, 128)].unsqueeze(1).to_broadcast([128, TILES, 128]),
                                      ALU.is_equal).then_inc(oh_ready, 1)

                def run_ends(u, m, k=0):
                    q = m % 2
                    dve.wait_ge(edges_in[q], 96 * turns(k, m, 2))
                    dve.tensor_tensor(ends[q][:, 1:128], dst_x[q][:, 1:128], dst_x[q][:, 0:127], ALU.not_equal).then_inc(ends_ready, 1)
                    dve.wait_ge(ends_ready, u + 1)
                    dve.tensor_scalar(cut[q][:, :], ends[q][:, 0:128], -BIG, None, ALU.mult).then_inc(prep_done, 1)

                def logits(u, m, k=0):
                    dve.wait_ge(gathered[m % 3], 16 * TILES * turns(k, m, 3))
                    dve.tensor_copy(slog[:, :, :], gath[m % 3][:, :, MSG:ROW].rearrange("p i h -> p h i")).then_inc(slog_ready, 1)

                def run_maxima(u, m):
                    dve.wait_ge(slogT_ready, u + 1)
                    dve.wait_ge(prep_done, u + 1)
                    dve.tensor_tensor_scan(vmax[:, :], cut[m % 2][:, :], slogT_p, -BIG, ALU.add, ALU.max).then_inc(vmax_ready, 1)
                    dve.wait_ge(vmax_ready, u + 1)
                    dve.tensor_tensor(vend[:, :], vmax[:, :], ends[m % 2][:, 1:129], ALU.mult).then_inc(vend_ready, 1)

                def split_maxima(u, m):
                    dve.wait_ge(vT_psum, u + 1)
                    parts(stepper(split_step, 3, u),
                          [vT[:, :, HEADS * j:HEADS * j + HEADS].rearrange("p i h -> p h i") for j in range(3)],
                          vT_p, vrest[:, :, :]).then_inc(vT_ready, 1)

                def node_maxima(u, m, win):
                    chain = stepper(gat_step, 7, u)
                    ad_w, mx_w, adp_w = of(ad_l, win, HEADS), of(mx_l, win, HEADS), of(ad_parts, win, 3 * HEADS)
                    dve.tensor_scalar(tab[0:WIN, 0:3 * HEADS], adp_w, 1.0, None, ALU.mult).then_inc(adp_ready, 1)
                    dve.wait_ge(nmax_psum, u + 1)
                    dve.tensor_reduce(cand[:, :, :], nmax_p[0:WIN, :, 0:3 * HEADS].rearrange("p i (j h) -> p h i j", j=3),
                                      AX.X, ALU.add).then_inc(cand_ready, 1)
                    dve.tensor_scalar(absent[:, :], nmax_p[0:WIN, :, 3 * HEADS], 0.0, -BIG, ALU.is_equal, ALU.mult).then_inc(cand_ready, 1)
                    dve.wait_ge(cand_ready, 2 * u + 2)
                    chain(dve.tensor_tensor(cand[:, :, :], cand[:, :, :], absent[:, :].unsqueeze(1).to_broadcast([WIN, HEADS, TILES]), ALU.add))
                    chain(dve.tensor_reduce(bmax[:, :], cand[:, :, :], AX.X, ALU.max))
                    chain(dve.tensor_tensor(zt[:, :], bmax[:, :], ad_w, ALU.add))
                    chain(dve.scalar_tensor_tensor(out=zt[:, :], in0=zt[:, :], scalar=SLOPE, in1=zt[:, :],
                                                   op0=ALU.mult, op1=ALU.max))
                    dve.tensor_tensor(mnew[:, :], zt[:, :], mx_w, ALU.max).then_inc(mnew_ready, 1)
                    dve.wait_ge(mnew_ready, u + 1)
                    parts(chain, [tab[0:WIN, HEADS * j:HEADS * j + HEADS] for j in range(3, 6)], mnew[:, :], mrest[:, :]).then_inc(tab_ready, 1)
                    dve.tensor_tensor(dm[:, :], mx_w, mnew[:, :], ALU.subtract).then_inc(dm_ready, 1)
                    dve.wait_ge(dm_ready, u + 1)
                    dve.tensor_scalar(mx_w, mnew[:, :], 1.0, None, ALU.mult).then_inc(mx_kept, 1)

                def weights(u, m):
                    chain = stepper(edge_step, 4, u)
                    dve.wait_ge(edge_psum, u + 1)
                    chain(dve.tensor_reduce(by_edge[:, :, :, :], edge_p.rearrange("p i (g j h) -> p g i h j", g=2, j=3), AX.X, ALU.add))
                    chain(dve.tensor_tensor(ez[:, :, :], slog[:, :, :].rearrange("p h i -> p i h"), by_edge[:, 0, :, :], ALU.add))
                    flat = ez[:, :, :].rearrange("p i h -> p (i h)")
                    chain(dve.scalar_tensor_tensor(out=flat, in0=flat, scalar=SLOPE, in1=flat, op0=ALU.mult, op1=ALU.max))
                    chain(dve.tensor_tensor(ez[:, :, :], ez[:, :, :], by_edge[:, 1, :, :], ALU.subtract))
                    dve.tensor_scalar(el[:, :, :], ez[:, :, :], 0.0, None, ALU.min).then_inc(el_ready, 1)

                def messages(u, m, j):
                    if j == 0:
                        dve.wait_ge(prob_ready, u + 1)
                    rows = gath[m % 3][:, GT * j:GT * j + GT, 0:MSG].rearrange("p i (h r) -> p i h r", h=HEADS)
                    dve.tensor_tensor(rows, rows, prob[m % 2][:, GT * j:GT * j + GT, :].unsqueeze(3).to_broadcast([128, GT, HEADS, HR]),
                                      ALU.mult).then_inc(msg_ready, 1)

                def shrink_sum(u, m, win):
                    acc_wh = of(acc, win, MSG).rearrange("p (h r) -> p h r", h=HEADS)
                    dve.wait_ge(shrink_ready, u + 1)
                    dve.tensor_tensor(acc_wh, acc_wh, shrink[:, :].unsqueeze(2).to_broadcast([WIN, HEADS, HR]), ALU.mult).then_inc(acc_shrunk, 1)

                def grow_sum(u, m, win):
                    acc_w = of(acc, win, MSG)
                    dve.wait_ge(acc_shrunk, u + 1)
                    dve.wait_ge(agg_done, GROUPS * u + 4 * GROUPS)
                    dve.tensor_tensor(acc_w, acc_w, agg_p[0:WIN, :], ALU.add).then_inc(acc_done, 1)

                def first_spread(u, m):
                    spread(u, m, window(u))
                    run_ends(u, m)

                def front(u, m):
                    logits(u, m)
                    run_maxima(u, m)
                    split_maxima(u, m)
                    node_maxima(u, m, window(u))
                    weights(u, m)

                def step(i, m, k):
                    logits(i + 1, m + 1, k)
                    messages(i, m, 0)
                    win0, win1, win2 = window(i), window(i + 1), window(i + 2)
                    run_maxima(i + 1, m + 1)
                    messages(i, m, 1)
                    shrink_sum(i, m, win0)
                    split_maxima(i + 1, m + 1)
                    messages(i, m, 2)
                    spread(i + 2, m + 2, win2)
                    node_maxima(i + 1, m + 1, win1)
                    run_ends(i + 2, m + 2, k)
                    grow_sum(i, m, win0)
                    weights(i + 1, m + 1)
                    index(i + 3, m + 3)

                def back(u, m):
                    for j in range(GROUPS):
                        messages(u, m, j)
                    win = window(u)
                    shrink_sum(u, m, win)
                    grow_sum(u, m, win)
                schedule(dve, index, first_spread, front, step, back)

        with ExitStack() as c3:
            def sb3(name, shape, dt=F32):
                return c3.enter_context(nc.sbuf_tensor(name, shape, dt))

            def sem3(name):
                return c3.enter_context(nc.semaphore(name))
            WB = 5
            gbias = sb3("gbias", [WIN, D])
            rden = sb3("rden", [WIN, NW, HEADS])
            stats3 = sb3("stats3", [WIN, WB, 6])
            mv3 = sb3("mv3", [WIN, WB, 2])
            var3 = sb3("var3", [WIN, WB])
            sd3 = sb3("sd3", [WIN, WB])
            inv3 = sb3("inv3", [WIN, WB])
            t3 = sb3("t3", [WIN, WB])
            y3 = sb3("y3", [WIN, WB, D])
            gat = y3
            y3T = sb3("y3T", [128, WB, 2, WIN])
            (bias_in, rden_ready, x1_step, var3_ready, sd3_ready, y3_ready, y3T_psum, y3T_ready,
             proj_psum, proj_done, inv_ready, waited3) = map(sem3, ("bias_in", "rden_ready", "x1_step", "var3_ready",
             "sd3_ready", "y3_ready", "y3T_psum", "y3T_ready",
             "proj_psum", "proj_done", "inv_ready", "waited3"))
            block = c3.enter_context(nc.Block())
            y3T_p = [bank[i][:, 0:2 * WIN].rearrange("p (a n) -> p a n", a=2) for i in range(2)]
            proj_p = [[bank[2 + 2 * i + j][:, 0:4 * WIN].rearrange("p (s n) -> p s n", s=4) for j in range(2)]
                      for i in range(2)]

            @block.sync
            def _(sp):
                sp.dma_start(gbias[:, :], gnn_bias.partition_broadcast(WIN)).then_inc(bias_in, 16)

            @block.scalar
            def _(act):
                with act.Fori(0, NW // WB) as b:
                    act.wait_ge(var3_ready, b + 1)
                    act.activation(sd3[:, :], var3[:, :], ACT.Sqrt).then_inc(sd3_ready, 1)
                    for i in range(WB):
                        act.wait_ge(y3T_psum, WB * b + i + 1)
                        act.activation(y3T[:, i, :, :], y3T_p[i % 2], ACT.Copy).then_inc(y3T_ready, 1)

            @block.vector
            def _(dve):
                dve.wait_ge(bias_in, 16)
                dve.reciprocal(rden[:, :, :], acc[:, :, 0:MSG].rearrange("p w (h r) -> p w h r", h=HEADS)[:, :, :, HD]
                               ).then_inc(rden_ready, 1)
                dve.wait_ge(rden_ready, 1)
                STEPS = 3 * WB + 2 * WB + 4

                def body(b):
                    n = 0

                    def each(make):
                        nonlocal n
                        for i in range(WB):
                            make(i).then_inc(x1_step, 1)
                        n += WB
                        dve.wait_ge(x1_step, STEPS * b + n)

                    def chain(ins):
                        nonlocal n
                        n += 1
                        ins.then_inc(x1_step, 1)
                        dve.wait_ge(x1_step, STEPS * b + n)

                    def win(t, i, size):
                        return t[:, bass.ds(WB * b + i, 1), 0:size].rearrange("p w r -> p (w r)")
                    each(lambda i: dve.tensor_tensor(
                        gat[:, i, :].rearrange("p (h r) -> p h r", h=HEADS),
                        win(acc, i, MSG).rearrange("p (h r) -> p h r", h=HEADS)[:, :, 0:HD],
                        win(rden, i, HEADS).unsqueeze(2).to_broadcast([WIN, HEADS, HD]), ALU.mult))
                    each(lambda i: dve.tensor_tensor(gat[:, i, :], gat[:, i, :], gbias[:, :], ALU.add))
                    each(lambda i: dve.tensor_tensor(win(x1, i, D), win(x1, i, D), gat[:, i, :], ALU.add))
                    dve.sem_inc(waited3, 1)
                    each(lambda i: dve.bn_stats(stats3[:, i, :], win(x1, i, D)))
                    dve.sem_inc(waited3, 1)
                    each(lambda i: dve.bn_aggr(mv3[:, i, :], stats3[:, i, :]))
                    dve.tensor_scalar(var3[:, :], mv3[:, :, 1], EPS, None, ALU.add).then_inc(var3_ready, 1)
                    dve.wait_ge(sd3_ready, b + 1)
                    chain(dve.reciprocal(inv3[:, :], sd3[:, :]))
                    chain(dve.tensor_tensor(t3[:, :], inv3[:, :], inv3[:, :], ALU.mult))
                    chain(dve.tensor_tensor(t3[:, :], t3[:, :], var3[:, :], ALU.mult))
                    chain(dve.tensor_scalar(t3[:, :], t3[:, :], -0.5, 1.5, ALU.mult, ALU.add))
                    assert n == STEPS, n
                    dve.tensor_tensor(inv3[:, :], inv3[:, :], t3[:, :], ALU.mult).then_inc(inv_ready, 1)
                    dve.wait_ge(inv_ready, b + 1)
                    for i in range(WB):
                        dve.tensor_scalar(y3[:, i, :], win(x1, i, D), mv3[:, i, 0:1], inv3[:, i:i + 1],
                                          ALU.subtract, ALU.mult).then_inc(y3_ready, 1)

                def evacuate(b):
                    for i in range(WB):
                        dve.wait_ge(proj_psum, WB * b + i + 1)
                        for j in range(2):
                            dst_v = xproj[:, 4 * j:4 * j + 4, :, bass.ds(5 * (WB * b + i), 5)].rearrange("p s k c -> p s c k")
                            for s in range(4):
                                dve.tensor_scalar(dst_v[:, s, :, :], proj_p[i % 2][j][:, s, :].rearrange("p (c k) -> p c k", c=5),
                                                  biasT[:, 4 * j + s:4 * j + s + 1], None, ALU.add).then_inc(proj_done, 1)
                    dve.wait_ge(proj_done, 8 * WB * b + 8 * WB)
                    dve.sem_inc(waited3, 1)
                with dve.Fori(0, NW // WB) as b:
                    body(b)
                    evacuate(b)

            @block.tensor
            def _(pe):
                def project(b, i):
                    pe.wait_ge(y3T_ready, WB * b + i + 1)
                    if i >= 2:
                        pe.wait_ge(proj_done, 8 * (WB * b + i - 1))
                    for j in range(2):
                        for s in range(4):
                            m = SLOT_GATE[4 * j + s]
                            for a in range(2):
                                last = pe.matmul(proj_p[i % 2][j][:, s, :], wihT[:, a, 128 * m:128 * m + 128],
                                                 y3T[:, i, a, :], start=(a == 0), stop=(a == 1))
                    last.then_inc(proj_psum, 1)
                with pe.Fori(0, NW // WB) as b:
                    for i in range(WB):
                        pe.wait_ge(y3_ready, WB * b + i + 1)
                        if i >= 2:
                            pe.wait_ge(y3T_ready, WB * b + i - 1)
                        for a in range(2):
                            last = pe.transpose(y3T_p[i % 2][:, a, :], y3[:, i, 128 * a:128 * a + 128], ident[0:WIN, 0:WIN])
                        last.then_inc(y3T_psum, 1)
                        if i >= 1:
                            project(b, i - 1)
                    project(b, WB - 1)

        with ExitStack() as c4:
            def sb4(name, shape, dt=F32):
                return c4.enter_context(nc.sbuf_tensor(name, shape, dt))

            def sem4(name):
                return c4.enter_context(nc.semaphore(name))
            H_UP = 2.0 ** 15
            w16 = acc_all[:, 0:8 * D].bitcast(F16).rearrange("p (j a g) -> p j a g", j=2, a=2)
            wmag = wihT[:, :, :].rearrange("p a g -> p (a g)")
            h16 = [sb4(f"h16_{q}", [128, 2, 2, 63], F16) for q in range(2)]
            wrow = sb4("wrow", [128, 1])
            wtop1 = sb4("wtop1", [1, 1])
            wtop = sb4("wtop", [128, 1])
            expo_f = sb4("expo_f", [128, 1])
            expo_i = sb4("expo_i", [128, 1], I32)
            up_i = sb4("up_i", [128, 1], I32)
            down_i = sb4("down_i", [128, 1], I32)
            gates = [sb4(f"gates{q}", [128, 8, 63]) for q in range(2)]
            fc = [sb4(f"fc{q}", [128, 2, 63]) for q in range(2)]
            ig = [sb4(f"ig{q}", [128, 2, 63]) for q in range(2)]
            th = [sb4(f"th{q}", [128, 2, 63]) for q in range(2)]
            diff = sb4("diff", [128, 2, 2, CH - 1])
            agree = sb4("agree", [128, 1])
            again_f = sb4("again_f", [1, 1])
            again = sb4("again", [1, 1], I32)
            h1_ready, h32_ready, h2_ready, gates_psum, gates_sum, sig_done, tanh_done, cell_ready, th_ready, cell_parts = (
                [sem4(f"{name}{q}") for q in range(2)] for name in
                ("h1_ready", "h32_ready", "h2_ready", "gates_psum", "gates_sum", "sig_done", "tanh_done", "cell_ready",
                 "th_ready", "cell_parts"))
            (zeroed, check_step, agree_ready, agree_psum, again_ready, restarted, waited4, wscale_step, wrow_ready,
             wrow_psum, wtop1_ready, wtop_psum, w16_ready) = map(
                sem4, ("zeroed", "check_step", "agree_ready", "agree_psum", "again_ready", "restarted", "waited4",
                       "wscale_step", "wrow_ready", "wrow_psum", "wtop1_ready", "wtop_psum", "w16_ready"))
            block = c4.enter_context(nc.Block())
            gates_p = [bank[q][:, 0:504].rearrange("p (s n) -> p s n", s=8) for q in range(2)]
            agree_p = bank[2][0:1, 0:1]
            wrow_p = bank[3][0:1, 0:128]
            wtop_p = bank[4][:, 0:1]
            RESTART = 7

            def phases(eng, step, reset, check):
                early = WARM - KS
                with eng.Fori(0, early) as s:
                    step(s, 0, s + (KS - early), 2, 2)
                with eng.Fori(0, KS) as s:
                    step(s + early, 0, s, 1, 1)
                if reset:
                    reset(0, WARM)
                with eng.Fori(0, KS) as s:
                    step(s + WARM, s + 1, s, 0, 0)
                if check:
                    check()
                eng.wait_ge(again_ready, 1)
                flag = eng.value_load(again[0:1, 0:1], min_val=0, max_val=1)
                with eng.If(flag > 0):
                    with eng.Fori(0, CH - 1) as r:
                        base = r * KS + (WARM + KS)
                        if reset:
                            reset(r + 1, base)
                        with eng.Fori(0, KS) as s:
                            step(base + s, s + 1, s, 0, 0)

            def span(q, lo):
                a, b = HALF[q]
                return max(a, lo), b, max(a, lo) - a, b - a

            def hrow(row, a, b):
                return h_rows[:, :, bass.ds(row, 1), a:b].rearrange("p a k c -> p a (k c)")

            @block.sync
            def _(sp):
                sp.wait_ge(again_ready, 1)

            @block.tensor
            def _(pe):
                pe.wait_ge(wrow_ready, 1)
                pe.transpose(wrow_p, wrow[:, :], ident[:, :]).then_inc(wrow_psum, 1)
                pe.wait_ge(wtop1_ready, 1)
                pe.matmul(wtop_p, ones[0:1, :], wtop1[:, :], start=True, stop=True).then_inc(wtop_psum, 1)
                pe.wait_ge(w16_ready, 2)
                pe.wait_ge(zeroed, 5)

                def step(n, row_out, k, lo, shift):
                    for q in range(2):
                        a, b, ca, cb = span(q, lo)
                        for part, ready in ((0, h1_ready[q]), (1, h2_ready[q])):
                            pe.wait_ge(ready, n + 1)
                            pe.sem_inc(waited4, 1)
                            for s, m in enumerate(SLOT_GATE):
                                for wpart in range(2):
                                    for kk in range(2):
                                        first = part + s + wpart + kk == 0
                                        final = part == 1 and s == 7 and wpart == 1 and kk == 1
                                        last = pe.matmul(gates_p[q][:, s, 0:b - a], w16[:, wpart, kk, 128 * m:128 * m + 128],
                                                         h16[q][:, part, kk, ca:cb], start=first, stop=final,
                                                         skip_group_check=True)
                        last.then_inc(gates_psum[q], 1)

                def restart(r, n):
                    if not isinstance(r, int):
                        pe.wait_ge(restarted, RESTART * r + 1)
                        pe.sem_inc(waited4, 1)

                def check():
                    pe.wait_ge(agree_ready, 1)
                    pe.matmul(agree_p, ones[:, 0:1], agree[:, :], start=True, stop=True).then_inc(agree_psum, 1)
                phases(pe, step, restart, check)

            @block.scalar
            def _(act):
                def step(n, row_out, k, lo, shift):
                    for q in range(2):
                        a, b, ca, cb = span(q, lo)
                        g = gates[q][:, :, 0:b - a]
                        act.wait_ge(gates_sum[q], n + 1)
                        act.activation(g[:, 0:6, :], g[:, 0:6, :], ACT.Sigmoid).then_inc(sig_done[q], 1)
                        act.activation(g[:, 6:8, :], g[:, 6:8, :], ACT.Tanh).then_inc(tanh_done[q], 1)
                        act.wait_ge(cell_ready[q], n + 1)
                        act.activation(th[q][:, :, 0:b - a], cell[:, :, a:b], ACT.Tanh).then_inc(th_ready[q], 1)
                phases(act, step, None, None)

            @block.vector
            def _(dve):
                dve.memset(hT[:, :], 0.0).then_inc(zeroed, 1)
                dve.memset(cell[:, :, :], 0.0).then_inc(zeroed, 1)
                dve.memset(start_c[:, :, :], 0.0).then_inc(zeroed, 1)
                for q in range(2):
                    dve.memset(h16[q][:, :, :, :], 0.0).then_inc(zeroed, 1)
                dve.wait_ge(zeroed, 5)
                for q in range(2):
                    for ready in (h1_ready[q], h2_ready[q]):
                        dve.engine_nop().then_inc(ready, 1)

                steps = 0

                def chain(ins):
                    nonlocal steps
                    steps += 1
                    ins.then_inc(wscale_step, 1)
                    dve.wait_ge(wscale_step, steps)
                w_flat = whhT[:, :, :].rearrange("p a g -> p (a g)")
                chain(dve.scalar_tensor_tensor(out=wmag, in0=w_flat, scalar=-1.0, in1=w_flat, op0=ALU.mult, op1=ALU.max))
                dve.tensor_reduce(wrow[:, :], wmag, AX.X, ALU.max).then_inc(wrow_ready, 1)
                dve.wait_ge(wrow_psum, 1)
                dve.tensor_reduce(wtop1[:, :], wrow_p, AX.X, ALU.max).then_inc(wtop1_ready, 1)
                dve.wait_ge(wtop_psum, 1)
                chain(dve.tensor_scalar(wtop[:, :], wtop_p, 2.0 ** -60, None, ALU.max))
                chain(dve.tensor_copy(expo_f[:, :], wtop[:, :].bitcast(I32)))
                chain(dve.tensor_scalar(expo_i[:, :], expo_f[:, :], 2.0 ** -23, None, ALU.mult))
                chain(dve.tensor_copy(expo_f[:, :], expo_i[:, :]))
                chain(dve.tensor_scalar(up_i[:, :], expo_f[:, :], -2.0 ** 23, 267 * 2.0 ** 23, ALU.mult, ALU.add))
                chain(dve.tensor_scalar(down_i[:, :], expo_f[:, :], 2.0 ** 23, -28 * 2.0 ** 23, ALU.mult, ALU.add))
                up, down = up_i[:, :].bitcast(F32), down_i[:, :].bitcast(F32)
                parts = [w16[:, j, :, :].rearrange("p a g -> p (a g)") for j in range(2)]
                dve.tensor_scalar(parts[0], w_flat, up, None, ALU.mult).then_inc(w16_ready, 1)
                dve.wait_ge(w16_ready, 1)
                dve.scalar_tensor_tensor(out=parts[1], in0=w_flat, scalar=up, in1=parts[0],
                                         op0=ALU.mult, op1=ALU.subtract).then_inc(w16_ready, 1)

                def sum_gates(q, n, k, lo, shift):
                    a, b, ca, cb = span(q, lo)
                    dve.wait_ge(gates_psum[q], n + 1)
                    dve.wait_ge(h2_ready[q], n + 1)
                    dve.scalar_tensor_tensor(out=gates[q][:, :, 0:b - a], in0=gates_p[q][:, :, 0:b - a], scalar=down,
                                             in1=xproj[:, :, bass.ds(k, 1), a - shift:b - shift].rearrange("p s k c -> p s (k c)"),
                                             op0=ALU.mult, op1=ALU.add).then_inc(gates_sum[q], 1)

                def move_cell(q, n, lo):
                    a, b, ca, cb = span(q, lo)
                    g = gates[q][:, :, 0:b - a]
                    dve.wait_ge(sig_done[q], n + 1)
                    dve.tensor_tensor(fc[q][:, :, 0:b - a], g[:, 2:4, :], cell[:, :, a:b], ALU.mult).then_inc(cell_parts[q], 1)
                    dve.wait_ge(tanh_done[q], n + 1)
                    dve.tensor_tensor(ig[q][:, :, 0:b - a], g[:, 0:2, :], g[:, 6:8, :], ALU.mult).then_inc(cell_parts[q], 1)
                    dve.wait_ge(cell_parts[q], 2 * n + 2)
                    dve.tensor_tensor(cell[:, :, a:b], fc[q][:, :, 0:b - a], ig[q][:, :, 0:b - a], ALU.add).then_inc(cell_ready[q], 1)

                def make_h(q, n, row_out, lo):
                    a, b, ca, cb = span(q, lo)
                    o, t = gates[q][:, 4:6, 0:b - a], th[q][:, :, 0:b - a]
                    dve.wait_ge(th_ready[q], n + 1)
                    dve.scalar_tensor_tensor(out=h16[q][:, 0, :, ca:cb], in0=o, scalar=H_UP, in1=t,
                                             op0=ALU.mult, op1=ALU.mult).then_inc(h1_ready[q], 1)
                    dve.tensor_tensor(hrow(row_out, a, b), o, t, ALU.mult).then_inc(h32_ready[q], 1)
                    dve.wait_ge(h1_ready[q], n + 2)
                    dve.wait_ge(h32_ready[q], n + 1)
                    dve.scalar_tensor_tensor(out=h16[q][:, 1, :, ca:cb], in0=hrow(row_out, a, b), scalar=H_UP,
                                             in1=h16[q][:, 0, :, ca:cb], op0=ALU.mult, op1=ALU.subtract).then_inc(h2_ready[q], 1)

                def step(n, row_out, k, lo, shift):
                    sum_gates(0, n, k, lo, shift)
                    move_cell(0, n, lo)
                    sum_gates(1, n, k, lo, shift)
                    make_h(0, n, row_out, lo)
                    move_cell(1, n, lo)
                    make_h(1, n, row_out, lo)

                def reset(r, n):
                    for q in range(2):
                        dve.wait_ge(h2_ready[q], n + 1)
                        dve.wait_ge(cell_ready[q], n)
                    if isinstance(r, int):
                        dve.tensor_copy(start_c[:, :, :], cell[:, :, :]).then_inc(restarted, 1)
                        dve.wait_ge(restarted, 1)
                    else:
                        done = RESTART * r - RESTART + 1
                        dve.tensor_copy(start_c[:, :, 1:CH], cell[:, :, 0:CH - 1]).then_inc(restarted, 1)
                        dve.wait_ge(restarted, done + 1)
                        dve.tensor_copy(cell[:, :, :], start_c[:, :, :]).then_inc(restarted, 1)
                        dve.tensor_copy(h_rows[:, :, 0, 1:CH], h_rows[:, :, KS, 0:CH - 1]).then_inc(restarted, 1)
                        dve.wait_ge(restarted, done + 3)
                        for q in range(2):
                            a, b = HALF[q]
                            dve.tensor_scalar(h16[q][:, 0, :, 0:b - a], h_rows[:, :, 0, a:b], H_UP, None, ALU.mult).then_inc(restarted, 1)
                        dve.wait_ge(restarted, done + 5)
                        for q in range(2):
                            a, b = HALF[q]
                            dve.scalar_tensor_tensor(out=h16[q][:, 1, :, 0:b - a], in0=h_rows[:, :, 0, a:b], scalar=H_UP,
                                                     in1=h16[q][:, 0, :, 0:b - a], op0=ALU.mult, op1=ALU.subtract).then_inc(restarted, 1)
                        dve.wait_ge(restarted, done + 7)
                        dve.sem_inc(waited4, 1)

                def check():
                    n = WARM + KS
                    for q in range(2):
                        dve.wait_ge(h2_ready[q], n + 1)
                        dve.wait_ge(cell_ready[q], n)
                    dve.tensor_tensor(diff[:, 0, :, :], h_rows[:, :, 0, 1:CH], h_rows[:, :, KS, 0:CH - 1], ALU.subtract).then_inc(check_step, 1)
                    dve.tensor_tensor(diff[:, 1, :, :], start_c[:, :, 1:CH], cell[:, :, 0:CH - 1], ALU.subtract).then_inc(check_step, 1)
                    dve.wait_ge(check_step, 2)
                    flat = diff[:, :, :, :].rearrange("p x a c -> p (x a c)")
                    dve.scalar_tensor_tensor(out=flat, in0=flat, scalar=-1.0, in1=flat, op0=ALU.mult, op1=ALU.max).then_inc(check_step, 1)
                    dve.wait_ge(check_step, 3)
                    dve.tensor_scalar(flat, flat, TOL, None, ALU.is_le).then_inc(check_step, 1)
                    dve.wait_ge(check_step, 4)
                    dve.tensor_reduce(agree[:, :], flat, AX.X, ALU.min).then_inc(agree_ready, 1)
                    dve.wait_ge(agree_psum, 1)
                    dve.tensor_scalar(again_f[:, :], agree_p, 127.5, None, ALU.is_lt).then_inc(check_step, 1)
                    dve.wait_ge(check_step, 5)
                    dve.tensor_copy(again[:, :], again_f[:, :]).then_inc(again_ready, 1)
                phases(dve, step, reset, check)

        with ExitStack() as c5:
            def sb5(name, shape, dt=F32):
                return c5.enter_context(nc.sbuf_tensor(name, shape, dt))

            def sem5(name):
                return c5.enter_context(nc.semaphore(name))
            masked = arena[:, 0:2 * N].rearrange("p (a t) -> p a t", a=2)
            incl = arena[:, 2 * N:4 * N].rearrange("p (a t) -> p a t", a=2)
            res = arena[:, 4 * N:6 * N].rearrange("p (a t) -> p a t", a=2)
            wdiff = sb5("wdiff", [128, 2, 128])
            wd = sb5("wd", [128, 2])
            blin = sb5("blin", [128, 2])
            tie = sb5("tie", [128, 1])
            nfw = sb5("nfw", [128, 2])
            fmb = sb5("fmb", [128, 2])
            tbw = sb5("tbw", [128, 2])
            zeros = arena[:, 6 * N:7 * N]
            (blin_in, out_step, wdiff_ready, logit_psum, mask_done, incl_done, scaled, tbw_ready, res_done,
             resT_psum, x_done, stored, zero_ready) = map(sem5, ("blin_in", "out_step", "wdiff_ready", "logit_psum", "mask_done",
             "incl_done", "scaled", "tbw_ready", "res_done", "resT_psum", "x_done", "stored", "zero_ready"))
            block = c5.enter_context(nc.Block())
            RB = 4
            blocks = [(k, min(k + RB, KS)) for k in range(0, KS, RB)]
            logit_p = [bank[i][:, :] for i in range(4)]
            resT_p = [bank[4 + i][0:WIN, 0:D] for i in range(4)]

            def in_time(v, k0, k1):
                return v.rearrange("p (c k) -> p k c", k=KS)[:, k0:k1, :]

            @block.sync
            def _(sp):
                sp.dma_start(blin[:, :], b_lin.partition_broadcast(128)).then_inc(blin_in, 16)
                rows = out.rearrange("(w p) f -> p w f", p=WIN)
                for b in range(5):
                    sp.wait_ge(x_done, 5 * b + 5)
                    sp.dma_start(rows[:, 5 * b:5 * b + 5, :], x1[:, 5 * b:5 * b + 5, :]).then_inc(stored, 16)
                sp.wait_ge(stored, 80)

            @block.gpsimd
            def _(pool):
                pool.memset(zeros, 0.0).then_inc(zero_ready, 1)

            @block.tensor
            def _(pe):
                pe.wait_ge(wdiff_ready, 2)
                for i, (k0, k1) in enumerate(blocks):
                    if i >= 4:
                        pe.wait_ge(mask_done, 2 * (i - 3))
                    for a in range(2):
                        last = pe.matmul(logit_p[i % 4][:, 0:(k1 - k0) * CH], wdiff[:, a, :],
                                         h_rows[:, a, 1 + k0:1 + k1, :].rearrange("p k c -> p (k c)"),
                                         start=(a == 0), stop=(a == 1))
                    last.then_inc(logit_psum, 1)
                pe.wait_ge(res_done, 2)
                for w in range(NW):
                    if w >= 4:
                        pe.wait_ge(x_done, w - 3)
                    for a in range(2):
                        last = pe.transpose(resT_p[w % 4][:, 128 * a:128 * a + 128], res[:, a, WIN * w:WIN * w + WIN], ident[:, :])
                    last.then_inc(resT_psum, 1)

            @block.scalar
            def _(act):
                act.wait_ge(tbw_ready, 1)
                for a in range(2):
                    act.activation(incl[:, a, :], incl[:, a, :], ACT.Identity, bias=tbw[:, a:a + 1],
                                   scale=fmb[:, a:a + 1]).then_inc(scaled, 1)

            @block.vector
            def _(dve):
                n = 0

                def chain(ins):
                    nonlocal n
                    n += 1
                    ins.then_inc(out_step, 1)
                    dve.wait_ge(out_step, n)
                chain(dve.tensor_tensor(wd[:, :], smallT[:, 18:20], smallT[:, 16:18], ALU.subtract))
                for a in range(2):
                    dve.tensor_scalar(wdiff[:, a, :], ones[:, :], wd[:, a:a + 1], None, ALU.mult).then_inc(wdiff_ready, 1)
                dve.wait_ge(blin_in, 16)
                chain(dve.tensor_tensor(tie[:, :], blin[:, 0:1], blin[:, 1:2], ALU.subtract))
                chain(dve.tensor_scalar(nfw[:, :], smallT[:, 20:22], -1.0, None, ALU.mult))
                chain(dve.tensor_tensor(fmb[:, :], smallT[:, 20:22], smallT[:, 22:24], ALU.subtract))
                for i, (k0, k1) in enumerate(blocks):
                    dve.wait_ge(logit_psum, i + 1)
                    for a in range(2):
                        dve.scalar_tensor_tensor(out=in_time(masked[:, a, :], k0, k1),
                                                 in0=logit_p[i % 4][:, 0:(k1 - k0) * CH].rearrange("p (k c) -> p k c", c=CH),
                                                 scalar=tie[:, :], in1=h_rows[:, a, 1 + k0:1 + k1, :],
                                                 op0=ALU.is_gt, op1=ALU.mult).then_inc(mask_done, 1)
                dve.wait_ge(mask_done, 2 * len(blocks))
                dve.wait_ge(zero_ready, 1)
                for a in range(2):
                    dve.tensor_tensor_scan(incl[:, a, :], masked[:, a, :], zeros, 0.0, ALU.add, ALU.add).then_inc(incl_done, 1)
                dve.wait_ge(incl_done, 2)
                dve.tensor_tensor(tbw[:, :], incl[:, :, N - 1], smallT[:, 22:24], ALU.mult).then_inc(tbw_ready, 1)
                for a in range(2):
                    dve.wait_ge(scaled, a + 1)
                    chain(dve.scalar_tensor_tensor(out=masked[:, a, :], in0=masked[:, a, :], scalar=nfw[:, a:a + 1],
                                                   in1=incl[:, a, :], op0=ALU.mult, op1=ALU.add))
                    dve.scalar_tensor_tensor(out=res[:, a, :].rearrange("p (c k) -> p c k", k=KS),
                                             in0=h_rows[:, a, 1:KS + 1, :].rearrange("p k c -> p c k"), scalar=2.0,
                                             in1=masked[:, a, :].rearrange("p (c k) -> p c k", k=KS),
                                             op0=ALU.mult, op1=ALU.add).then_inc(res_done, 1)
                for w in range(NW):
                    dve.wait_ge(resT_psum, w + 1)
                    dve.tensor_tensor(x1[:, w, :], x1[:, w, :], resT_p[w % 4], ALU.add).then_inc(x_done, 1)


_INS = ["x", "src", "dst", "L0_gnn_W", "L0_gnn_att_src", "L0_gnn_att_dst", "L0_gnn_bias", "L0_ffn_W_ih",
        "L0_ffn_W_hh", "L0_ffn_b_ih", "L0_ffn_b_hh", "L0_ffn_W_lin", "L0_ffn_b_lin", "L0_ffn_fw_att",
        "L0_ffn_bw_att"]


def kernel(**inputs):
    import concourse.bacc as bacc
    from concourse.bass_utils import run_bass_kernel_spmd

    nc = bacc.Bacc("TRN2", target_bir_lowering=False, num_devices=1)
    arrays, args = {}, []
    for name in _INS:
        a = np.ascontiguousarray(inputs[name])
        arrays[f"in_{name}"] = a
        args.append(nc.dram_tensor(f"in_{name}", a.shape, mybir.dt.from_np(a.dtype), kind="ExternalInput").ap())
    out = nc.dram_tensor("out", [N, D], F32, kind="ExternalOutput").ap()
    build(nc, *args, out)
    r = run_bass_kernel_spmd(nc, [arrays], core_ids=[0])
    return r.results[0]["out"]
```

```python
from contextlib import ExitStack

import numpy as np

import concourse.bass as bass
from concourse import mybir

F32 = mybir.dt.float32
F16 = mybir.dt.float16
BF16 = mybir.dt.bfloat16
I32 = mybir.dt.int32
ALU = mybir.AluOpType
ACT = mybir.ActivationFunctionType
AX = mybir.AxisListType

N = 3125
D = 256
HEADS, HD = 4, 64
EDGES = 53125
WIN = 125
NW = N // WIN
TILES = 18
UNIT = TILES * 128
HR = HD + 1
MSG = HEADS * HR
ROW = MSG + HEADS
BIG = 1.0e30
EXTRA = EDGES // UNIT
SPAN = 6
SLOTS = NW + EXTRA + 8
CH, KS = 125, 25
WARM = 32
HALF = [(0, 63), (63, CH)]
SLOT_GATE = [6, 7, 0, 1, 2, 3, 4, 5]
TOL = 2.0 ** -20
H_UP = 2.0 ** 15
EPS = 1e-5
SLOPE = 0.2


def build(nc, x, src, dst, gnn_w, att_src, att_dst, gnn_bias, w_ih, w_hh, b_ih, b_hh,
          w_lin, b_lin, fw_att, bw_att, out):
    ctx = ExitStack()

    def sb(name, shape, dt=F32):
        return ctx.enter_context(nc.sbuf_tensor(name, shape, dt))

    def ps(name, shape=(128, 512)):
        return ctx.enter_context(nc.psum_tensor(name, list(shape), F32))

    def sem(name):
        return ctx.enter_context(nc.semaphore(name))

    with ctx:
        table = nc.dram_tensor("node_table", [N, ROW], F32).ap()
        dst_f = nc.dram_tensor("dst_f", [EDGES + UNIT], F32).ap()
        src_f = nc.dram_tensor("src_f", [EDGES + UNIT], F32).ap()

        x1 = sb("x1", [WIN, NW, D])
        hT = sb("hT", [128, 2 * (KS + 1) * CH])
        arena = sb("arena", [128, 8 * N])
        acc_all = sb("acc_all", [128, NW * ROW])
        wihT = sb("wihT", [128, 2, 4 * D])
        whhT = sb("whhT", [128, 2, 4 * D])
        ident = sb("ident", [128, 128])
        ones = sb("ones", [128, 128])
        small = sb("small", [24, 128])
        smallT = sb("smallT", [128, 24])
        biasT = sb("biasT", [128, 8])
        ad_l = sb("ad_l", [WIN, NW, HEADS])
        mx_l = sb("mx_l", [WIN, NW, HEADS])
        wtop = sb("wtop", [128, 1])
        expo_f = sb("expo_f", [128, 1])
        expo_i = sb("expo_i", [128, 1], I32)
        up_i = sb("up_i", [128, 1], I32)
        down_i = sb("down_i", [128, 1], I32)
        wrow = sb("wrow", [128, 1])
        wtop1 = sb("wtop1", [1, 1])
        units_i = sb("units_i", [1, 2, SLOTS], I32)
        pairs_i = sb("pairs_i", [1, 1], I32)

        acc = acc_all[0:WIN, :].rearrange("p (w r) -> p w r", w=NW)
        w16 = acc_all[:, 0:8 * D].bitcast(F16).rearrange("p (j a g) -> p j a g", j=2, a=2)
        h_rows = hT[:, :].rearrange("p (a k c) -> p a k c", a=2, k=KS + 1)
        xproj = arena[:, :].rearrange("p (s k c) -> p s k c", s=8, k=KS)
        at = 0

        def carve(rows, size):
            nonlocal at
            at += size
            return arena[0:rows, at - size:at]
        gath = [carve(128, TILES * ROW).rearrange("p (i r) -> p i r", i=TILES) for _ in range(3)]
        onehot = [carve(128, TILES * 128).rearrange("p (i n) -> p i n", i=TILES) for _ in range(2)]
        onehot_h = [carve(128, TILES * 128 // 2).bitcast(BF16).rearrange("p (i n) -> p i n", i=TILES) for _ in range(2)]
        onehotT = [carve(128, UNIT // 2).bitcast(BF16).rearrange("p (i e) -> p i e", i=TILES) for _ in range(2)]
        ad_rest = carve(WIN, NW * HEADS).rearrange("p (w h) -> p w h", w=NW)
        cand = carve(WIN, HEADS * TILES).rearrange("p (h i) -> p h i", h=HEADS)
        slog = carve(128, HEADS * TILES).rearrange("p (h i) -> p h i", h=HEADS)
        by_edge = carve(128, 2 * TILES * HEADS).rearrange("p (g i h) -> p g i h", g=2, i=TILES)
        vmax, vend = [carve(HEADS * TILES, 128) for _ in range(2)]
        node_id = hT[:, 0:N + 3]
        stage_w = [arena[:, i * 8 * D:(i + 1) * 8 * D]
                   .rearrange("p (m d) -> p m d", m=8) for i in range(2)]

        bank = [ps(f"bank{i}") for i in range(8)]

        with ExitStack() as c1:
            def sb1(name, shape, dt=F32):
                return c1.enter_context(nc.sbuf_tensor(name, shape, dt))

            def sem1(name):
                return c1.enter_context(nc.semaphore(name))
            XB = 5
            gw = sb1("gw", [128, 2, D + 2 * HEADS])
            at = 2 * 8 * D
            edge_i = carve(WIN, 2 * (EDGES // WIN)).bitcast(I32).rearrange("p (a e) -> p a e", a=2)
            edge_f = carve(WIN, 2 * (EDGES // WIN)).rearrange("p (a e) -> p a e", a=2)
            pad = sb1("pad", [128, 2, TILES])
            below = [carve(WIN, EDGES // WIN) for _ in range(2)]
            counts = sb1("counts", [WIN, NW + 1])
            stats = sb1("stats", [WIN, NW, 6])
            meanvar = sb1("meanvar", [WIN, NW, 2])
            rstd = sb1("rstd", [WIN, NW])
            tmp = sb1("tmp", [WIN, 3, NW])
            yn = carve(WIN, 5 * D).rearrange("p (b d) -> p b d", b=5)
            ynT = carve(128, 10 * WIN).rearrange("p (b a n) -> p b a n", b=5, a=2)
            gbias = carve(WIN, D)
            att = carve(128, 2 * D).rearrange("p (j d) -> p j d", j=2)
            prod = carve(128, 4 * D).rearrange("p (j a d) -> p j a d", j=2, a=2)
            shift = sb1("shift", [WIN, NW])
            fst = sb1("fst", [1, NW + 1])
            blk = sb1("blk", [1, NW, EXTRA + 1])
            step_k = sb1("step_k", [1, EXTRA + 1])
            nblk = sb1("nblk", [1, NW])
            zer = sb1("zer", [1, NW])
            uend = sb1("uend", [1, NW + 1])
            ubeg = sb1("ubeg", [1, NW + 1])
            adj = sb1("adj", [1, NW + 1])
            uid = sb1("uid", [1, SLOTS])
            wid = sb1("wid", [1, NW + 1])
            cmp = carve(1, SLOTS * (NW + 1)).rearrange("p (u w) -> p u w", u=SLOTS)
            uwin = sb1("uwin", [1, SLOTS])
            uoff = sb1("uoff", [1, SLOTS])
            pcmp = sb1("pcmp", [1, EXTRA + 2])
            pairs = sb1("pairs", [1, 1])

            x_in = [sem1(f"x_in{b}") for b in range(NW // XB)]
            bias_in, bias_added = map(sem1, ("bias_in", "bias_added"))
            w_in, e_in, att_in, lw_in, sm_in = map(sem1, ("w_in", "e_in", "att_in", "lw_in", "sm_in"))
            pool_step, const_done, e_float, scratch = map(sem1, ("pool_step", "const_done", "e_float", "scratch"))
            dve_step, var_ready, sd_ready = map(sem1, ("dve_step", "var_ready", "sd_ready"))
            yn_ready, ynt_psum, ynt_ready, h_psum = map(sem1, ("yn_ready", "ynt_psum", "ynt_ready", "h_psum"))
            h_copied, cnt_ready, fst_psum = map(sem1, ("h_copied", "cnt_ready", "fst_psum"))
            prod_ready, gw_ready, norm_ready, ids_made, count_done = map(sem1, ("prod_ready", "gw_ready", "norm_ready", "ids_made", "count_done"))
            wt_psum, wt_copied, smt_psum, tab_out = map(sem1, ("wt_psum", "wt_copied", "smt_psum", "tab_out"))
            units_done = sem1("units_done")
            block = c1.enter_context(nc.Block())

            yT_p = [bank[0][:, 0:2 * WIN].rearrange("p (a n) -> p a n", a=2),
                    bank[1][:, 0:2 * WIN].rearrange("p (a n) -> p a n", a=2)]
            h_p = [bank[2][0:WIN, 0:D + 2 * HEADS], bank[3][0:WIN, 0:D + 2 * HEADS]]
            fst_p = bank[4][0:1, 0:NW + 1]
            wT_p = [bank[5], bank[6]]
            small_p = bank[7][:, 0:24]

            @block.sync
            def _(sp):
                x_rows = x.rearrange("(w p) f -> p w f", p=WIN)
                for b in range(NW // XB):
                    sp.dma_start(x1[:, XB * b:XB * b + XB, :], x_rows[:, XB * b:XB * b + XB, :]).then_inc(x_in[b], 16)
                    if b == 0:
                        sp.dma_start(edge_i[:, 0, :], dst.rearrange("(p e) -> p e", p=WIN)).then_inc(e_in, 16)
                        sp.dma_start(edge_i[:, 1, :], src.rearrange("(p e) -> p e", p=WIN)).then_inc(e_in, 16)
                sp.dma_start(gbias[:, :], gnn_bias.partition_broadcast(WIN)).then_inc(bias_in, 16)
                sp.wait_ge(e_float, 2)
                sp.dma_start(dst_f[0:EDGES].rearrange("(p e) -> p e", p=WIN), edge_f[:, 0, :]).then_inc(scratch, 16)
                sp.dma_start(src_f[0:EDGES].rearrange("(p e) -> p e", p=WIN), edge_f[:, 1, :]).then_inc(scratch, 16)
                sp.wait_ge(const_done, 1)
                sp.dma_start(dst_f[EDGES:EDGES + UNIT].rearrange("(p e) -> p e", p=128), pad[:, 0, :]).then_inc(scratch, 16)
                sp.dma_start(src_f[EDGES:EDGES + UNIT].rearrange("(p e) -> p e", p=128), pad[:, 1, :]).then_inc(scratch, 16)
                rows = table.rearrange("(w p) r -> p w r", p=WIN)
                for b in range(5):
                    sp.wait_ge(h_copied, 3 * (5 * b + 5))
                    sp.dma_start(rows[:, 5 * b:5 * b + 5, :], acc[:, 5 * b:5 * b + 5, :]).then_inc(tab_out, 16)
                sp.wait_ge(scratch, 64)
                sp.wait_ge(tab_out, 80)

            @block.gpsimd
            def _(pool):
                pool.memset(ident[:, :], 0.0).then_inc(pool_step, 1)
                pool.wait_ge(pool_step, 1)
                pool.affine_select(out=ident[:, :], in_=ident[:, :], compare_op=ALU.not_equal, fill=1.0, base=0,
                                   pattern=[[-1, 128]], channel_multiplier=1).then_inc(pool_step, 1)
                pool.memset(ones[:, :], 1.0).then_inc(pool_step, 1)
                pool.memset(pad[:, 0, :], 4096.0).then_inc(pool_step, 1)
                pool.memset(pad[:, 1, :], 0.0).then_inc(pool_step, 1)
                pool.memset(acc[:, :, 0:MSG].rearrange("p w (h r) -> p w h r", h=HEADS)[:, :, :, HD:HR], 1.0).then_inc(pool_step, 1)
                pool.iota(step_k[:, :], pattern=[[UNIT, EXTRA + 1]], base=0, channel_multiplier=0,
                          allow_small_or_imprecise_dtypes=True).then_inc(pool_step, 1)
                pool.iota(uid[:, :], pattern=[[1, SLOTS]], base=0, channel_multiplier=0,
                          allow_small_or_imprecise_dtypes=True).then_inc(pool_step, 1)
                pool.iota(wid[:, :], pattern=[[1, NW + 1]], base=0, channel_multiplier=0,
                          allow_small_or_imprecise_dtypes=True).then_inc(pool_step, 1)
                pool.memset(counts[:, 0:1], 0.0).then_inc(pool_step, 1)
                pool.memset(counts[:, NW:NW + 1], float(EDGES // WIN)).then_inc(pool_step, 1)
                pool.memset(zer[:, :], 0.0).then_inc(pool_step, 1)
                pool.wait_ge(pool_step, 12)
                pool.memset(ubeg[:, 0:1], 0.0).then_inc(const_done, 1)
                pool.iota(node_id, pattern=[[1, N + 3]], base=0, channel_multiplier=0,
                          allow_small_or_imprecise_dtypes=True).then_inc(ids_made, 1)
                pool.wait_ge(bias_in, 16)
                for b in range(NW // XB):
                    v = x1[:, XB * b:XB * b + XB, :]
                    pool.wait_ge(yn_ready, XB * b + XB)
                    pool.tensor_tensor(v, v, gbias[:, :].unsqueeze(1).to_broadcast([WIN, XB, D]), ALU.add).then_inc(bias_added, 1)

            @block.scalar
            def _(act):
                act.dma_start(gw[:, :, 0:D], gnn_w.rearrange("(a p) n -> p a n", p=128)).then_inc(w_in, 16)
                act.dma_start(att[:, 0, :], att_src.rearrange("h d -> (h d)").partition_broadcast(128)).then_inc(att_in, 16)
                act.dma_start(att[:, 1, :], att_dst.rearrange("h d -> (h d)").partition_broadcast(128)).then_inc(att_in, 16)
                act.dma_start(small[0:8, :], b_ih.rearrange("(m p) -> m p", p=128)).then_inc(sm_in, 16)
                act.dma_start(small[8:16, :], b_hh.rearrange("(m p) -> m p", p=128)).then_inc(sm_in, 16)
                act.dma_start(small[16:20, :], w_lin.rearrange("l (a p) -> (l a) p", p=128)).then_inc(sm_in, 16)
                act.dma_start(small[20:22, :], fw_att.rearrange("o (a p) -> (o a) p", p=128)).then_inc(sm_in, 16)
                act.dma_start(small[22:24, :], bw_att.rearrange("o (a p) -> (o a) p", p=128)).then_inc(sm_in, 16)
                act.dma_start(stage_w[0], w_ih.rearrange("(m p) d -> p m d", p=128)).then_inc(lw_in, 16)
                act.dma_start(stage_w[1], w_hh.rearrange("(m p) d -> p m d", p=128)).then_inc(lw_in, 16)

                def deviation(b):
                    act.wait_ge(var_ready, b + 1)
                    act.activation(rstd[:, XB * b:XB * b + XB], tmp[:, 0, XB * b:XB * b + XB], ACT.Sqrt).then_inc(sd_ready, 1)

                def normalise(w):
                    act.wait_ge(norm_ready, w // XB + 1)
                    if w >= 5:
                        act.wait_ge(ynt_psum, w - 4)
                    act.activation(yn[:, w % 5, :], x1[:, w, :], ACT.Identity, bias=shift[:, w:w + 1],
                                   scale=rstd[:, w:w + 1]).then_inc(yn_ready, 1)

                def turned(w):
                    act.wait_ge(ynt_psum, w + 1)
                    act.activation(ynT[:, w % 5, :, :], yT_p[w % 2], ACT.Copy).then_inc(ynt_ready, 1)
                deviation(0)
                for w in range(3):
                    normalise(w)
                turned(0)
                for w in range(NW):
                    if w % XB == 1 and w // XB + 1 < NW // XB:
                        deviation(w // XB + 1)
                    if w + 3 < NW:
                        normalise(w + 3)
                    if w + 1 < NW:
                        turned(w + 1)
                    act.wait_ge(h_psum, w + 1)
                    act.activation(acc[:, w, 0:MSG].rearrange("p (h r) -> p h r", h=HEADS)[:, :, 0:HD],
                                   h_p[w % 2][:, 0:D].rearrange("p (h r) -> p h r", h=HEADS), ACT.Copy).then_inc(h_copied, 1)
                    act.activation(acc[:, w, MSG:ROW], h_p[w % 2][:, D:D + HEADS], ACT.Copy).then_inc(h_copied, 1)
                    act.activation(ad_l[:, w, :], h_p[w % 2][:, D + HEADS:D + 2 * HEADS], ACT.Copy).then_inc(h_copied, 1)
                for g in range(8):
                    act.wait_ge(wt_psum, g + 1)
                    w_t, a, half = (wihT, whhT)[g // 4], (g % 4) // 2, g % 2
                    act.activation(w_t[:, a, 512 * half:512 * half + 512], wT_p[g % 2][:, :], ACT.Copy).then_inc(wt_copied, 1)

            @block.vector
            def _(dve):
                n = 0

                def chain(ins):
                    nonlocal n
                    n += 1
                    ins.then_inc(dve_step, 1)
                    dve.wait_ge(dve_step, n)
                dve.wait_ge(w_in, 16)
                dve.wait_ge(att_in, 32)
                for j in range(2):
                    dve.tensor_tensor(prod[:, j, :, :], gw[:, :, 0:D], att[:, j, :].unsqueeze(1).to_broadcast([128, 2, D]),
                                      ALU.mult).then_inc(prod_ready, 1)
                dve.wait_ge(prod_ready, 2)
                for j in range(2):
                    dve.tensor_reduce(gw[:, :, D + HEADS * j:D + HEADS * j + HEADS],
                                      prod[:, j, :, :].rearrange("p a (h r) -> p a h r", h=HEADS), AX.X, ALU.add).then_inc(gw_ready, 1)
                counted = 1
                for b in range(NW // XB):
                    rows = range(XB * b, XB * b + XB)
                    cols = slice(XB * b, XB * b + XB)
                    dve.wait_ge(x_in[b], 16)
                    for w in rows:
                        dve.bn_stats(stats[:, w, :], x1[:, w, :]).then_inc(dve_step, 1)
                    n += XB
                    dve.wait_ge(dve_step, n)
                    for w in rows:
                        dve.bn_aggr(meanvar[:, w, :], stats[:, w, :]).then_inc(dve_step, 1)
                    n += XB
                    dve.wait_ge(dve_step, n)
                    dve.tensor_scalar(tmp[:, 0, cols], meanvar[:, cols, 1], EPS, None, ALU.add).then_inc(var_ready, 1)
                    if b == 0:
                        dve.wait_ge(e_in, 32)
                        dve.tensor_copy(edge_f[:, 0, :], edge_i[:, 0, :]).then_inc(e_float, 1)
                        dve.tensor_copy(edge_f[:, 1, :], edge_i[:, 1, :]).then_inc(e_float, 1)
                        dve.wait_ge(e_float, 2)
                        dve.wait_ge(const_done, 1)
                    else:
                        for w in range(counted, counted + (NW - 1) // (NW // XB - 1)):
                            if w > 2:
                                dve.wait_ge(count_done, w - 2)
                            dve.tensor_scalar(below[w % 2], edge_f[:, 0, :], float(WIN * w), 0.0, ALU.is_lt, ALU.add,
                                              accum_out=counts[:, w:w + 1]).then_inc(count_done, 1)
                            counted += 1
                    dve.wait_ge(var_ready, b + 1)
                    dve.wait_ge(sd_ready, b + 1)
                    chain(dve.reciprocal(tmp[:, 1, cols], rstd[:, cols]))
                    chain(dve.tensor_tensor(tmp[:, 2, cols], tmp[:, 1, cols], tmp[:, 1, cols], ALU.mult))
                    chain(dve.tensor_tensor(tmp[:, 2, cols], tmp[:, 2, cols], tmp[:, 0, cols], ALU.mult))
                    chain(dve.tensor_scalar(tmp[:, 2, cols], tmp[:, 2, cols], -0.5, 1.5, ALU.mult, ALU.add))
                    chain(dve.tensor_tensor(rstd[:, cols], tmp[:, 2, cols], tmp[:, 1, cols], ALU.mult))
                    dve.scalar_tensor_tensor(out=shift[:, cols], in0=meanvar[:, cols, 0], scalar=-1.0, in1=rstd[:, cols],
                                             op0=ALU.mult, op1=ALU.mult).then_inc(norm_ready, 1)
                assert counted == NW
                dve.wait_ge(count_done, NW - 1)
                dve.tensor_copy(counts[:, 0:1], counts[:, 0:1]).then_inc(cnt_ready, 1)
                dve.wait_ge(fst_psum, 1)
                chain(dve.tensor_copy(fst[:, :], fst_p))
                chain(dve.tensor_tensor(nblk[:, :], fst[:, 1:NW + 1], fst[:, 0:NW], ALU.subtract))
                chain(dve.tensor_tensor(blk[:, :, :], nblk[:, :].unsqueeze(2).to_broadcast([1, NW, EXTRA + 1]),
                                        step_k[:, :].unsqueeze(1).to_broadcast([1, NW, EXTRA + 1]), ALU.is_gt))
                chain(dve.tensor_reduce(nblk[:, :], blk[:, :, :], AX.X, ALU.add))
                chain(dve.tensor_scalar(nblk[:, :], nblk[:, :], 1.0, None, ALU.max))
                chain(dve.tensor_tensor_scan(uend[:, 0:NW], nblk[:, :], zer[:, :], 0.0, ALU.add, ALU.add))
                chain(dve.tensor_copy(ubeg[:, 1:NW + 1], uend[:, 0:NW]))
                chain(dve.tensor_tensor(cmp[:, :, 0:NW], uend[:, 0:NW].unsqueeze(1).to_broadcast([1, SLOTS, NW]),
                                        uid[:, :].unsqueeze(2).to_broadcast([1, SLOTS, NW]), ALU.is_le))
                chain(dve.tensor_reduce(uwin[:, :], cmp[:, :, 0:NW], AX.X, ALU.add))
                chain(dve.scalar_tensor_tensor(out=adj[:, :], in0=ubeg[:, :], scalar=-float(UNIT), in1=fst[:, :],
                                               op0=ALU.mult, op1=ALU.add))
                chain(dve.tensor_tensor(cmp[:, :, :], uwin[:, :].unsqueeze(2).to_broadcast([1, SLOTS, NW + 1]),
                                        wid[:, :].unsqueeze(1).to_broadcast([1, SLOTS, NW + 1]), ALU.is_equal))
                chain(dve.tensor_tensor(cmp[:, :, :], cmp[:, :, :], adj[:, :].unsqueeze(1).to_broadcast([1, SLOTS, NW + 1]), ALU.mult))
                chain(dve.tensor_reduce(uoff[:, :], cmp[:, :, :], AX.X, ALU.add))
                chain(dve.scalar_tensor_tensor(out=uoff[:, :], in0=uid[:, :], scalar=float(UNIT), in1=uoff[:, :],
                                               op0=ALU.mult, op1=ALU.add))
                chain(dve.tensor_scalar(uoff[:, :], uoff[:, :], float(EDGES), None, ALU.min))
                chain(dve.tensor_copy(units_i[:, 1, :], uoff[:, :]))
                chain(dve.tensor_scalar(uwin[:, :], uwin[:, :], float(NW - 1), None, ALU.min))
                chain(dve.tensor_copy(units_i[:, 0, :], uwin[:, :]))
                chain(dve.tensor_scalar(uid[:, :], uid[:, :], float(SPAN), 1.0, ALU.mult, ALU.add))
                chain(dve.tensor_tensor(uwin[:, :], uend[:, NW - 1:NW].to_broadcast([1, SLOTS]), uid[:, :], ALU.is_gt))
                chain(dve.tensor_reduce(pairs[:, :], uwin[:, :], AX.X, ALU.add))
                dve.tensor_copy(pairs_i[:, :], pairs[:, :]).then_inc(units_done, 1)
                dve.wait_ge(smt_psum, 1)
                chain(dve.tensor_copy(smallT[:, :], small_p))
                for s, m in enumerate(SLOT_GATE):
                    dve.tensor_tensor(biasT[:, s:s + 1], smallT[:, m:m + 1], smallT[:, 8 + m:9 + m], ALU.add).then_inc(dve_step, 1)
                n += 8
                dve.wait_ge(h_copied, 3 * NW)
                chain(dve.tensor_tensor(mx_l[:, :, :], acc[:, :, MSG:ROW], ad_l[:, :, :], ALU.add))
                chain(dve.scalar_tensor_tensor(out=mx_l[:, :, :].rearrange("p w h -> p (w h)"),
                                               in0=mx_l[:, :, :].rearrange("p w h -> p (w h)"), scalar=SLOPE,
                                               in1=mx_l[:, :, :].rearrange("p w h -> p (w h)"),
                                               op0=ALU.mult, op1=ALU.max))

            @block.tensor
            def _(pe):
                pe.wait_ge(const_done, 1)
                pe.wait_ge(w_in, 16)
                pe.wait_ge(gw_ready, 2)

                def project(w):
                    pe.wait_ge(ynt_ready, w + 1)
                    if w >= 2:
                        pe.wait_ge(h_copied, 3 * (w - 1))
                    for a in range(2):
                        last = pe.matmul(h_p[w % 2], ynT[:, w % 5, a, :], gw[:, a, :], start=(a == 0), stop=(a == 1))
                    last.then_inc(h_psum, 1)
                for w in range(NW):
                    pe.wait_ge(yn_ready, w + 1)
                    if w >= 2:
                        pe.wait_ge(ynt_ready, w - 1)
                    for a in range(2):
                        last = pe.transpose(yT_p[w % 2][:, a, :], yn[:, w % 5, 128 * a:128 * a + 128], ident[0:WIN, 0:WIN])
                    last.then_inc(ynt_psum, 1)
                    if w >= 1:
                        project(w - 1)
                    if w == 18:
                        pe.wait_ge(cnt_ready, 1)
                        pe.matmul(fst_p, ones[0:WIN, 0:1], counts[:, :], start=True, stop=True).then_inc(fst_psum, 1)
                project(NW - 1)
                pe.wait_ge(sm_in, 80)
                pe.transpose(small_p, small[:, :], ident[0:24, 0:24]).then_inc(smt_psum, 1)
                pe.wait_ge(lw_in, 32)
                for g in range(8):
                    a, half = (g % 4) // 2, g % 2
                    if g >= 2:
                        pe.wait_ge(wt_copied, g - 1)
                    for j in range(4):
                        m = 4 * half + j
                        last = pe.transpose(wT_p[g % 2][:, 128 * j:128 * j + 128],
                                            stage_w[g // 4][:, m, 128 * a:128 * a + 128], ident[:, :])
                    last.then_inc(wt_psum, 1)

        with ExitStack() as c2:
            def sb2(name, shape, dt=F32):
                return c2.enter_context(nc.sbuf_tensor(name, shape, dt))

            def sem2(name):
                return c2.enter_context(nc.semaphore(name))
            H18 = HEADS * TILES
            raw = [sb2(f"raw{q}", [2 * TILES, 128]) for q in range(2)]
            dst_x = [sb2(f"dst_x{q}", [H18, 128]) for q in range(2)]
            ends = [sb2(f"ends{q}", [H18, 129]) for q in range(2)]
            cut = [sb2(f"cut{q}", [H18, 128]) for q in range(2)]
            dst_p = [sb2(f"dst_p{q}", [128, TILES]) for q in range(2)]
            src_p = [sb2(f"src_p{t}", [128, TILES], I32) for t in range(3)]
            ident_h = sb2("ident_h", [128, 128], BF16)
            vrest = sb2("vrest", [128, HEADS, TILES])
            vT = sb2("vT", [128, TILES, 3 * HEADS + 1], BF16)
            absent = sb2("absent", [WIN, TILES])
            bmax = sb2("bmax", [WIN, HEADS])
            zt = sb2("zt", [WIN, HEADS])
            mnew = sb2("mnew", [WIN, HEADS])
            mrest = sb2("mrest", [WIN, HEADS])
            tab = sb2("tab", [128, 6 * HEADS], BF16)
            ad_parts = sb2("ad_parts", [WIN, NW, 3 * HEADS], BF16)
            dm = sb2("dm", [WIN, HEADS])
            shrink = sb2("shrink", [WIN, HEADS])
            ez = sb2("ez", [128, TILES, HEADS])
            el = sb2("el", [128, TILES, HEADS])
            prob = [sb2(f"prob{q}", [128, TILES, HEADS]) for q in range(2)]

            edges_in = [sem2("edges_in0"), sem2("edges_in1")]
            gathered = [sem2(f"gathered{t}") for t in range(3)]
            (prep_done, pidx_ready, idx_ready, oh_ready, oht_psum, oht_ready, slog_ready, slogT_ready, vend_ready,
             vT_psum, vT_ready, nmax_psum, tab_ready, dm_ready, shrink_ready, edge_psum, el_ready, prob_ready,
             msg_ready, agg_done, acc_done, set_once, dst_ready, ends_ready, gat_step, waited,
             ident_ready, ohf_ready, adp_ready, cand_ready, mnew_ready, mx_kept, acc_shrunk, edge_step,
             vmax_ready, split_step, act_msg_ready) = map(sem2, (
                 "prep_done", "pidx_ready", "idx_ready", "oh_ready", "oht_psum", "oht_ready", "slog_ready",
                 "slogT_ready", "vend_ready", "vT_psum", "vT_ready", "nmax_psum", "tab_ready", "dm_ready",
                 "shrink_ready", "edge_psum", "el_ready", "prob_ready", "msg_ready", "agg_done", "acc_done",
                 "set_once", "dst_ready", "ends_ready", "gat_step", "waited", "ident_ready",
                 "ohf_ready", "adp_ready", "cand_ready", "mnew_ready", "mx_kept", "acc_shrunk", "edge_step",
                 "vmax_ready", "split_step", "act_msg_ready"))
            block = c2.enter_context(nc.Block())

            pidx_p = bank[0][:, 0:2 * TILES]
            slogT_p = bank[1][0:H18, 0:128]
            vT_p = bank[2][:, 0:H18].rearrange("p (h i) -> p h i", h=HEADS)
            nmax_p = bank[3][:, 0:TILES * (3 * HEADS + 1)].rearrange("p (i h) -> p i h", i=TILES)
            edge_p = bank[4][:, 0:TILES * 6 * HEADS].rearrange("p (i h) -> p i h", i=TILES)
            agg_p = bank[5][:, 0:MSG]
            def g_bank(u, q, g):
                return (q + g) % 2
            GT = 6
            GROUPS = TILES // GT
            ACT_TILES = 4
            oht_p = [bank[6 + b][:, :].bitcast(BF16)[:, 0:GT * 128] for b in range(2)]

            def after(eng, signal, count):
                if not (isinstance(count, int) and count <= 0):
                    eng.wait_ge(signal, count)

            def schedule(eng, index, spread, front, step, back):
                index(0, 0)
                for u in range(2):
                    index(u + 1, u + 1)
                    spread(u, u)
                front(0, 0)
                groups = eng.value_load(pairs_i[0:1, 0:1], min_val=(NW - 1) // SPAN, max_val=(NW + EXTRA) // SPAN)
                with eng.Fori(0, groups) as k:
                    for m in range(SPAN):
                        step(SPAN * k + m, m, k)
                back(eng.snap(groups * SPAN), 0)

            def nothing(u, m):
                pass

            def turns(k, m, n):
                return k * (SPAN // n) + (m // n + 1)

            @block.sync
            def _(sp):
                def load(u, m):
                    q = m % 2
                    after(sp, prep_done, u - 1)
                    off = sp.value_load(units_i[0:1, 1, bass.ds(u, 1)], min_val=0, max_val=EDGES)
                    sp.dma_start(raw[q][0:TILES, :], dst_f[bass.ds(off, UNIT)].rearrange("(i p) -> i p", p=128)).then_inc(edges_in[q], 16)
                    sp.dma_start(raw[q][TILES:2 * TILES, :], src_f[bass.ds(off, UNIT)].rearrange("(i p) -> i p", p=128)).then_inc(edges_in[q], 16)
                    for h in range(HEADS):
                        sp.dma_start(dst_x[q][TILES * h:TILES * h + TILES, :],
                                     dst_f[bass.ds(off, UNIT)].rearrange("(i p) -> i p", p=128)).then_inc(edges_in[q], 16)
                schedule(sp, load, nothing, nothing, lambda i, m, k: load(i + 3, m + 3), nothing)

            @block.gpsimd
            def _(pool):
                def gather(u, m):
                    t = m % 3
                    pool.wait_ge(idx_ready, u + 1)
                    for j in range(GROUPS):
                        pool.wait_ge(agg_done, GROUPS * u + j + 1)
                        pool.sem_inc(waited, 1)
                        for i in range(GT * j, GT * j + GT):
                            pool.indirect_dma_start(out=gath[t][:, i, :], out_offset=None, in_=table,
                                                    in_offset=bass.IndirectOffsetOnAxis(src_p[t][:, i:i + 1], 0)
                                                    ).then_inc(gathered[t], 16)
                schedule(pool, nothing, nothing, gather, lambda i, m, k: gather(i + 1, m + 1), nothing)

            @block.scalar
            def _(act):
                act.activation(ident_h[:, :], ident[:, :], ACT.Copy).then_inc(ident_ready, 1)

                def spread(u, m):
                    q = m % 2
                    after(act, edge_psum, u - 1)
                    for g in range(GROUPS):
                        act.wait_ge(oht_psum, GROUPS * u + g + 1)
                        act.activation(onehotT[q][:, GT * g:GT * g + GT, :], oht_p[(m + g) % 2].rearrange("p (i e) -> p i e", i=GT),
                                       ACT.Copy).then_inc(oht_ready, 1)
                    act.wait_ge(agg_done, GROUPS * u + 2 * GROUPS)
                    act.activation(onehot[q], onehot_h[q], ACT.Copy).then_inc(ohf_ready, 1)

                def front(u, m):
                    act.wait_ge(dm_ready, u + 1)
                    after(act, acc_shrunk, u)
                    act.activation(shrink[:, :], dm[:, :], ACT.Exp).then_inc(shrink_ready, 1)
                    act.wait_ge(el_ready, u + 1)
                    act.activation(prob[m % 2][:, :, :], el[:, :, :], ACT.Exp).then_inc(prob_ready, 1)

                def messages(u, m):
                    act.wait_ge(prob_ready, u + 1)
                    for i in range(TILES - ACT_TILES, TILES):
                        for h in range(HEADS):
                            rows = gath[m % 3][:, i, HR * h:HR * h + HR]
                            act.activation(rows, rows, ACT.Copy, scale=prob[m % 2][:, i, h:h + 1]).then_inc(act_msg_ready, 1)

                def step(i, m, k):
                    messages(i, m)
                    front(i + 1, m + 1)
                    spread(i + 2, m + 2)
                schedule(act, nothing, spread, front, step, messages)

            @block.tensor
            def _(pe):
                pe.sem_inc(agg_done, 3 * GROUPS)
                pe.wait_ge(ident_ready, 1)

                def index(u, m, k=0):
                    q = m % 2
                    pe.wait_ge(edges_in[q], 96 * turns(k, m, 2))
                    after(pe, idx_ready, u)
                    pe.sem_inc(waited, 1)
                    pe.transpose(pidx_p, raw[q][:, :], ident[0:2 * TILES, 0:2 * TILES]).then_inc(pidx_ready, 1)

                def spread(u, m):
                    q = m % 2
                    pe.wait_ge(oh_ready, u + 1)
                    for g in range(GROUPS):
                        after(pe, oht_ready, GROUPS * u + g - 1)
                        pe.sem_inc(waited, 1)
                        for j in range(GT):
                            last = pe.transpose(oht_p[(m + g) % 2][:, 128 * j:128 * j + 128],
                                                onehot_h[q][:, GT * g + j, :], ident_h[:, :])
                        last.then_inc(oht_psum, 1)

                def turn_logits(u, m):
                    pe.wait_ge(slog_ready, u + 1)
                    pe.transpose(slogT_p, slog[:, :, :].rearrange("p h i -> p (h i)"), ident[:, :]).then_inc(slogT_ready, 1)

                def turn_ends(u, m):
                    pe.wait_ge(vend_ready, u + 1)
                    pe.sem_inc(waited, 1)
                    pe.transpose(vT_p.rearrange("p h i -> p (h i)"), vend[:, :], ident[0:H18, 0:H18]).then_inc(vT_psum, 1)

                def tile_maxima(u, m):
                    pe.wait_ge(vT_ready, u + 1)
                    pe.sem_inc(waited, 1)
                    for i in range(TILES):
                        last = pe.matmul(nmax_p[:, i, :], onehot_h[m % 2][:, i, :], vT[:, i, :], start=True, stop=True)
                    last.then_inc(nmax_psum, 1)

                def expand(u, m):
                    pe.wait_ge(tab_ready, u + 1)
                    pe.wait_ge(oht_ready, GROUPS * u + GROUPS)
                    pe.sem_inc(waited, 1)
                    for i in range(TILES):
                        last = pe.matmul(edge_p[:, i, :], onehotT[m % 2][:, i, :], tab[:, :], start=True, stop=True)
                    last.then_inc(edge_psum, 1)

                def add_up(u, m, g):
                    if g == 0:
                        after(pe, acc_done, u + 1)
                        pe.wait_ge(ohf_ready, u + 1)
                    pe.wait_ge(msg_ready, GROUPS * u + g + 1)
                    if g == GROUPS - 1:
                        pe.wait_ge(act_msg_ready, (ACT_TILES * HEADS) * (u + 1))
                    for i in range(GT * g, GT * g + GT):
                        last = pe.matmul(agg_p, onehot[m % 2][:, i, :], gath[m % 3][:, i, 0:MSG], start=(i == 0), stop=(i == TILES - 1))
                    last.then_inc(agg_done, 1)

                def front(u, m):
                    turn_logits(u, m)
                    turn_ends(u, m)
                    tile_maxima(u, m)
                    expand(u, m)

                def step(i, m, k):
                    index(i + 3, m + 3, k)
                    turn_logits(i + 1, m + 1)
                    add_up(i, m, 0)
                    turn_ends(i + 1, m + 1)
                    add_up(i, m, 1)
                    tile_maxima(i + 1, m + 1)
                    add_up(i, m, 2)
                    expand(i + 1, m + 1)
                    spread(i + 2, m + 2)

                def back(u, m):
                    for g in range(GROUPS):
                        add_up(u, m, g)
                schedule(pe, index, spread, front, step, back)

            @block.vector
            def _(dve):
                for q in range(2):
                    dve.memset(ends[q][:, :], 1.0).then_inc(set_once, 1)
                dve.memset(vT[:, :, :], 1.0).then_inc(set_once, 1)
                dve.memset(tab[:, :], 0.0).then_inc(set_once, 1)
                dve.wait_ge(set_once, 4)
                dve.sem_inc(acc_done, 1)
                dve.tensor_copy(ad_parts[:, :, 0:HEADS], ad_l[:, :, :]).then_inc(set_once, 1)
                dve.wait_ge(set_once, 5)
                dve.tensor_tensor(ad_rest[:, :, :], ad_l[:, :, :], ad_parts[:, :, 0:HEADS], ALU.subtract).then_inc(set_once, 1)
                dve.wait_ge(set_once, 6)
                dve.tensor_copy(ad_parts[:, :, HEADS:2 * HEADS], ad_rest[:, :, :]).then_inc(set_once, 1)
                dve.wait_ge(set_once, 7)
                dve.tensor_tensor(ad_parts[:, :, 2 * HEADS:3 * HEADS], ad_rest[:, :, :], ad_parts[:, :, HEADS:2 * HEADS],
                                  ALU.subtract).then_inc(set_once, 1)
                dve.wait_ge(set_once, 8)

                def window(u):
                    return dve.value_load(units_i[0:1, 0, bass.ds(u, 1)], min_val=0, max_val=NW - 1)

                def of(t, win, size):
                    return t[:, bass.ds(win, 1), 0:size].rearrange("p w r -> p (w r)")

                def stepper(signal, count, u):
                    n = 0

                    def chain(ins):
                        nonlocal n
                        n += 1
                        assert n <= count
                        ins.then_inc(signal, 1)
                        dve.wait_ge(signal, count * u + n)
                    return chain

                def parts(chain, out3, value, rest):
                    chain(dve.tensor_copy(out3[0], value))
                    chain(dve.tensor_tensor(rest, value, out3[0], ALU.subtract))
                    chain(dve.tensor_copy(out3[1], rest))
                    return dve.tensor_tensor(out3[2], rest, out3[1], ALU.subtract)

                def index(u, m):
                    dve.wait_ge(pidx_ready, u + 1)
                    dve.tensor_copy(dst_p[m % 2][:, :], pidx_p[:, 0:TILES]).then_inc(dst_ready, 1)
                    dve.tensor_copy(src_p[m % 3][:, :], pidx_p[:, TILES:2 * TILES]).then_inc(idx_ready, 1)

                def spread(u, m, win):
                    q = m % 2
                    dve.wait_ge(dst_ready, u + 1)
                    after(dve, ohf_ready, u - 1)
                    after(dve, nmax_psum, u - 1)
                    after(dve, oht_psum, GROUPS * u - GROUPS)
                    dve.tensor_tensor(onehot_h[q], dst_p[q][:, :].unsqueeze(2).to_broadcast([128, TILES, 128]),
                                      node_id[:, bass.ds(win * WIN, 128)].unsqueeze(1).to_broadcast([128, TILES, 128]),
                                      ALU.is_equal).then_inc(oh_ready, 1)

                def run_ends(u, m, k=0):
                    q = m % 2
                    dve.wait_ge(edges_in[q], 96 * turns(k, m, 2))
                    dve.tensor_tensor(ends[q][:, 1:128], dst_x[q][:, 1:128], dst_x[q][:, 0:127], ALU.not_equal).then_inc(ends_ready, 1)
                    dve.wait_ge(ends_ready, u + 1)
                    dve.tensor_scalar(cut[q][:, :], ends[q][:, 0:128], -BIG, None, ALU.mult).then_inc(prep_done, 1)

                def logits(u, m, k=0):
                    dve.wait_ge(gathered[m % 3], 16 * TILES * turns(k, m, 3))
                    dve.tensor_copy(slog[:, :, :], gath[m % 3][:, :, MSG:ROW].rearrange("p i h -> p h i")).then_inc(slog_ready, 1)

                def run_maxima(u, m):
                    dve.wait_ge(slogT_ready, u + 1)
                    dve.wait_ge(prep_done, u + 1)
                    dve.tensor_tensor_scan(vmax[:, :], cut[m % 2][:, :], slogT_p, -BIG, ALU.add, ALU.max).then_inc(vmax_ready, 1)
                    dve.wait_ge(vmax_ready, u + 1)
                    dve.tensor_tensor(vend[:, :], vmax[:, :], ends[m % 2][:, 1:129], ALU.mult).then_inc(vend_ready, 1)

                def split_maxima(u, m):
                    dve.wait_ge(vT_psum, u + 1)
                    parts(stepper(split_step, 3, u),
                          [vT[:, :, HEADS * j:HEADS * j + HEADS].rearrange("p i h -> p h i") for j in range(3)],
                          vT_p, vrest[:, :, :]).then_inc(vT_ready, 1)

                def node_maxima(u, m, win):
                    chain = stepper(gat_step, 7, u)
                    ad_w, mx_w, adp_w = of(ad_l, win, HEADS), of(mx_l, win, HEADS), of(ad_parts, win, 3 * HEADS)
                    dve.tensor_scalar(tab[0:WIN, 0:3 * HEADS], adp_w, 1.0, None, ALU.mult).then_inc(adp_ready, 1)
                    dve.wait_ge(nmax_psum, u + 1)
                    dve.tensor_reduce(cand[:, :, :], nmax_p[0:WIN, :, 0:3 * HEADS].rearrange("p i (j h) -> p h i j", j=3),
                                      AX.X, ALU.add).then_inc(cand_ready, 1)
                    dve.tensor_scalar(absent[:, :], nmax_p[0:WIN, :, 3 * HEADS], 0.0, -BIG, ALU.is_equal, ALU.mult).then_inc(cand_ready, 1)
                    dve.wait_ge(cand_ready, 2 * u + 2)
                    chain(dve.tensor_tensor(cand[:, :, :], cand[:, :, :], absent[:, :].unsqueeze(1).to_broadcast([WIN, HEADS, TILES]), ALU.add))
                    chain(dve.tensor_reduce(bmax[:, :], cand[:, :, :], AX.X, ALU.max))
                    chain(dve.tensor_tensor(zt[:, :], bmax[:, :], ad_w, ALU.add))
                    chain(dve.scalar_tensor_tensor(out=zt[:, :], in0=zt[:, :], scalar=SLOPE, in1=zt[:, :],
                                                   op0=ALU.mult, op1=ALU.max))
                    dve.tensor_tensor(mnew[:, :], zt[:, :], mx_w, ALU.max).then_inc(mnew_ready, 1)
                    dve.wait_ge(mnew_ready, u + 1)
                    parts(chain, [tab[0:WIN, HEADS * j:HEADS * j + HEADS] for j in range(3, 6)], mnew[:, :], mrest[:, :]).then_inc(tab_ready, 1)
                    dve.tensor_tensor(dm[:, :], mx_w, mnew[:, :], ALU.subtract).then_inc(dm_ready, 1)
                    dve.wait_ge(dm_ready, u + 1)
                    dve.tensor_scalar(mx_w, mnew[:, :], 1.0, None, ALU.mult).then_inc(mx_kept, 1)

                def weights(u, m):
                    chain = stepper(edge_step, 4, u)
                    dve.wait_ge(edge_psum, u + 1)
                    chain(dve.tensor_reduce(by_edge[:, :, :, :], edge_p.rearrange("p i (g j h) -> p g i h j", g=2, j=3), AX.X, ALU.add))
                    chain(dve.tensor_tensor(ez[:, :, :], slog[:, :, :].rearrange("p h i -> p i h"), by_edge[:, 0, :, :], ALU.add))
                    flat = ez[:, :, :].rearrange("p i h -> p (i h)")
                    chain(dve.scalar_tensor_tensor(out=flat, in0=flat, scalar=SLOPE, in1=flat, op0=ALU.mult, op1=ALU.max))
                    chain(dve.tensor_tensor(ez[:, :, :], ez[:, :, :], by_edge[:, 1, :, :], ALU.subtract))
                    dve.tensor_scalar(el[:, :, :], ez[:, :, :], 0.0, None, ALU.min).then_inc(el_ready, 1)

                def messages(u, m, j):
                    if j == 0:
                        dve.wait_ge(prob_ready, u + 1)
                    end = min(GT * j + GT, TILES - ACT_TILES)
                    rows = gath[m % 3][:, GT * j:end, 0:MSG].rearrange("p i (h r) -> p i h r", h=HEADS)
                    dve.tensor_tensor(rows, rows, prob[m % 2][:, GT * j:end, :].unsqueeze(3).to_broadcast([128, end - GT * j, HEADS, HR]),
                                      ALU.mult).then_inc(msg_ready, 1)

                def shrink_sum(u, m, win):
                    acc_wh = of(acc, win, MSG).rearrange("p (h r) -> p h r", h=HEADS)
                    dve.wait_ge(shrink_ready, u + 1)
                    dve.tensor_tensor(acc_wh, acc_wh, shrink[:, :].unsqueeze(2).to_broadcast([WIN, HEADS, HR]), ALU.mult).then_inc(acc_shrunk, 1)

                def grow_sum(u, m, win):
                    acc_w = of(acc, win, MSG)
                    dve.wait_ge(acc_shrunk, u + 1)
                    dve.wait_ge(agg_done, GROUPS * u + 4 * GROUPS)
                    dve.tensor_tensor(acc_w, acc_w, agg_p[0:WIN, :], ALU.add).then_inc(acc_done, 1)

                def first_spread(u, m):
                    spread(u, m, window(u))
                    run_ends(u, m)

                def front(u, m):
                    logits(u, m)
                    run_maxima(u, m)
                    split_maxima(u, m)
                    node_maxima(u, m, window(u))
                    weights(u, m)

                def step(i, m, k):
                    logits(i + 1, m + 1, k)
                    messages(i, m, 0)
                    win0, win1, win2 = window(i), window(i + 1), window(i + 2)
                    run_maxima(i + 1, m + 1)
                    messages(i, m, 1)
                    index(i + 3, m + 3)
                    shrink_sum(i, m, win0)
                    split_maxima(i + 1, m + 1)
                    messages(i, m, 2)
                    spread(i + 2, m + 2, win2)
                    node_maxima(i + 1, m + 1, win1)
                    run_ends(i + 2, m + 2, k)
                    grow_sum(i, m, win0)
                    weights(i + 1, m + 1)

                def back(u, m):
                    for j in range(GROUPS):
                        messages(u, m, j)
                    win = window(u)
                    shrink_sum(u, m, win)
                    grow_sum(u, m, win)
                schedule(dve, index, first_spread, front, step, back)

        with ExitStack() as c3:
            def sb3(name, shape, dt=F32):
                return c3.enter_context(nc.sbuf_tensor(name, shape, dt))

            def sem3(name):
                return c3.enter_context(nc.semaphore(name))
            WB = 4
            BATCHES = NW // WB
            rden = sb3("rden", [WIN, NW, HEADS])
            stats3 = sb3("stats3", [WIN, WB, 6])
            mv3 = sb3("mv3", [WIN, WB, 2])
            var3 = sb3("var3", [WIN, WB])
            sd3 = sb3("sd3", [WIN, WB])
            inv3 = sb3("inv3", [WIN, WB])
            t3 = sb3("t3", [WIN, WB])
            y3 = sb3("y3", [WIN, WB, D])
            y3T = sb3("y3T", [128, WB, 2, WIN])
            (rden_ready, x1_step, norm_step, stats_ready, var3_ready, sd3_ready, y3_ready, y3T_psum,
             y3T_ready, proj_psum, proj_done, inv_ready, waited3, wmag_ready, wrow_ready, wrow_psum, wtop1_ready,
             h_zeroed, wscale_step, wtop_psum, w16_ready) = map(
                sem3, ("rden_ready", "x1_step", "norm_step", "stats_ready", "var3_ready", "sd3_ready",
                       "y3_ready", "y3T_psum", "y3T_ready", "proj_psum", "proj_done", "inv_ready", "waited3",
                       "wmag_ready", "wrow_ready", "wrow_psum", "wtop1_ready", "h_zeroed", "wscale_step",
                       "wtop_psum", "w16_ready"))
            block = c3.enter_context(nc.Block())
            y3T_p = [bank[i][:, 0:2 * WIN].rearrange("p (a n) -> p a n", a=2) for i in range(2)]
            proj_p = [[bank[2 + 2 * i + j][:, 0:4 * WIN].rearrange("p (s n) -> p s n", s=4) for j in range(2)]
                      for i in range(2)]
            wrow_p = bank[6][0:1, 0:128]
            wtop_p = bank[7][:, 0:1]

            def batch_of(t, w, count, size):
                return t[:, bass.ds(w, count), 0:size]

            @block.gpsimd
            def _(pool):
                pool.wait_ge(wrow_ready, 1)
                pool.memset(hT[:, :], 0.0).then_inc(h_zeroed, 1)

            @block.scalar
            def _(act):
                act.sem_inc(proj_done, 16)
                act.sem_inc(y3T_ready, 2)

                def deviation(b):
                    act.wait_ge(var3_ready, b + 1)
                    act.activation(sd3[:, :], var3[:, :], ACT.Sqrt).then_inc(sd3_ready, 1)

                def turned(w, i):
                    act.wait_ge(y3T_psum, w + WB + 1)
                    act.activation(y3T[:, i % WB, :, :], y3T_p[i % 2], ACT.Copy).then_inc(y3T_ready, 1)

                def projected(w, i):
                    act.wait_ge(proj_psum, w + 1)
                    for s in range(8):
                        act.activation(xproj[:, s, :, bass.ds(5 * w, 5)].rearrange("p k c -> p c k"),
                                       proj_p[i % 2][s // 4][:, s % 4, :].rearrange("p (c k) -> p c k", c=5),
                                       ACT.Identity, bias=biasT[:, s:s + 1]).then_inc(proj_done, 1)
                deviation(0)
                turned(0, 0)
                with act.Fori(0, BATCHES) as b:
                    for i in range(WB):
                        turned(WB * b + i + 1, i + 1)
                        projected(WB * b + i, i)
                        if i == 1:
                            deviation(b + 1)
                projected(NW - 1, 0)

            @block.vector
            def _(dve):
                w_flat = whhT[:, :, :].rearrange("p a g -> p (a g)")
                wmag = hT[:, 0:8 * D]
                dve.reciprocal(rden[:, :, :], acc[:, :, 0:MSG].rearrange("p w (h r) -> p w h r", h=HEADS)[:, :, :, HD]
                               ).then_inc(rden_ready, 1)
                dve.wait_ge(rden_ready, 1)

                def x_new(w, count):
                    total = batch_of(acc, w, count, MSG).rearrange("p w (h r) -> p w h r", h=HEADS)[:, :, :, 0:HD]
                    dve.tensor_tensor(total, total, batch_of(rden, w, count, HEADS).unsqueeze(3).to_broadcast([WIN, count, HEADS, HD]),
                                      ALU.mult).then_inc(x1_step, 1)

                def x_sum(w, count):
                    total = batch_of(acc, w, count, MSG).rearrange("p w (h r) -> p w h r", h=HEADS)[:, :, :, 0:HD]
                    v = batch_of(x1, w, count, D).rearrange("p w (h r) -> p w h r", h=HEADS)
                    dve.tensor_tensor(v, v, total, ALU.add).then_inc(x1_step, 1)

                def normalise(b, count):
                    w = WB * b
                    x_new(w, count)
                    dve.wait_ge(x1_step, 2 * b + 1)
                    x_sum(w, count)
                    dve.wait_ge(x1_step, 2 * b + 2)
                    dve.sem_inc(waited3, 1)
                    for i in range(count):
                        dve.bn_stats(stats3[:, i, :], batch_of(x1, w + i, 1, D).rearrange("p w r -> p (w r)")).then_inc(stats_ready, 1)
                    dve.wait_ge(stats_ready, 2 * w + count)
                    dve.sem_inc(waited3, 1)
                    for i in range(count):
                        dve.bn_aggr(mv3[:, i, :], stats3[:, i, :]).then_inc(stats_ready, 1)
                    dve.wait_ge(stats_ready, 2 * w + 2 * count)
                    dve.tensor_scalar(var3[:, 0:count], mv3[:, 0:count, 1], EPS, None, ALU.add).then_inc(var3_ready, 1)
                    dve.wait_ge(sd3_ready, b + 1)
                    steps = 0

                    def chain(ins):
                        nonlocal steps
                        steps += 1
                        ins.then_inc(norm_step, 1)
                        dve.wait_ge(norm_step, 4 * b + steps)
                    chain(dve.reciprocal(inv3[:, :], sd3[:, :]))
                    chain(dve.tensor_tensor(t3[:, :], inv3[:, :], inv3[:, :], ALU.mult))
                    chain(dve.tensor_tensor(t3[:, :], t3[:, :], var3[:, :], ALU.mult))
                    chain(dve.tensor_scalar(t3[:, :], t3[:, :], -0.5, 1.5, ALU.mult, ALU.add))
                    dve.tensor_tensor(inv3[:, :], inv3[:, :], t3[:, :], ALU.mult).then_inc(inv_ready, 1)
                    dve.wait_ge(inv_ready, b + 1)
                    for i in range(count):
                        dve.wait_ge(y3T_psum, w + i + 1)
                        dve.tensor_scalar(y3[:, i, :], batch_of(x1, w + i, 1, D).rearrange("p w r -> p (w r)"), mv3[:, i, 0:1], inv3[:, i:i + 1],
                                          ALU.subtract, ALU.mult).then_inc(y3_ready, 1)
                with dve.Fori(0, BATCHES) as b:
                    normalise(b, WB)
                dve.scalar_tensor_tensor(out=wmag, in0=w_flat, scalar=-1.0, in1=w_flat, op0=ALU.mult, op1=ALU.max).then_inc(wmag_ready, 1)
                dve.wait_ge(wmag_ready, 1)
                dve.tensor_reduce(wrow[:, :], wmag, AX.X, ALU.max).then_inc(wrow_ready, 1)
                normalise(BATCHES, 1)
                dve.wait_ge(wrow_psum, 1)
                dve.tensor_reduce(wtop1[:, :], wrow_p, AX.X, ALU.max).then_inc(wtop1_ready, 1)
                steps = 0

                def chain(ins):
                    nonlocal steps
                    steps += 1
                    ins.then_inc(wscale_step, 1)
                    dve.wait_ge(wscale_step, steps)
                dve.wait_ge(wtop_psum, 1)
                chain(dve.tensor_scalar(wtop[:, :], wtop_p, 2.0 ** -60, None, ALU.max))
                chain(dve.tensor_copy(expo_f[:, :], wtop[:, :].bitcast(I32)))
                chain(dve.tensor_scalar(expo_i[:, :], expo_f[:, :], 2.0 ** -23, None, ALU.mult))
                chain(dve.tensor_copy(expo_f[:, :], expo_i[:, :]))
                chain(dve.tensor_scalar(up_i[:, :], expo_f[:, :], -2.0 ** 23, 267 * 2.0 ** 23, ALU.mult, ALU.add))
                chain(dve.tensor_scalar(down_i[:, :], expo_f[:, :], 2.0 ** 23, -28 * 2.0 ** 23, ALU.mult, ALU.add))
                up = up_i[:, :].bitcast(F32)
                for a in range(2):
                    dve.tensor_scalar(w16[:, 0, a, :], whhT[:, a, :], up, None, ALU.mult).then_inc(w16_ready, 1)
                for a in range(2):
                    dve.wait_ge(w16_ready, a + 1)
                    dve.scalar_tensor_tensor(out=w16[:, 1, a, :], in0=whhT[:, a, :], scalar=up, in1=w16[:, 0, a, :],
                                             op0=ALU.mult, op1=ALU.subtract).then_inc(w16_ready, 1)

            @block.tensor
            def _(pe):
                pe.sem_inc(y3T_psum, WB)

                def turn(w, i):
                    pe.wait_ge(y3_ready, w + 1)
                    pe.wait_ge(y3T_ready, w + 1)
                    for a in range(2):
                        last = pe.transpose(y3T_p[i % 2][:, a, :], y3[:, i % WB, 128 * a:128 * a + 128], ident[0:WIN, 0:WIN])
                    last.then_inc(y3T_psum, 1)

                def project(w, i):
                    pe.wait_ge(y3T_ready, w + 3)
                    pe.wait_ge(proj_done, 8 * w + 8)
                    for s, m in enumerate(SLOT_GATE):
                        for a in range(2):
                            last = pe.matmul(proj_p[i % 2][s // 4][:, s % 4, :], wihT[:, a, 128 * m:128 * m + 128],
                                             y3T[:, i % WB, a, :], start=(a == 0), stop=(a == 1))
                    last.then_inc(proj_psum, 1)
                turn(0, 0)
                with pe.Fori(0, BATCHES) as b:
                    for i in range(WB):
                        turn(WB * b + i + 1, i + 1)
                        project(WB * b + i, i)
                pe.wait_ge(wrow_ready, 1)
                pe.transpose(wrow_p, wrow[:, :], ident[:, :]).then_inc(wrow_psum, 1)
                pe.wait_ge(wtop1_ready, 1)
                pe.matmul(wtop_p, ones[0:1, :], wtop1[:, :], start=True, stop=True).then_inc(wtop_psum, 1)
                project(NW - 1, 0)

        with ExitStack() as c4:
            def sb4(name, shape, dt=F32):
                return c4.enter_context(nc.sbuf_tensor(name, shape, dt))

            def sem4(name):
                return c4.enter_context(nc.semaphore(name))
            h16 = [sb4(f"h16_{q}", [128, 2, 2, 63], F16) for q in range(2)]
            gates = [sb4(f"gates{q}", [128, 10, 63]) for q in range(2)]
            cell = [gates[q][:, 8:10, :] for q in range(2)]
            start_c = sb4("start_c", [128, 2, CH])
            ig_fc = [sb4(f"ig_fc{q}", [128, 4, 63]) for q in range(2)]
            end_c = sb4("end_c", [128, 2, CH])
            th = [sb4(f"th{q}", [128, 2, 63]) for q in range(2)]
            diff = sb4("diff", [128, 2, 2, CH - 1])
            agree = sb4("agree", [128, 1])
            again_f = sb4("again_f", [1, 1])
            again = sb4("again", [1, 1], I32)
            h1_ready, h32_ready, h2_ready, ifg_psum, o_psum, ifg_sum, o_sum, act_done, cell_ready, th_ready, cell_parts = (
                [sem4(f"{name}{q}") for q in range(2)] for name in
                ("h1_ready", "h32_ready", "h2_ready", "ifg_psum", "o_psum", "ifg_sum", "o_sum", "act_done", "cell_ready",
                 "th_ready", "cell_parts"))
            (zeroed, check_step, agree_ready, agree_psum, again_ready, restarted, waited4) = map(
                sem4, ("zeroed", "check_step", "agree_ready", "agree_psum", "again_ready", "restarted", "waited4",))
            block = c4.enter_context(nc.Block())
            ifg_p = [bank[q][:, 0:378].rearrange("p (s n) -> p s n", s=6) for q in range(2)]
            o_p = [bank[2 + q][:, 0:126].rearrange("p (s n) -> p s n", s=2) for q in range(2)]
            agree_p = bank[5][0:1, 0:1]
            RESTART = 11

            def phases(eng, step, reset, check):
                early = WARM - KS

                def steps(count, unroll, one):
                    assert count % unroll == 0
                    with eng.Fori(0, count // unroll) as g:
                        for j in range(unroll):
                            one(g * unroll + j, (j > 0, j < unroll - 1))
                steps(early, early, lambda s, place: step(s, 0, s + (KS - early), 2, 2, place))
                steps(KS, 5, lambda s, place: step(s + early, 0, s, 1, 1, place))
                if reset:
                    reset(0, WARM)
                steps(KS, 5, lambda s, place: step(s + WARM, s + 1, s, 0, 0, place))
                if check:
                    check(0, WARM + KS)
                eng.wait_ge(again_ready, 1)
                flag = eng.value_load(again[0:1, 0:1], min_val=0, max_val=1)
                with eng.If(flag > 0):
                    with eng.Fori(0, CH - 1) as r:
                        more = eng.value_load(again[0:1, 0:1], min_val=0, max_val=1)
                        with eng.If(more > 0):
                            base = r * KS + (WARM + KS)
                            if reset:
                                reset(r + 1, base)
                            steps(KS, 5, lambda s, place: step(base + s, s + 1, s, 0, 0, place))
                            if check:
                                check(r + 1, base + KS)
                            eng.wait_ge(again_ready, r + 2)
                            eng.sem_inc(waited4, 1)

            def span(q, lo):
                a, b = HALF[q]
                return max(a, lo), b, max(a, lo) - a, b - a

            def hrow(row, a, b):
                return h_rows[:, :, bass.ds(row, 1), a:b].rearrange("p a k c -> p a (k c)")

            @block.sync
            def _(sp):
                sp.wait_ge(again_ready, 1)

            @block.tensor
            def _(pe):
                def step(n, row_out, k, lo, shift, place):
                    for q in range(2):
                        a, b, ca, cb = span(q, lo)
                        for part, ready in ((0, h1_ready[q]), (1, h2_ready[q])):
                            pe.wait_ge(ready, n + 1)
                            pe.sem_inc(waited4, 1)
                            for dest, slots, done in ((ifg_p[q], range(2, 8), ifg_psum[q]), (o_p[q], range(2), o_psum[q])):
                                for s in slots:
                                    m = SLOT_GATE[s]
                                    for wpart in range(2):
                                        for kk in range(2):
                                            first = part + wpart + kk == 0 and s == slots[0]
                                            final = part == 1 and s == slots[-1] and wpart == 1 and kk == 1
                                            last = pe.matmul(dest[:, s - slots[0], ca:cb], w16[:, wpart, kk, 128 * m:128 * m + 128],
                                                             h16[q][:, part, kk, ca:cb], start=first, stop=final,
                                                             skip_group_check=True)
                                if part == 1:
                                    last.then_inc(done, 1)

                def restart(r, n):
                    if not isinstance(r, int):
                        pe.wait_ge(restarted, RESTART * r + 2)
                        pe.sem_inc(waited4, 1)

                def check(r, n):
                    pe.wait_ge(agree_ready, r + 1)
                    pe.matmul(agree_p, ones[:, 0:1], agree[:, :], start=True, stop=True).then_inc(agree_psum, 1)
                phases(pe, step, restart, check)

            @block.scalar
            def _(act):
                def step(n, row_out, k, lo, shift, place):
                    for q in range(2):
                        a, b, ca, cb = span(q, lo)
                        g = gates[q][:, :, ca:cb]
                        act.wait_ge(ifg_sum[q], n + 1)
                        act.activation(g[:, 2:6, :], g[:, 2:6, :], ACT.Sigmoid).then_inc(act_done[q], 1)
                        act.activation(g[:, 6:8, :], g[:, 6:8, :], ACT.Tanh).then_inc(act_done[q], 1)
                        act.wait_ge(o_sum[q], n + 1)
                        act.activation(g[:, 0:2, :], g[:, 0:2, :], ACT.Sigmoid).then_inc(th_ready[q], 1)
                        act.wait_ge(cell_ready[q], n + 1)
                        act.activation(th[q][:, :, ca:cb], cell[q][:, :, ca:cb], ACT.Tanh).then_inc(th_ready[q], 1)
                phases(act, step, None, None)

            @block.vector
            def _(dve):
                down = down_i[:, :].bitcast(F32)
                for q in range(2):
                    dve.memset(h16[q][:, :, :, :], 0.0).then_inc(h2_ready[q], 1)
                    dve.wait_ge(h2_ready[q], 1)
                    dve.engine_nop().then_inc(h1_ready[q], 1)
                for q in range(2):
                    dve.memset(cell[q], 0.0).then_inc(zeroed, 1)
                dve.memset(start_c[:, :, :], 0.0).then_inc(zeroed, 1)
                dve.wait_ge(zeroed, 3)

                def sum_ifg(q, n, k, lo, shift):
                    a, b, ca, cb = span(q, lo)
                    dve.wait_ge(ifg_psum[q], n + 1)
                    dve.scalar_tensor_tensor(out=gates[q][:, 2:8, ca:cb], in0=ifg_p[q][:, :, ca:cb], scalar=down,
                                             in1=xproj[:, 2:8, bass.ds(k, 1), a - shift:b - shift].rearrange("p s k c -> p s (k c)"),
                                             op0=ALU.mult, op1=ALU.add).then_inc(ifg_sum[q], 1)

                def sum_o(q, n, k, lo, shift):
                    a, b, ca, cb = span(q, lo)
                    dve.wait_ge(o_psum[q], n + 1)
                    dve.scalar_tensor_tensor(out=gates[q][:, 0:2, ca:cb], in0=o_p[q][:, :, ca:cb], scalar=down,
                                             in1=xproj[:, 0:2, bass.ds(k, 1), a - shift:b - shift].rearrange("p s k c -> p s (k c)"),
                                             op0=ALU.mult, op1=ALU.add).then_inc(o_sum[q], 1)

                def move_cell(q, n, lo):
                    a, b, ca, cb = span(q, lo)
                    dve.wait_ge(act_done[q], 2 * n + 2)
                    dve.tensor_tensor(ig_fc[q][:, :, ca:cb], gates[q][:, 2:6, ca:cb], gates[q][:, 6:10, ca:cb],
                                      ALU.mult).then_inc(cell_parts[q], 1)
                    dve.wait_ge(cell_parts[q], n + 1)
                    dve.tensor_tensor(cell[q][:, :, ca:cb], ig_fc[q][:, 0:2, ca:cb], ig_fc[q][:, 2:4, ca:cb],
                                      ALU.add).then_inc(cell_ready[q], 1)

                def make_h(q, n, row_out, lo):
                    a, b, ca, cb = span(q, lo)
                    o, t = gates[q][:, 0:2, ca:cb], th[q][:, :, ca:cb]
                    dve.wait_ge(th_ready[q], 2 * n + 2)
                    dve.scalar_tensor_tensor(out=h16[q][:, 0, :, ca:cb], in0=o, scalar=H_UP, in1=t,
                                             op0=ALU.mult, op1=ALU.mult).then_inc(h1_ready[q], 1)
                    dve.tensor_tensor(hrow(row_out, a, b), o, t, ALU.mult).then_inc(h32_ready[q], 1)

                def make_h2(q, n, row_out, lo):
                    a, b, ca, cb = span(q, lo)
                    dve.wait_ge(h32_ready[q], n + 1)
                    dve.scalar_tensor_tensor(out=h16[q][:, 1, :, ca:cb], in0=hrow(row_out, a, b), scalar=H_UP,
                                             in1=h16[q][:, 0, :, ca:cb], op0=ALU.mult, op1=ALU.subtract).then_inc(h2_ready[q], 1)

                left = []

                def step(n, row_out, k, lo, shift, place):
                    sum_ifg(0, n, k, lo, shift)
                    follows, goes_on = place
                    if follows:
                        make_h2(1, *left.pop())
                    sum_o(0, n, k, lo, shift)
                    move_cell(0, n, lo)
                    sum_ifg(1, n, k, lo, shift)
                    make_h(0, n, row_out, lo)
                    sum_o(1, n, k, lo, shift)
                    make_h2(0, n, row_out, lo)
                    move_cell(1, n, lo)
                    make_h(1, n, row_out, lo)
                    if goes_on:
                        left.append((n, row_out, lo))
                    else:
                        make_h2(1, n, row_out, lo)

                def reset(r, n):
                    for q in range(2):
                        dve.wait_ge(h2_ready[q], n + 1)
                        dve.wait_ge(cell_ready[q], n)
                    if isinstance(r, int):
                        for q in range(2):
                            dve.tensor_copy(start_c[:, :, HALF[q][0]:HALF[q][1]], cell[q][:, :, 0:HALF[q][1] - HALF[q][0]]).then_inc(restarted, 1)
                        dve.wait_ge(restarted, 2)
                    else:
                        done = RESTART * r - RESTART + 2
                        for q in range(2):
                            dve.tensor_copy(end_c[:, :, HALF[q][0]:HALF[q][1]], cell[q][:, :, 0:HALF[q][1] - HALF[q][0]]).then_inc(restarted, 1)
                        dve.wait_ge(restarted, done + 2)
                        dve.tensor_copy(cell[0][:, :, 1:63], end_c[:, :, 0:62]).then_inc(restarted, 1)
                        dve.tensor_copy(cell[1][:, :, 0:CH - 63], end_c[:, :, 62:CH - 1]).then_inc(restarted, 1)
                        dve.memset(cell[0][:, :, 0:1], 0.0).then_inc(restarted, 1)
                        dve.tensor_copy(start_c[:, :, 1:CH], end_c[:, :, 0:CH - 1]).then_inc(restarted, 1)
                        dve.tensor_copy(h_rows[:, :, 0, 1:CH], h_rows[:, :, KS, 0:CH - 1]).then_inc(restarted, 1)
                        dve.wait_ge(restarted, done + 7)
                        for q in range(2):
                            a, b = HALF[q]
                            dve.tensor_scalar(h16[q][:, 0, :, 0:b - a], h_rows[:, :, 0, a:b], H_UP, None, ALU.mult).then_inc(restarted, 1)
                        dve.wait_ge(restarted, done + 9)
                        for q in range(2):
                            a, b = HALF[q]
                            dve.scalar_tensor_tensor(out=h16[q][:, 1, :, 0:b - a], in0=h_rows[:, :, 0, a:b], scalar=H_UP,
                                                     in1=h16[q][:, 0, :, 0:b - a], op0=ALU.mult, op1=ALU.subtract).then_inc(restarted, 1)
                        dve.wait_ge(restarted, done + 11)
                        dve.sem_inc(waited4, 1)

                def check(r, n):
                    done = 7 * r
                    for q in range(2):
                        dve.wait_ge(h2_ready[q], n + 1)
                        dve.wait_ge(cell_ready[q], n)
                    for q in range(2):
                        dve.tensor_copy(end_c[:, :, HALF[q][0]:HALF[q][1]], cell[q][:, :, 0:HALF[q][1] - HALF[q][0]]).then_inc(check_step, 1)
                    dve.wait_ge(check_step, done + 2)
                    dve.tensor_tensor(diff[:, 0, :, :], h_rows[:, :, 0, 1:CH], h_rows[:, :, KS, 0:CH - 1], ALU.subtract).then_inc(check_step, 1)
                    dve.tensor_tensor(diff[:, 1, :, :], start_c[:, :, 1:CH], end_c[:, :, 0:CH - 1], ALU.subtract).then_inc(check_step, 1)
                    dve.wait_ge(check_step, done + 4)
                    flat = diff[:, :, :, :].rearrange("p x a c -> p (x a c)")
                    dve.scalar_tensor_tensor(out=flat, in0=flat, scalar=-1.0, in1=flat, op0=ALU.mult, op1=ALU.max).then_inc(check_step, 1)
                    dve.wait_ge(check_step, done + 5)
                    dve.tensor_scalar(flat, flat, TOL, None, ALU.is_le).then_inc(check_step, 1)
                    dve.wait_ge(check_step, done + 6)
                    dve.tensor_reduce(agree[:, :], flat, AX.X, ALU.min).then_inc(agree_ready, 1)
                    dve.wait_ge(agree_psum, r + 1)
                    dve.tensor_scalar(again_f[:, :], agree_p, 127.5, None, ALU.is_lt).then_inc(check_step, 1)
                    dve.wait_ge(check_step, done + 7)
                    dve.tensor_copy(again[:, :], again_f[:, :]).then_inc(again_ready, 1)
                phases(dve, step, reset, check)

        with ExitStack() as c5:
            def sb5(name, shape, dt=F32):
                return c5.enter_context(nc.sbuf_tensor(name, shape, dt))

            def sem5(name):
                return c5.enter_context(nc.semaphore(name))
            masked = arena[:, 0:2 * N].rearrange("p (a t) -> p a t", a=2)
            incl = arena[:, 2 * N:4 * N].rearrange("p (a t) -> p a t", a=2)
            res = arena[:, 4 * N:6 * N].rearrange("p (a t) -> p a t", a=2)
            wdiff = sb5("wdiff", [128, 2, 128])
            wd = sb5("wd", [128, 2])
            blin = sb5("blin", [128, 2])
            tie = sb5("tie", [128, 1])
            nfw = sb5("nfw", [128, 2])
            fmb = sb5("fmb", [128, 2])
            tbw = sb5("tbw", [128, 2])
            zeros = arena[:, 6 * N:7 * N]
            (blin_in, out_step, wdiff_ready, logit_psum, mask_done, incl_done, scaled, tbw_ready, res_done,
             resT_psum, x_done, stored, zero_ready, weighed, h_added) = map(sem5, ("blin_in", "out_step", "wdiff_ready", "logit_psum", "mask_done",
             "incl_done", "scaled", "tbw_ready", "res_done", "resT_psum", "x_done", "stored", "zero_ready", "weighed", "h_added"))
            block = c5.enter_context(nc.Block())
            RB = 4
            blocks = [(k, min(k + RB, KS)) for k in range(0, KS, RB)]
            logit_p = [bank[i][:, :] for i in range(4)]
            resT_p = [bank[4 + i][0:WIN, 0:D] for i in range(4)]

            def in_time(v, k0, k1):
                return v.rearrange("p (c k) -> p k c", k=KS)[:, k0:k1, :]

            @block.sync
            def _(sp):
                sp.dma_start(blin[:, :], b_lin.partition_broadcast(128)).then_inc(blin_in, 16)
                rows = out.rearrange("(w p) f -> p w f", p=WIN)
                for b in range(5):
                    sp.wait_ge(x_done, 5 * b + 5)
                    sp.dma_start(rows[:, 5 * b:5 * b + 5, :], x1[:, 5 * b:5 * b + 5, :]).then_inc(stored, 16)
                sp.wait_ge(stored, 80)

            @block.gpsimd
            def _(pool):
                pool.memset(zeros, 0.0).then_inc(zero_ready, 1)

            @block.tensor
            def _(pe):
                pe.wait_ge(wdiff_ready, 2)
                for i, (k0, k1) in enumerate(blocks):
                    if i >= 4:
                        pe.wait_ge(mask_done, 2 * (i - 3))
                    for a in range(2):
                        last = pe.matmul(logit_p[i % 4][:, 0:(k1 - k0) * CH], wdiff[:, a, :],
                                         h_rows[:, a, 1 + k0:1 + k1, :].rearrange("p k c -> p (k c)"),
                                         start=(a == 0), stop=(a == 1))
                    last.then_inc(logit_psum, 1)
                for w in range(NW):
                    if w % 5 == 0:
                        pe.wait_ge(res_done, w // 5 + 1)
                    if w >= 4:
                        pe.wait_ge(x_done, w - 3)
                    for a in range(2):
                        last = pe.transpose(resT_p[w % 4][:, 128 * a:128 * a + 128], res[:, a, WIN * w:WIN * w + WIN], ident[:, :])
                    last.then_inc(resT_psum, 1)

            @block.scalar
            def _(act):
                act.wait_ge(mask_done, 2 * len(blocks))
                for a in range(2):
                    act.activation(res[:, a, :], masked[:, a, :], ACT.Copy, scale=nfw[:, a:a + 1]).then_inc(weighed, 1)
                act.wait_ge(tbw_ready, 1)
                for a in range(2):
                    act.activation(incl[:, a, :], incl[:, a, :], ACT.Identity, bias=tbw[:, a:a + 1],
                                   scale=fmb[:, a:a + 1]).then_inc(scaled, 1)

            @block.vector
            def _(dve):
                n = 0

                def chain(ins):
                    nonlocal n
                    n += 1
                    ins.then_inc(out_step, 1)
                    dve.wait_ge(out_step, n)
                def add_out(b):
                    for w in range(5 * b, 5 * b + 5):
                        dve.wait_ge(resT_psum, w + 1)
                        dve.tensor_tensor(x1[:, w, :], x1[:, w, :], resT_p[w % 4], ALU.add).then_inc(x_done, 1)

                chain(dve.tensor_tensor(wd[:, :], smallT[:, 18:20], smallT[:, 16:18], ALU.subtract))
                for a in range(2):
                    dve.tensor_scalar(wdiff[:, a, :], ones[:, :], wd[:, a:a + 1], None, ALU.mult).then_inc(wdiff_ready, 1)
                dve.wait_ge(blin_in, 16)
                chain(dve.tensor_tensor(tie[:, :], blin[:, 0:1], blin[:, 1:2], ALU.subtract))
                chain(dve.tensor_scalar(nfw[:, :], smallT[:, 20:22], -1.0, None, ALU.mult))
                chain(dve.tensor_tensor(fmb[:, :], smallT[:, 20:22], smallT[:, 22:24], ALU.subtract))
                for i, (k0, k1) in enumerate(blocks):
                    dve.wait_ge(logit_psum, i + 1)
                    for a in range(2):
                        dve.scalar_tensor_tensor(out=in_time(masked[:, a, :], k0, k1),
                                                 in0=logit_p[i % 4][:, 0:(k1 - k0) * CH].rearrange("p (k c) -> p k c", c=CH),
                                                 scalar=tie[:, :], in1=h_rows[:, a, 1 + k0:1 + k1, :],
                                                 op0=ALU.is_gt, op1=ALU.mult).then_inc(mask_done, 1)
                dve.wait_ge(mask_done, 2 * len(blocks))
                dve.wait_ge(zero_ready, 1)
                for a in range(2):
                    dve.tensor_tensor_scan(incl[:, a, :], masked[:, a, :], zeros, 0.0, ALU.add, ALU.add).then_inc(incl_done, 1)
                dve.wait_ge(incl_done, 2)
                dve.tensor_tensor(tbw[:, :], incl[:, :, N - 1], smallT[:, 22:24], ALU.mult).then_inc(tbw_ready, 1)
                for a in range(2):
                    dve.wait_ge(weighed, a + 1)
                    in_chunks = res[:, a, :].rearrange("p (c k) -> p c k", k=KS)
                    dve.scalar_tensor_tensor(out=in_chunks, in0=h_rows[:, a, 1:KS + 1, :].rearrange("p k c -> p c k"), scalar=2.0,
                                             in1=in_chunks, op0=ALU.mult, op1=ALU.add).then_inc(h_added, 1)
                dve.wait_ge(scaled, 2)
                dve.wait_ge(h_added, 2)
                for b in range(5):
                    part = slice(5 * WIN * b, 5 * WIN * b + 5 * WIN)
                    dve.tensor_tensor(res[:, :, part], res[:, :, part], incl[:, :, part], ALU.add).then_inc(res_done, 1)
                    if b:
                        add_out(b - 1)
                add_out(4)


_INS = ["x", "src", "dst", "L0_gnn_W", "L0_gnn_att_src", "L0_gnn_att_dst", "L0_gnn_bias", "L0_ffn_W_ih",
        "L0_ffn_W_hh", "L0_ffn_b_ih", "L0_ffn_b_hh", "L0_ffn_W_lin", "L0_ffn_b_lin", "L0_ffn_fw_att",
        "L0_ffn_bw_att"]


def kernel(**inputs):
    import concourse.bacc as bacc
    from concourse.bass_utils import run_bass_kernel_spmd

    nc = bacc.Bacc("TRN2", target_bir_lowering=False, num_devices=1)
    arrays, args = {}, []
    for name in _INS:
        a = np.ascontiguousarray(inputs[name])
        arrays[f"in_{name}"] = a
        args.append(nc.dram_tensor(f"in_{name}", a.shape, mybir.dt.from_np(a.dtype), kind="ExternalInput").ap())
    out = nc.dram_tensor("out", [N, D], F32, kind="ExternalOutput").ap()
    build(nc, *args, out)
    r = run_bass_kernel_spmd(nc, [arrays], core_ids=[0])
    return r.results[0]["out"]
```
